# Optimizing a Trainium2 kernel written in Bass

```python
import numpy as np
import jax
import jax.numpy as jnp

def _softmax(x, axis=-1):
    return jax.nn.softmax(x, axis=axis)

def _gelu(x):
    return jax.nn.gelu(x, approximate=True)

def _silu(x):
    return jax.nn.silu(x)

def _sigmoid(x):
    return jax.nn.sigmoid(x)

def _layernorm(x, axis=-1, eps=1e-05):
    m = jnp.mean(x, axis=axis, keepdims=True)
    v = jnp.var(x, axis=axis, keepdims=True)
    return (x - m) / jnp.sqrt(v + eps)

def _scatter_add(tgt, idx, src, axis=0):
    return tgt.at[idx].add(src)

def _segment_sum(src, seg, n):
    return jax.ops.segment_sum(src, seg, n)
kernel_name = 'mk_flamingo_gated_d4_seqx_r8_f85d6c'

def setup_inputs(seed: int=0):
    np.random.seed(seed)
    _w = jnp.asarray

    def _rec_inputs():
        import jax
        import jax.numpy as jnp
        _rk = jax.random.key(seed)
        x = 0.002226 + 0.9996 * jax.random.normal(jax.random.fold_in(_rk, 1), (128, 64, 128), jnp.float32)
        _lenS = 64 - jax.random.randint(jax.random.fold_in(_rk, 7), (128,), 0, max(1, 64 // 4) + 1, jnp.int32)
        _lenS2 = 64 - jax.random.randint(jax.random.fold_in(_rk, 8), (128,), 0, max(1, 64 // 4) + 1, jnp.int32)
        _ctx_1024P = jax.random.normal(jax.random.fold_in(_rk, 11), (128, 16, 128), jnp.float32)
        _ctx_1024c = jax.random.dirichlet(jax.random.fold_in(_rk, 511), 0.3 * jnp.ones((16,), jnp.float32), (128, 64))
        _ctx_1024t = jnp.einsum('bsk,bkd->bsd', _ctx_1024c, _ctx_1024P)
        _ctx_1024t = _ctx_1024t * jax.lax.rsqrt(jnp.mean(jnp.square(_ctx_1024t)) + 1e-12) * 0.953939
        ctx_1024 = -7.10856e-05 + 0.999911 * (_ctx_1024t + 0.3 * jax.random.normal(jax.random.fold_in(_rk, 611), (128, 64, 128), jnp.float32))
        _g = jax.random.normal(jax.random.fold_in(_rk, 9001), (2, 4), jnp.float32)
        _g = jnp.sign(_g) * jnp.maximum(jnp.abs(_g), 1.0) + (_g == 0) * 1.0
        g_xattn = _g[0]
        g_ffn = _g[1]
        return (x, ctx_1024, g_xattn, g_ffn)
    x, ctx_1024, g_xattn, g_ffn = _rec_inputs()

    def _L0_xattn_setup():
        import jax, jax.numpy as jnp
        import numpy as np
        DIM = 128
        HEAD_DIM = 64
        NUM_HEADS = 8
        INNER = HEAD_DIM * NUM_HEADS
        ROT_DIM = HEAD_DIM
        ROPE_BASE = 10000.0
        EPS = 1e-05

        def layer_norm(x, g, b):
            mu = jnp.mean(x, axis=-1, keepdims=True)
            var = jnp.var(x, axis=-1, keepdims=True)
            return (x - mu) * jax.lax.rsqrt(var + EPS) * g + b

        def rope_rotate_k(k):
            n = k.shape[1]
            half = ROT_DIM // 2
            inv_freq = 1.0 / ROPE_BASE ** (jnp.arange(0, ROT_DIM, 2, dtype=jnp.float32) / ROT_DIM)
            theta = jnp.arange(n, dtype=jnp.float32)[:, None] * inv_freq[None, :]
            angles = jnp.concatenate([theta, theta], axis=-1)
            cos = jnp.cos(angles)[None, :, None, :].astype(k.dtype)
            sin = jnp.sin(angles)[None, :, None, :].astype(k.dtype)
            k_rope, k_pass = (k[..., :ROT_DIM], k[..., ROT_DIM:])
            neg_half = jnp.concatenate([-k_rope[..., half:], k_rope[..., :half]], axis=-1)
            k_rope = k_rope * cos + neg_half * sin
            return jnp.concatenate([k_rope, k_pass], axis=-1)
        key = jax.random.key(seed)
        ks = jax.random.split(key, 5)
        b, n, m = (8, 1024, 64)
        s = 1.0 / np.sqrt(DIM)
        return {'x': jax.random.normal(ks[0], (b, n, DIM), jnp.float32), 'latents': jax.random.normal(ks[1], (b, m, DIM), jnp.float32), 'gamma_x': jnp.ones((DIM,), jnp.float32), 'beta_x': jnp.zeros((DIM,), jnp.float32), 'gamma_l': jnp.ones((DIM,), jnp.float32), 'beta_l': jnp.zeros((DIM,), jnp.float32), 'Wq': jax.random.normal(ks[2], (DIM, INNER), jnp.float32) * s, 'Wkv': jax.random.normal(ks[3], (DIM, 2 * INNER), jnp.float32) * s, 'Wo': jax.random.normal(ks[4], (INNER, DIM), jnp.float32) * (1.0 / np.sqrt(INNER))}
    _L0_xattn_all = _L0_xattn_setup()
    _L0_xattn_in = {k: v for k, v in _L0_xattn_all.items() if k in ('gamma_x', 'beta_x', 'gamma_l', 'beta_l', 'Wq', 'Wkv', 'Wo')}
    del _L0_xattn_all

    def _L0_ffn_setup():
        import jax, jax.numpy as jnp
        import numpy as np
        key = jax.random.key(seed)
        k1, k2, k3 = jax.random.split(key, 3)
        B, T, D, E = (4, 256, 128, 8)
        x = jax.random.normal(k1, (B, T, D), dtype=jnp.float32)
        gate_w = jax.random.normal(k2, (E, D), dtype=jnp.float32) * (1.0 / np.sqrt(D))
        bound = float(np.sqrt(6.0 / (D + D)))
        We = jax.random.uniform(k3, (E, D, D), dtype=jnp.float32, minval=-bound, maxval=bound)
        return {'x': x, 'gate_w': gate_w, 'We': We}
    _L0_ffn_all = _L0_ffn_setup()
    _L0_ffn_in = {k: v for k, v in _L0_ffn_all.items() if k in ('gate_w', 'We')}
    del _L0_ffn_all

    def _L1_xattn_setup():
        import jax, jax.numpy as jnp
        import numpy as np
        DIM = 128
        HEADS = 16
        HEAD_DIM = DIM // HEADS
        SCALE = HEAD_DIM ** (-0.5)
        EPS = 1e-05

        def layer_norm(x, g, b):
            mu = jnp.mean(x, axis=-1, keepdims=True)
            var = jnp.mean(jnp.square(x - mu), axis=-1, keepdims=True)
            return (x - mu) * jax.lax.rsqrt(var + EPS) * g + b
        key = jax.random.key(seed)
        ks = jax.random.split(key, 8)
        B, Ls, Lt = (2, 256, 128)
        w_std = DIM ** (-0.5)
        return {'src': jax.random.normal(ks[0], (B, Ls, DIM), jnp.float32), 'tgt': jax.random.normal(ks[1], (B, Lt, DIM), jnp.float32), 'ln1_g': jnp.ones((DIM,), jnp.float32), 'ln1_b': jnp.zeros((DIM,), jnp.float32), 'ln2_g': jnp.ones((DIM,), jnp.float32), 'ln2_b': jnp.zeros((DIM,), jnp.float32), 'Wq': jax.random.normal(ks[2], (DIM, DIM), jnp.float32) * w_std, 'Wk': jax.random.normal(ks[3], (DIM, DIM), jnp.float32) * w_std, 'Wv': jax.random.normal(ks[4], (DIM, DIM), jnp.float32) * w_std, 'Wfc': jax.random.normal(ks[5], (DIM, DIM), jnp.float32) * w_std}
    _L1_xattn_all = _L1_xattn_setup()
    _L1_xattn_in = {k: v for k, v in _L1_xattn_all.items() if k in ('ln1_g', 'ln1_b', 'ln2_g', 'ln2_b', 'Wq', 'Wk', 'Wv', 'Wfc')}
    del _L1_xattn_all

    def _L1_ffn_setup():
        import jax, jax.numpy as jnp
        import numpy as np
        import math
        BETA = 0.9
        THRESHOLD = 1.0
        NUM_STEPS = 5
        ALPHA = 2.0

        @jax.custom_vjp
        def spike_fn(u):
            return (u > 0).astype(u.dtype)

        def _spike_fwd(u):
            return (spike_fn(u), u)

        def _spike_bwd(u, g):
            s = jnp.pi / 2.0 * ALPHA * u
            return (g * (ALPHA / 2.0) / (1.0 + s * s),)
        spike_fn.defvjp(_spike_fwd, _spike_bwd)
        key = jax.random.key(seed)
        k1, k2, k3 = jax.random.split(key, 3)
        n_embd = 128
        x = jax.random.normal(k1, (4, 256, n_embd), dtype=jnp.float32)
        W_fc = jax.random.normal(k2, (4 * n_embd, n_embd), dtype=jnp.float32) / math.sqrt(n_embd)
        W_proj = jax.random.normal(k3, (n_embd, 4 * n_embd), dtype=jnp.float32) / math.sqrt(4 * n_embd)
        return {'x': x, 'W_fc': W_fc, 'W_proj': W_proj}
    _L1_ffn_all = _L1_ffn_setup()
    _L1_ffn_in = {k: v for k, v in _L1_ffn_all.items() if k in ('W_fc', 'W_proj')}
    del _L1_ffn_all

    def _L2_xattn_setup():
        import jax, jax.numpy as jnp
        import numpy as np
        D_MODEL = 128
        B, S = (4, 256)
        key = jax.random.key(seed)
        ks = jax.random.split(key, 10)
        s = 1.0 / np.sqrt(D_MODEL)
        return {'k': jax.random.normal(ks[0], (B, S, D_MODEL), jnp.float32), 'v': jax.random.normal(ks[1], (B, S, D_MODEL), jnp.float32), 'q': jax.random.normal(ks[2], (B, S, D_MODEL), jnp.float32), 'Wk': jax.random.normal(ks[3], (D_MODEL, D_MODEL), jnp.float32) * s, 'Wv': jax.random.normal(ks[4], (D_MODEL, D_MODEL), jnp.float32) * s, 'bv': jnp.zeros((D_MODEL,), jnp.float32), 'Wq': jax.random.normal(ks[5], (D_MODEL, D_MODEL), jnp.float32) * s, 'bq': jnp.zeros((D_MODEL,), jnp.float32), 'Wo': jax.random.normal(ks[6], (D_MODEL, D_MODEL), jnp.float32) * s, 'bo': jnp.zeros((D_MODEL,), jnp.float32)}
    _L2_xattn_all = _L2_xattn_setup()
    _L2_xattn_in = {k: v for k, v in _L2_xattn_all.items() if k in ('Wk', 'Wv', 'bv', 'Wq', 'bq', 'Wo', 'bo')}
    del _L2_xattn_all

    def _L2_ffn_setup():
        import jax, jax.numpy as jnp
        import numpy as np
        B, N, E = (8, 256, 128)
        NUM_EXPERTS = 8
        HIDDEN = 192
        TOP_K = 2
        key = jax.random.key(seed)
        ks = jax.random.split(key, 7)
        s = 0.02
        return {'x': jax.random.normal(ks[0], (B, N, E), dtype=jnp.float32), 'Wr': jax.random.normal(ks[1], (E, NUM_EXPERTS), dtype=jnp.float32) * s, 'br': jnp.zeros((NUM_EXPERTS,), dtype=jnp.float32), 'W1': jax.random.normal(ks[2], (NUM_EXPERTS, E, HIDDEN), dtype=jnp.float32) * s, 'b1': jnp.zeros((NUM_EXPERTS, HIDDEN), dtype=jnp.float32), 'W2': jax.random.normal(ks[3], (NUM_EXPERTS, HIDDEN, E), dtype=jnp.float32) * s, 'b2': jnp.zeros((NUM_EXPERTS, E), dtype=jnp.float32)}
    _L2_ffn_all = _L2_ffn_setup()
    _L2_ffn_in = {k: v for k, v in _L2_ffn_all.items() if k in ('Wr', 'br', 'W1', 'b1', 'W2', 'b2')}
    del _L2_ffn_all

    def _L3_xattn_setup():
        import jax, jax.numpy as jnp
        import numpy as np
        import math
        D = 128
        key = jax.random.key(seed)
        ks = jax.random.split(key, 6)
        B, S = (4, 256)
        scale = 1.0 / math.sqrt(D)
        return {'Q': jax.random.normal(ks[0], (B, S, D), dtype=jnp.float32), 'K': jax.random.normal(ks[1], (B, S, D), dtype=jnp.float32), 'V': jax.random.normal(ks[2], (B, S, D), dtype=jnp.float32), 'WQ': jax.random.normal(ks[3], (D, D), dtype=jnp.float32) * scale, 'WK': jax.random.normal(ks[4], (D, D), dtype=jnp.float32) * scale, 'WV': jax.random.normal(ks[5], (D, D), dtype=jnp.float32) * scale}
    _L3_xattn_all = _L3_xattn_setup()
    _L3_xattn_in = {k: v for k, v in _L3_xattn_all.items() if k in ('WQ', 'WK', 'WV')}
    del _L3_xattn_all

    def _L3_ffn_setup():
        import jax, jax.numpy as jnp
        import numpy as np
        BLOCK = 32
        W_BITS = 4
        ACT_BITS = 16

        def act_qdq(x):
            qmax = 2.0 ** (ACT_BITS - 1) - 1.0
            scale = jnp.maximum(jnp.max(jnp.abs(x)) / qmax, 1e-12)
            return jnp.clip(jnp.round(x / scale), -qmax - 1.0, qmax) * scale

        def fixed_qdq_u16(x):
            scale = 1.0 / 65536.0
            return jnp.clip(jnp.round(x / scale), 0.0, 65535.0) * scale

        def lpbq_dequant(w):
            O, I = w.shape
            qmax = 2.0 ** (W_BITS - 1) - 1.0
            wb = w.reshape(O, I // BLOCK, BLOCK)
            s = jnp.maximum(jnp.max(jnp.abs(wb), axis=-1, keepdims=True) / qmax, 1e-12)
            wq = jnp.clip(jnp.round(wb / s), -qmax - 1.0, qmax) * s
            return wq.reshape(O, I)
        key = jax.random.key(seed)
        k1, k2, k3, k4 = jax.random.split(key, 4)
        B, S, H, I = (2, 512, 128, 384)
        x = jax.random.normal(k1, (B, S, H), jnp.float32)
        w_gate = jax.random.normal(k2, (I, H), jnp.float32) * 0.02
        w_up = jax.random.normal(k3, (I, H), jnp.float32) * 0.02
        w_down = jax.random.normal(k4, (H, I), jnp.float32) * 0.02
        return {'x': x, 'w_gate': w_gate, 'w_up': w_up, 'w_down': w_down}
    _L3_ffn_all = _L3_ffn_setup()
    _L3_ffn_in = {k: v for k, v in _L3_ffn_all.items() if k in ('w_gate', 'w_up', 'w_down')}
    del _L3_ffn_all
    return {'x': x, 'ctx_1024': ctx_1024, 'g_xattn': g_xattn, 'g_ffn': g_ffn, 'L0_xattn_gamma_x': _L0_xattn_in['gamma_x'], 'L0_xattn_beta_x': _L0_xattn_in['beta_x'], 'L0_xattn_gamma_l': _L0_xattn_in['gamma_l'], 'L0_xattn_beta_l': _L0_xattn_in['beta_l'], 'L0_xattn_Wq': _L0_xattn_in['Wq'], 'L0_xattn_Wkv': _L0_xattn_in['Wkv'], 'L0_xattn_Wo': _L0_xattn_in['Wo'], 'L0_ffn_gate_w': _L0_ffn_in['gate_w'], 'L0_ffn_We': _L0_ffn_in['We'], 'L1_xattn_ln1_g': _L1_xattn_in['ln1_g'], 'L1_xattn_ln1_b': _L1_xattn_in['ln1_b'], 'L1_xattn_ln2_g': _L1_xattn_in['ln2_g'], 'L1_xattn_ln2_b': _L1_xattn_in['ln2_b'], 'L1_xattn_Wq': _L1_xattn_in['Wq'], 'L1_xattn_Wk': _L1_xattn_in['Wk'], 'L1_xattn_Wv': _L1_xattn_in['Wv'], 'L1_xattn_Wfc': _L1_xattn_in['Wfc'], 'L1_ffn_W_fc': _L1_ffn_in['W_fc'], 'L1_ffn_W_proj': _L1_ffn_in['W_proj'], 'L2_xattn_Wk': _L2_xattn_in['Wk'], 'L2_xattn_Wv': _L2_xattn_in['Wv'], 'L2_xattn_bv': _L2_xattn_in['bv'], 'L2_xattn_Wq': _L2_xattn_in['Wq'], 'L2_xattn_bq': _L2_xattn_in['bq'], 'L2_xattn_Wo': _L2_xattn_in['Wo'], 'L2_xattn_bo': _L2_xattn_in['bo'], 'L2_ffn_Wr': _L2_ffn_in['Wr'], 'L2_ffn_br': _L2_ffn_in['br'], 'L2_ffn_W1': _L2_ffn_in['W1'], 'L2_ffn_b1': _L2_ffn_in['b1'], 'L2_ffn_W2': _L2_ffn_in['W2'], 'L2_ffn_b2': _L2_ffn_in['b2'], 'L3_xattn_WQ': _L3_xattn_in['WQ'], 'L3_xattn_WK': _L3_xattn_in['WK'], 'L3_xattn_WV': _L3_xattn_in['WV'], 'L3_ffn_w_gate': _L3_ffn_in['w_gate'], 'L3_ffn_w_up': _L3_ffn_in['w_up'], 'L3_ffn_w_down': _L3_ffn_in['w_down']}

def reference(x, ctx_1024, g_xattn, g_ffn, L0_xattn_gamma_x, L0_xattn_beta_x, L0_xattn_gamma_l, L0_xattn_beta_l, L0_xattn_Wq, L0_xattn_Wkv, L0_xattn_Wo, L0_ffn_gate_w, L0_ffn_We, L1_xattn_ln1_g, L1_xattn_ln1_b, L1_xattn_ln2_g, L1_xattn_ln2_b, L1_xattn_Wq, L1_xattn_Wk, L1_xattn_Wv, L1_xattn_Wfc, L1_ffn_W_fc, L1_ffn_W_proj, L2_xattn_Wk, L2_xattn_Wv, L2_xattn_bv, L2_xattn_Wq, L2_xattn_bq, L2_xattn_Wo, L2_xattn_bo, L2_ffn_Wr, L2_ffn_br, L2_ffn_W1, L2_ffn_b1, L2_ffn_W2, L2_ffn_b2, L3_xattn_WQ, L3_xattn_WK, L3_xattn_WV, L3_ffn_w_gate, L3_ffn_w_up, L3_ffn_w_down):
    import jax
    import jax.numpy as jnp

    def _L0_xattn_ref(x, latents, gamma_x, beta_x, gamma_l, beta_l, Wq, Wkv, Wo):
        import jax, jax.numpy as jnp
        import numpy as np
        DIM = 128
        HEAD_DIM = 64
        NUM_HEADS = 8
        INNER = HEAD_DIM * NUM_HEADS
        ROT_DIM = HEAD_DIM
        ROPE_BASE = 10000.0
        EPS = 1e-05

        def layer_norm(x, g, b):
            mu = jnp.mean(x, axis=-1, keepdims=True)
            var = jnp.var(x, axis=-1, keepdims=True)
            return (x - mu) * jax.lax.rsqrt(var + EPS) * g + b

        def rope_rotate_k(k):
            n = k.shape[1]
            half = ROT_DIM // 2
            inv_freq = 1.0 / ROPE_BASE ** (jnp.arange(0, ROT_DIM, 2, dtype=jnp.float32) / ROT_DIM)
            theta = jnp.arange(n, dtype=jnp.float32)[:, None] * inv_freq[None, :]
            angles = jnp.concatenate([theta, theta], axis=-1)
            cos = jnp.cos(angles)[None, :, None, :].astype(k.dtype)
            sin = jnp.sin(angles)[None, :, None, :].astype(k.dtype)
            k_rope, k_pass = (k[..., :ROT_DIM], k[..., ROT_DIM:])
            neg_half = jnp.concatenate([-k_rope[..., half:], k_rope[..., :half]], axis=-1)
            k_rope = k_rope * cos + neg_half * sin
            return jnp.concatenate([k_rope, k_pass], axis=-1)
        b, n, _ = x.shape
        m = latents.shape[1]
        h, d = (NUM_HEADS, HEAD_DIM)
        scale = d ** (-0.5)
        xn = layer_norm(x, gamma_x, beta_x)
        ln = layer_norm(latents, gamma_l, beta_l)
        q = (ln @ Wq).reshape(b, m, h, d)
        kv_x = xn @ Wkv
        k_x, v_x = (kv_x[..., :INNER], kv_x[..., INNER:])
        kv_l = ln @ Wkv
        k_l, v_l = (kv_l[..., :INNER], kv_l[..., INNER:])
        k_x = k_x.reshape(b, n, h, d)
        v_x = v_x.reshape(b, n, h, d)
        k_x = rope_rotate_k(k_x)
        q = jnp.transpose(q, (0, 2, 1, 3)) * scale
        k_x = jnp.transpose(k_x, (0, 2, 1, 3))
        v_x = jnp.transpose(v_x, (0, 2, 1, 3))
        k_l = jnp.transpose(k_l.reshape(b, m, h, d), (0, 2, 1, 3))
        v_l = jnp.transpose(v_l.reshape(b, m, h, d), (0, 2, 1, 3))
        k = jnp.concatenate([k_x, k_l], axis=2)
        v = jnp.concatenate([v_x, v_l], axis=2)
        sim = jnp.einsum('bhid,bhjd->bhij', q, k)
        attn = jax.nn.softmax(sim, axis=-1)
        out = jnp.einsum('bhij,bhjd->bhid', attn, v)
        out = jnp.transpose(out, (0, 2, 1, 3)).reshape(b, m, INNER)
        return out @ Wo

    def _L0_ffn_ref(x, gate_w, We):
        import jax, jax.numpy as jnp
        import numpy as np
        top_k = 2
        logits = jnp.einsum('btd,ed->bte', x, gate_w)
        top_val, top_idx = jax.lax.top_k(logits, top_k)
        top_w = jax.nn.softmax(top_val, axis=-1)
        y_all = jnp.einsum('btd,edm->btem', x, We)
        x_experts = jnp.take_along_axis(y_all, top_idx[..., None], axis=2)
        out = jnp.sum(x_experts * top_w[..., None], axis=2)
        return out

    def _L1_xattn_ref(src, tgt, ln1_g, ln1_b, ln2_g, ln2_b, Wq, Wk, Wv, Wfc):
        import jax, jax.numpy as jnp
        import numpy as np
        DIM = 128
        HEADS = 16
        HEAD_DIM = DIM // HEADS
        SCALE = HEAD_DIM ** (-0.5)
        EPS = 1e-05

        def layer_norm(x, g, b):
            mu = jnp.mean(x, axis=-1, keepdims=True)
            var = jnp.mean(jnp.square(x - mu), axis=-1, keepdims=True)
            return (x - mu) * jax.lax.rsqrt(var + EPS) * g + b
        B = src.shape[0]
        s = layer_norm(src, ln1_g, ln1_b)
        t = layer_norm(tgt, ln2_g, ln2_b)
        q = (t @ Wq).reshape(B, -1, HEADS, HEAD_DIM)
        k = (s @ Wk).reshape(B, -1, HEADS, HEAD_DIM)
        v = (s @ Wv).reshape(B, -1, HEADS, HEAD_DIM)
        attn = jnp.einsum('bqhd,bkhd->bhqk', q, k) * SCALE
        attn = jax.nn.softmax(attn, axis=-1)
        out = jnp.einsum('bhqk,bkhd->bqhd', attn, v).reshape(B, -1, DIM)
        return out @ Wfc

    def _L1_ffn_ref(x, W_fc, W_proj):
        import jax, jax.numpy as jnp
        import numpy as np
        import math
        BETA = 0.9
        THRESHOLD = 1.0
        NUM_STEPS = 5
        ALPHA = 2.0

        @jax.custom_vjp
        def spike_fn(u):
            return (u > 0).astype(u.dtype)

        def _spike_fwd(u):
            return (spike_fn(u), u)

        def _spike_bwd(u, g):
            s = jnp.pi / 2.0 * ALPHA * u
            return (g * (ALPHA / 2.0) / (1.0 + s * s),)
        spike_fn.defvjp(_spike_fwd, _spike_bwd)
        h = jnp.square(jax.nn.relu(jnp.einsum('bsd,fd->bsf', x, W_fc)))
        y = jnp.einsum('bsf,df->bsd', h, W_proj)

        def step(mem, _):
            reset = jax.lax.stop_gradient(spike_fn(mem - THRESHOLD))
            mem_new = BETA * mem + y - reset * THRESHOLD
            spk = spike_fn(mem_new - THRESHOLD)
            return (mem_new, spk)
        mem0 = jnp.zeros_like(y)
        _, spks = jax.lax.scan(step, mem0, None, length=NUM_STEPS)
        return jnp.sum(spks, axis=0) / NUM_STEPS

    def _L2_xattn_ref(k, v, q, Wk, Wv, bv, Wq, bq, Wo, bo):
        import jax, jax.numpy as jnp
        import numpy as np
        D_MODEL = 128
        B, S = (4, 256)
        kp = jnp.einsum('bsd,ed->bse', k, Wk)
        vp = jnp.einsum('bsd,ed->bse', v, Wv) + bv
        qp = jnp.einsum('bsd,ed->bse', q, Wq) + bq
        scale = 1.0 / jnp.sqrt(jnp.float32(kp.shape[-1]))
        scores = jnp.einsum('bqd,bkd->bqk', qp, kp) * scale
        probs = jax.nn.softmax(scores, axis=-1)
        ctx = jnp.einsum('bqk,bkd->bqd', probs, vp)
        return jnp.einsum('bqd,ed->bqe', ctx, Wo) + bo

    def _L2_ffn_ref(x, Wr, br, W1, b1, W2, b2):
        import jax, jax.numpy as jnp
        import numpy as np
        B, N, E = (8, 256, 128)
        NUM_EXPERTS = 8
        HIDDEN = 192
        TOP_K = 2
        b, n, e = x.shape
        T = b * n
        logits = jnp.einsum('bne,ec->bnc', x, Wr) + br
        probs = jax.nn.softmax(logits, axis=-1)
        topk_probs, topk_idx = jax.lax.top_k(probs, TOP_K)
        flat_x = x.reshape(T, e)
        flat_w = topk_probs.reshape(T, TOP_K)
        flat_idx = topk_idx.reshape(T, TOP_K)
        onehot = jax.nn.one_hot(flat_idx, NUM_EXPERTS, dtype=flat_w.dtype)
        combine = jnp.einsum('tk,tke->te', flat_w, onehot)
        out = jnp.zeros_like(flat_x)
        for ei in range(NUM_EXPERTS):
            h = jax.nn.gelu(flat_x @ W1[ei] + b1[ei], approximate=False)
            y = h @ W2[ei] + b2[ei]
            out = out + combine[:, ei:ei + 1] * y
        return out.reshape(b, n, e)

    def _L3_xattn_ref(Q, K, V, WQ, WK, WV):
        import jax, jax.numpy as jnp
        import numpy as np
        import math
        D = 128
        q = jnp.einsum('bsd,ed->bse', Q, WQ)
        k = jnp.einsum('bsd,ed->bse', K, WK)
        v = jnp.einsum('bsd,ed->bse', V, WV)
        scores = jnp.einsum('bqd,bkd->bqk', q, k)
        S = scores.shape[-1]
        causal = jnp.tril(jnp.ones((S, S), dtype=bool))
        scores = jnp.where(causal, scores, 0.0) / math.sqrt(D)
        probs = jax.nn.softmax(scores, axis=-1)
        return jnp.einsum('bqk,bkd->bqd', probs, v)

    def _L3_ffn_ref(x, w_gate, w_up, w_down):
        import jax, jax.numpy as jnp
        import numpy as np
        BLOCK = 32
        W_BITS = 4
        ACT_BITS = 16

        def act_qdq(x):
            qmax = 2.0 ** (ACT_BITS - 1) - 1.0
            scale = jnp.maximum(jnp.max(jnp.abs(x)) / qmax, 1e-12)
            return jnp.clip(jnp.round(x / scale), -qmax - 1.0, qmax) * scale

        def fixed_qdq_u16(x):
            scale = 1.0 / 65536.0
            return jnp.clip(jnp.round(x / scale), 0.0, 65535.0) * scale

        def lpbq_dequant(w):
            O, I = w.shape
            qmax = 2.0 ** (W_BITS - 1) - 1.0
            wb = w.reshape(O, I // BLOCK, BLOCK)
            s = jnp.maximum(jnp.max(jnp.abs(wb), axis=-1, keepdims=True) / qmax, 1e-12)
            wq = jnp.clip(jnp.round(wb / s), -qmax - 1.0, qmax) * s
            return wq.reshape(O, I)
        x = act_qdq(x)
        up = act_qdq(x @ lpbq_dequant(w_up).T)
        gate = act_qdq(x @ lpbq_dequant(w_gate).T)
        sig = fixed_qdq_u16(jax.nn.sigmoid(gate))
        gate = act_qdq(gate * sig)
        o = act_qdq(gate * up)
        return o @ lpbq_dequant(w_down).T
    x = x + jnp.tanh(g_xattn[0]) * _L0_xattn_ref(ctx_1024, _layernorm(x, axis=-1), L0_xattn_gamma_x, L0_xattn_beta_x, L0_xattn_gamma_l, L0_xattn_beta_l, L0_xattn_Wq, L0_xattn_Wkv, L0_xattn_Wo)
    x = x + jnp.tanh(g_ffn[0]) * _L0_ffn_ref(_layernorm(x, axis=-1), L0_ffn_gate_w, L0_ffn_We)
    x = x + jnp.tanh(g_xattn[1]) * _L1_xattn_ref(ctx_1024, _layernorm(x, axis=-1), L1_xattn_ln1_g, L1_xattn_ln1_b, L1_xattn_ln2_g, L1_xattn_ln2_b, L1_xattn_Wq, L1_xattn_Wk, L1_xattn_Wv, L1_xattn_Wfc)
    x = x + jnp.tanh(g_ffn[1]) * _L1_ffn_ref(_layernorm(x, axis=-1), L1_ffn_W_fc, L1_ffn_W_proj)
    x = x + jnp.tanh(g_xattn[2]) * _L2_xattn_ref(ctx_1024, ctx_1024, _layernorm(x, axis=-1), L2_xattn_Wk, L2_xattn_Wv, L2_xattn_bv, L2_xattn_Wq, L2_xattn_bq, L2_xattn_Wo, L2_xattn_bo)
    x = x + jnp.tanh(g_ffn[2]) * _L2_ffn_ref(_layernorm(x, axis=-1), L2_ffn_Wr, L2_ffn_br, L2_ffn_W1, L2_ffn_b1, L2_ffn_W2, L2_ffn_b2)
    x = x + jnp.tanh(g_xattn[3]) * _L3_xattn_ref(_layernorm(x, axis=-1), ctx_1024, ctx_1024, L3_xattn_WQ, L3_xattn_WK, L3_xattn_WV)
    x = x + jnp.tanh(g_ffn[3]) * _L3_ffn_ref(_layernorm(x, axis=-1), L3_ffn_w_gate, L3_ffn_w_up, L3_ffn_w_down)
    return x

_drawn_inputs = setup_inputs


def setup_inputs(seed=0):
    import zlib

    import numpy as np

    out = dict(_drawn_inputs(seed))
    spreads = {'L0_xattn_gamma_x': (1.0, 0.2),
     'L0_xattn_beta_x': (0.0, 0.1),
     'L0_xattn_gamma_l': (1.0, 0.2),
     'L0_xattn_beta_l': (0.0, 0.1),
     'L1_xattn_ln1_g': (1.0, 0.2),
     'L1_xattn_ln1_b': (0.0, 0.1),
     'L1_xattn_ln2_g': (1.0, 0.2),
     'L1_xattn_ln2_b': (0.0, 0.36),
     'L2_xattn_bv': (0.0, 0.1),
     'L2_xattn_bq': (0.0, 0.639),
     'L2_xattn_bo': (0.0, 0.1),
     'L2_ffn_br': (0.0, 0.8),
     'L2_ffn_b1': (0.0, 0.8),
     'L2_ffn_b2': (0.0, 0.651)}
    factors = {'g_ffn': 38.112,
     'L2_ffn_Wr': 5.311,
     'L2_ffn_W1': 8.0,
     'L2_ffn_W2': 8.0,
     'L3_ffn_w_gate': 8.0,
     'L3_ffn_w_up': 8.0,
     'L3_ffn_w_down': 8.0}
    for name, (base, spread) in spreads.items():
        noise = np.random.default_rng([zlib.crc32(name.encode()), seed]).standard_normal(out[name].shape)
        drawn = base * np.exp(spread * noise) if base else spread * noise
        out[name] = jnp.asarray(drawn.astype(out[name].dtype))
    for name, factor in factors.items():
        out[name] = (out[name] * factor).astype(out[name].dtype)
    return out
```

```python
from contextlib import ExitStack

import concourse.bass as bass
from concourse import mybir

ALU = mybir.AluOpType
ACT = mybir.ActivationFunctionType
AX = mybir.AxisListType
F32 = mybir.dt.float32
I16 = mybir.dt.int16
U16 = mybir.dt.uint16
U32 = mybir.dt.uint32

P = 128
SEQ = 64
D = 128
PAIR = P // SEQ
EPS = 1e-5
EXPERTS = 8
GROUP = 4
GCOLS = GROUP * P
H0, HD0 = 8, 64
INNER = H0 * HD0
HPAIRS = H0 // 2
VW = HD0 + 1
H1, HD1 = 16, 8
ROWS4 = 4
FF1 = 512
SPIKE_STEPS, BETA = 5, 0.9
HID2 = 192
CHUNKS2 = EXPERTS * HID2 // P
FF3 = 384
CHUNKS3 = FF3 // P
BLOCK = 32
QMAX_A, QMAX_W, QSIG = 32767.0, 7.0, 65536.0

C_IDENT, C_COS, C_SIN, C_IOTA, C_MASK4, C_CAUSAL, C_MHALF, C_ONES = 0, 128, 192, 256, 264, 272, 336, 340
C_END = C_ONES + 128


class Tile:

    def __init__(self, idx, par):
        self.idx, self.par = idx, par

    def has(self, k):
        return not isinstance(self.idx, int) or self.idx >= k

    def back(self, k):
        return Tile(self.idx - k, (self.par - k) % 2)


class Signal:

    def __init__(self, sem, per=1, base=0):
        self.sem, self.per, self.base = sem, per, base

    def __call__(self, t, k=None):
        return self.sem, self.base + self.per * t.idx + (self.per if k is None else k)

    def all(self, n):
        return self.sem, self.base + self.per * n


class Transfers:

    def __init__(self, even, odd, base):
        self.sems, self.base = (even, odd), base

    def at(self, t):
        return self.sems[t.par]

    def __call__(self, t):
        return self.sems[t.par], self.base + (t.idx - t.par) * 8 + 16

    def wait_all(self, eng, n):
        for sem in self.sems:
            eng.wait_ge(sem, self.base + n // 2 * 16)


def steps(eng, n, lead, lag, body):
    def fixed(s):
        body(lambda k: Tile(s + k, (s + k) % 2) if 0 <= s + k < n else None)

    first = (lag + 3) // 2 * 2
    end = first + (n - lead - first) // 2 * 2
    if end - first < 4:
        for s in range(-lead, n + lag):
            fixed(s)
        return
    for s in range(-lead, first):
        fixed(s)
    with eng.Fori(first // 2, end // 2) as i:
        for u in range(2):
            body(lambda k, u=u: Tile(i * 2 + (u + k), (u + k) % 2))
    for s in range(end, n + lag):
        fixed(s)


class Kit:

    def __init__(self, nc, ctx, args, out):
        self.nc, self.ctx, self.a, self.out = nc, ctx, args, out
        self.T = args["x"].shape[0] // PAIR
        self.psum = ctx.enter_context(nc.psum_tensor("banks", [P, 8, 512], F32))
        self.x = self.sb("x_tiles", [P, self.T, D])
        self.konst = self.sb("konst", [P, C_END])
        self.arena = self.sb("arena", [P, 30500])
        self.taken, self.fronts, self.sems, self.counted = 0, {}, {}, {}
        self.ident = self.konst[:, C_IDENT:C_IDENT + P]
        self.st = self.sb("bn_parts", [P, GROUP, 2, 6])
        self.mv = self.sb("mean_var", [P, GROUP, 2, 2])
        self.ve = self.sb("var_eps", [P, GROUP, 2])
        self.rstd = self.sb("rstd", [P, GROUP, 2])
        self.xh = self.sb("xhat", [P, GROUP, D])
        self.gate_pass = self.sem("form_has_no_register_wait")
        names = ("stats", "aggr", "vareps", "rstd_ready", "xhat_ready", "x_updated")
        self.shared = {n: self.sem(n) for n in names}
        self.ctxT_dram = nc.dram_tensor("ctxT_scratch", [self.T, P, P], F32, kind="Internal").ap()
        self.z1T_dram = nc.dram_tensor("z1T_scratch", [self.T, P, P], F32, kind="Internal").ap()
        self.ctxT_stored, self.z1T_stored = (
            self.transfers(self.T, n) for n in ("ctxT_stored", "z1T_stored"))

    def sb(self, name, shape, dt=F32):
        return self.ctx.enter_context(self.nc.sbuf_tensor(name, shape, dt))

    def sem(self, name):
        return self.ctx.enter_context(self.nc.semaphore(name))

    def shared_sem(self, name):
        if name not in self.sems:
            self.sems[name], self.counted[name] = self.sem(name), 0
        return self.sems[name], self.counted[name]

    def sig(self, n, name, per=1):
        sem, base = self.shared_sem(name)
        self.counted[name] = base + per * n
        return Signal(sem, per, base)

    def sigs(self, n, names):
        return {name: self.sig(n, name, per) for name, per in names.items()}

    def transfers(self, n, name):
        (even, base), (odd, _) = (self.shared_sem(name + side) for side in ("_even", "_odd"))
        for side in ("_even", "_odd"):
            self.counted[name + side] = base + n // 2 * 16
        return Transfers(even, odd, base)

    def stage_memory(self):
        self.taken = 0

    def take(self, cols):
        a = self.arena[:, self.taken:self.taken + cols]
        self.taken += cols
        assert self.taken <= 30500, self.taken
        return a

    def front(self, no):
        if no not in self.fronts:
            self.fronts[no] = {n: Signal(s, 1, no * self.T) for n, s in self.shared.items()}
        return self.fronts[no]

    def hold(self, eng):
        eng.sem_inc(self.gate_pass, 1)


def tile_stats(k, f, dve, t, slot):
    dve.bn_stats(k.st[:, slot, 0, :], k.x[:, t.idx, :]).then_inc(f["stats"].sem, 1)
    dve.wait_ge(*f["stats"](t))
    k.hold(dve)
    dve.bn_aggr(k.mv[:, slot, 0, :], k.st[:, slot, 0, :]).then_inc(f["aggr"].sem, 1)


def tile_rstd(k, f, pool, t, slot, twice):
    pool.wait_ge(*f["aggr"](t))
    k.hold(pool)
    pool.tensor_scalar(k.ve[:, slot, 0:1], k.mv[:, slot, 0, 1:2], 1.0 + EPS if twice else 1.0,
                       EPS * EPS if twice else EPS, ALU.mult, ALU.add).then_inc(f["vareps"].sem, 1)
    pool.wait_ge(*f["vareps"](t))
    pool.tensor_tensor(k.rstd[:, slot, 0:1], k.ve[:, slot, 0:1], k.konst[:, C_MHALF:C_MHALF + 1],
                       ALU.pow).then_inc(f["rstd_ready"].sem, 1)


def tile_xhat(k, f, dve, t, slot, out=None):
    dve.wait_ge(*f["rstd_ready"](t))
    dve.tensor_scalar(k.xh[:, slot, :] if out is None else out, k.x[:, t.idx, :], k.mv[:, slot, 0, 0:1],
                      k.rstd[:, slot, 0:1], ALU.subtract, ALU.mult).then_inc(f["xhat_ready"].sem, 1)


def stage_start(eng, k, no):
    if no:
        eng.wait_ge(*k.front(no)["x_updated"].all(0))
    if no == 1:
        k.ctxT_stored.wait_all(eng, k.T)
        k.z1T_stored.wait_all(eng, k.T)


def prepare(k):
    nc, a, ps = k.nc, k.a, k.psum
    sb = k.sb
    raw = k.take
    k.gates, k.spike_gate = sb("gates", [P, 8]), sb("spike_gate", [P, 1])
    gates_raw = raw(8)
    k.wq0, k.wk0, k.wv0, k.wr0 = (sb(n, [P, INNER]) for n in ("wq0", "wk0", "wv0", "wk0_rotated"))
    k.wo0 = sb("wo0", [P, HPAIRS, D])
    k.aff = sb("affine_columns", [P, 8])
    k.we0, k.wg0 = sb("we0", [P, EXPERTS, D]), sb("wg0", [P, EXPERTS])
    gw_raw = raw(D)
    k.w1a = sb("w1a", [P, 4, D])
    k.wfc1, k.wpr1 = sb("wfc1", [P, FF1]), sb("wpr1", [P, 4, D])
    fc_raw, pr_raw = raw(4 * D), raw(FF1)
    w2_raw, w3_raw = raw(4 * D), raw(3 * D)
    woT = raw(D)
    bcol = raw(2)
    bo_row = raw(D)
    bv_wide, b1_raw = raw(D), raw(P)
    k.A = [sb("A2", [P, D]), sb("A3", [P, D])]
    k.B = [sb("B2", [P, D]), sb("B3", [P, D])]
    k.bqk, k.bout = sb("bqk", [P, 1]), sb("bout", [P, D])
    k.wr2, k.br2 = sb("wr2", [P, EXPERTS]), sb("br2", [P, EXPERTS])
    k.w1s, k.w1tail = sb("w1s", [P, EXPERTS, P]), sb("w1tail", [P, EXPERTS // 2, P])
    k.w2a, k.w2b = sb("w2a", [P, EXPERTS, D]), sb("w2b", [P, EXPERTS // 2, D])
    k.b1c, k.b2r = sb("b1c", [P, CHUNKS2]), sb("b2r", [EXPERTS, D])
    q_raw = raw(3 * FF3).rearrange("p (w b i) -> p w b i", w=3, i=BLOCK)
    q_max, q_inv = raw(36).rearrange("p (w b) -> p w b", w=3), raw(36).rearrange("p (w b) -> p w b", w=3)
    q_int = raw(3 * FF3 // 2).bitcast(I16).rearrange("p (w b i) -> p w b i", w=3, i=BLOCK)
    q_clip = raw(3 * FF3 // 2).bitcast(I16).rearrange("p (w b i) -> p w b i", w=3, i=BLOCK)
    q_deq = raw(3 * FF3).rearrange("p (w b i) -> p w b i", w=3, i=BLOCK)
    k.wup3, k.wgt3, k.wdn3 = (sb(n, [P, CHUNKS3, D]) for n in ("wup3", "wgt3", "wdn3"))

    loaded, x_loaded = k.sem("weights_loaded"), k.sem("x_loaded")
    gates_ready, built, dequant = k.sem("gates_ready"), k.sem("weights_built"), k.sem("dequantised")
    turned, turned_sb, folded, folded_sb = (k.sem(n) for n in ("turned", "turned_sb", "folded", "folded_sb"))
    wkv = a["L0_xattn_Wkv"]
    loads = [
        (k.konst[:, :], a["shape_constants"]),
        (gates_raw[:, 0:4], a["g_xattn"].partition_broadcast(P)),
        (gates_raw[:, 4:8], a["g_ffn"].partition_broadcast(P)),
        (k.wq0[:, :], a["L0_xattn_Wq"]), (k.wk0[:, :], wkv[:, 0:INNER]), (k.wv0[:, :], wkv[:, INNER:2 * INNER]),
        (k.wo0[:, :, :], a["L0_xattn_Wo"].rearrange("(c p) d -> p c d", p=P)),
        (k.we0[:, :, :], a["L0_ffn_We"].rearrange("e d m -> d e m")),
        (gw_raw[0:EXPERTS, :], a["L0_ffn_gate_w"]),
        (fc_raw.rearrange("p (c d) -> p c d", c=4), a["L1_ffn_W_fc"].rearrange("(c p) d -> p c d", p=P)),
        (pr_raw, a["L1_ffn_W_proj"]),
        (bo_row[0:1, :], a["L2_xattn_bo"].rearrange("(a n) -> a n", a=1)),
        (k.wr2[:, :], a["L2_ffn_Wr"]), (k.br2[:, :], a["L2_ffn_br"].partition_broadcast(P)),
        (k.w1s[:, :, :], a["L2_ffn_W1"][:, :, 0:P].rearrange("e d h -> d e h")),
        (k.w2a[:, :, :], a["L2_ffn_W2"][:, 0:P, :].rearrange("e h d -> h e d")),
        (q_raw[:, 0].rearrange("p (c b) i -> p c (b i)", c=CHUNKS3), a["L3_ffn_w_up"].rearrange("(c p) d -> p c d", p=P)),
        (q_raw[:, 1].rearrange("p (c b) i -> p c (b i)", c=CHUNKS3), a["L3_ffn_w_gate"].rearrange("(c p) d -> p c d", p=P)),
        (q_raw[:, 2].rearrange("p b i -> p (b i)"), a["L3_ffn_w_down"]),
    ]
    for i, n in enumerate(("L0_xattn_gamma_x", "L0_xattn_beta_x", "L0_xattn_gamma_l", "L0_xattn_beta_l",
                           "L1_xattn_ln1_g", "L1_xattn_ln1_b", "L1_xattn_ln2_g", "L1_xattn_ln2_b")):
        loads.append((k.aff[:, i:i + 1], a[n].rearrange("(p a) -> p a", a=1)))
    for i, n in enumerate(("Wq", "Wk", "Wv", "Wfc")):
        loads.append((k.w1a[:, i, :], a["L1_xattn_" + n]))
    for i, n in enumerate(("Wk", "Wv", "Wq", "Wo")):
        loads.append((w2_raw[:, i * D:(i + 1) * D], a["L2_xattn_" + n]))
    for i, n in enumerate(("WQ", "WK", "WV")):
        loads.append((w3_raw[:, i * D:(i + 1) * D], a["L3_xattn_" + n]))
    for i, n in enumerate(("bv", "bq")):
        loads.append((bcol[:, i:i + 1], a["L2_xattn_" + n].rearrange("(p a) -> p a", a=1)))
    for h in range(2):
        w2 = a["L2_ffn_W2"].rearrange("(k h) n d -> h n k d", h=2)
        b1 = a["L2_ffn_b1"].rearrange("(k h) n -> h k n", h=2)[:, :, P:HID2]
        w1 = a["L2_ffn_W1"].rearrange("(k h) d n -> h d k n", h=2)
        loads.append((k.w1tail[:, :, h * 64:h * 64 + 64], w1[h][:, :, P:HID2]))
        loads.append((k.w2b[h * 64:h * 64 + 64, :, :], w2[h, P:HID2]))
        loads.append((b1_raw[EXPERTS:CHUNKS2, h * 64:h * 64 + 64], b1[h]))
    loads.append((b1_raw[0:EXPERTS, :], a["L2_ffn_b1"][:, 0:P]))
    loads.append((k.b2r[:, :], a["L2_ffn_b2"]))
    xv = a["x"].rearrange("(t b) s d -> (b s) t d", b=PAIR)
    XPARTS = 4

    def sync(sp):
        for j in range(XPARTS):
            n = k.T // XPARTS
            sp.dma_start(k.x[:, j * n:(j + 1) * n, :], xv[:, j * n:(j + 1) * n, :]).then_inc(x_loaded, 16)
        for dst, src in loads[0::2]:
            sp.dma_start(dst, src).then_inc(loaded, 16)

    def all_loaded(eng):
        eng.wait_ge(loaded, 16 * len(loads))

    def scalar(act):
        for dst, src in loads[1::2]:
            act.dma_start(dst, src).then_inc(loaded, 16)
        all_loaded(act)
        act.activation(k.gates[:, :], gates_raw, ACT.Tanh).then_inc(gates_ready, 1)
        act.wait_ge(gates_ready, 1)
        act.activation(k.spike_gate[:, :], k.gates[:, 5:6], ACT.Copy, scale=1.0 / SPIKE_STEPS).then_inc(gates_ready, 1)
        act.wait_ge(turned, 1)
        for dst, src in ((k.wfc1[:, :], ps[:, 0, :]), (k.wpr1[:, :, :].rearrange("p c d -> p (c d)"), ps[:, 1, :]),
                         (woT, ps[:, 2, 0:D]), (k.wg0[:, :], ps[:, 2, 2 * D:2 * D + EXPERTS]),
                         (k.b1c[:, :], ps[:, 2, 3 * D:3 * D + CHUNKS2])):
            act.activation(dst, src, ACT.Copy).then_inc(turned_sb, 1)
        act.wait_ge(gates_ready, 1)
        act.activation(k.B[1][:, :], ps[:, 2, D:2 * D], ACT.Copy, scale=k.gates[:, 3:4]).then_inc(turned_sb, 1)
        act.wait_ge(turned, 2)
        for i, w in enumerate((k.wup3, k.wgt3, k.wdn3)):
            act.activation(w[:, :, :].rearrange("p c d -> p (c d)"), ps[:, 3 + i, 0:3 * D], ACT.Copy).then_inc(turned_sb, 1)
        act.wait_ge(folded, 1)
        act.activation(k.A[0][:, :], ps[:, 6, 0:D], ACT.Copy).then_inc(folded_sb, 1)
        act.activation(k.A[1][:, :], ps[:, 6, D:2 * D], ACT.Copy).then_inc(folded_sb, 1)
        act.activation(k.bqk[:, :], ps[:, 6, 2 * D:2 * D + 1], ACT.Copy).then_inc(folded_sb, 1)
        act.wait_ge(folded, 2)
        act.activation(k.B[0][:, :], ps[:, 7, 0:D], ACT.Copy, scale=k.gates[:, 2:3]).then_inc(folded_sb, 1)
        act.activation(k.bout[:, :], ps[:, 7, D:2 * D], ACT.Copy, scale=k.gates[:, 2:3]).then_inc(folded_sb, 1)

    def vector(dve):
        all_loaded(dve)
        src = k.wk0[:, :].rearrange("p (h s i) -> p h s i", s=2, i=HD0 // 2)
        dst = k.wr0[:, :].rearrange("p (h s i) -> p h s i", s=2, i=HD0 // 2)
        dve.tensor_scalar(dst[:, :, 0], src[:, :, 1], -1.0, None, ALU.mult).then_inc(built, 1)
        dve.tensor_copy(dst[:, :, 1], src[:, :, 0]).then_inc(built, 1)
        dve.tensor_scalar(bv_wide, k.konst[:, C_ONES:C_ONES + P], bcol[:, 0:1], None, ALU.mult).then_inc(built, 1)
        blocks = [P, 3, 12, BLOCK]
        dve.tensor_reduce(q_max, q_raw, AX.X, ALU.max, apply_absolute_value=True).then_inc(dequant, 1)
        dve.wait_ge(dequant, 1)
        dve.tensor_scalar(q_max, q_max, 1.0 / QMAX_W, 1e-12, ALU.mult, ALU.max).then_inc(dequant, 1)
        dve.wait_ge(dequant, 2)
        dve.reciprocal(q_inv, q_max).then_inc(dequant, 1)
        dve.wait_ge(dequant, 3)
        for w in range(3):
            dve.tensor_tensor(q_int[:, w], q_raw[:, w], q_inv[:, w].unsqueeze(2).broadcast_to(blocks[:1] + blocks[2:]),
                              ALU.mult).then_inc(dequant, 1)
        dve.wait_ge(dequant, 6)
        dve.tensor_scalar(q_clip, q_int, -QMAX_W - 1.0, QMAX_W, ALU.max, ALU.min).then_inc(dequant, 1)
        dve.wait_ge(dequant, 7)
        for w in range(3):
            dve.tensor_tensor(q_deq[:, w], q_clip[:, w], q_max[:, w].unsqueeze(2).broadcast_to(blocks[:1] + blocks[2:]),
                              ALU.mult).then_inc(dequant, 1)

    def tensor(pe):
        all_loaded(pe)
        for c in range(4):
            pe.transpose(ps[:, 0, c * P:(c + 1) * P], fc_raw[:, c * D:(c + 1) * D], k.ident)
            pe.transpose(ps[:, 1, c * P:(c + 1) * P], pr_raw[:, c * P:(c + 1) * P], k.ident)
        pe.transpose(ps[:, 2, 0:D], w2_raw[:, 3 * D:4 * D], k.ident)
        pe.transpose(ps[:, 2, D:2 * D], w3_raw[:, 2 * D:3 * D], k.ident)
        pe.transpose(ps[:, 2, 2 * D:2 * D + EXPERTS], gw_raw[0:EXPERTS, :],
                     k.konst[0:EXPERTS, C_IDENT:C_IDENT + EXPERTS])
        pe.transpose(ps[:, 2, 3 * D:3 * D + CHUNKS2], b1_raw[0:CHUNKS2, :],
                     k.konst[0:CHUNKS2, C_IDENT:C_IDENT + CHUNKS2]).then_inc(turned, 1)
        pe.matmul(ps[:, 6, 0:D], w2_raw[:, 2 * D:3 * D], w2_raw[:, 0:D], start=True, stop=True)
        pe.matmul(ps[:, 6, D:2 * D], w3_raw[:, 0:D], w3_raw[:, D:2 * D], start=True, stop=True)
        pe.matmul(ps[:, 6, 2 * D:2 * D + 1], w2_raw[:, 0:D], bcol[:, 1:2], start=True, stop=True).then_inc(folded, 1)
        pe.wait_ge(dequant, 10)
        for w in range(3):
            for c in range(3):
                flat = q_deq[:, w].rearrange("p b i -> p (b i)")[:, c * P:(c + 1) * P]
                mm = pe.transpose(ps[:, 3 + w, c * P:(c + 1) * P], flat, k.ident)
        mm.then_inc(turned, 1)
        pe.wait_ge(turned_sb, 6)
        pe.wait_ge(built, 3)
        pe.matmul(ps[:, 7, 0:D], w2_raw[:, D:2 * D], woT, start=True, stop=True)
        pe.matmul(ps[:, 7, D:2 * D], bv_wide, woT, start=True, stop=False)
        pe.matmul(ps[:, 7, D:2 * D], k.konst[0:1, C_ONES:C_ONES + P], bo_row[0:1, :], start=False, stop=True)\
            .then_inc(folded, 1)

    def ready(eng):
        eng.wait_ge(x_loaded, 16 * XPARTS)
        all_loaded(eng)
        eng.wait_ge(gates_ready, 2)
        eng.wait_ge(built, 3)
        eng.wait_ge(turned_sb, 9)
        eng.wait_ge(folded_sb, 5)

    k.ready = ready
    return dict(sync=sync, scalar=scalar, vector=vector, tensor=tensor)


def attention0(k, no):
    nc, ps, T = k.nc, k.psum, k.T
    f = k.front(no)
    f["xT_psum"] = k.sig(T, "xT_psum")
    k.stage_memory()
    two = lambda n: [k.take(n) for _ in range(2)]
    cin, zh = two(D), two(D)
    Z = [z.rearrange("p (b s i) -> p b s i", b=PAIR, s=2) for z in two(2 * P)]
    z1o, cto = two(P), two(P)
    KT = k.take(HPAIRS * 4 * SEQ).rearrange("p (c s b i) -> p c s b i", c=HPAIRS, s=2, b=PAIR)
    rotA, rotB = k.take(512), k.take(512)
    QBD = k.take(HPAIRS * PAIR * P).rearrange("p (c b h i) -> p c b h i", c=HPAIRS, b=PAIR, h=2)
    V = [v.rearrange("p (b h e) -> p b h e", b=PAIR, e=VW) for v in two(PAIR * H0 * VW)]
    mx = k.take(PAIR * HPAIRS)
    prob = k.take(PAIR * 512).rearrange("p (b n) -> p b n", b=PAIR)
    probT = k.take(PAIR * 512).rearrange("p (b c n) -> p b c n", b=PAIR, c=HPAIRS)
    rec = k.take(H0)
    on = k.take(INNER)
    oT = k.take(INNER)
    s = k.sigs(T, dict(
        zhat=1, z_ready=3, ctxT_sb=1, k_psum=1, k2_psum=1, q_psum=1, v_psum=2, kcos=1, ksin=1,
        krot=1, klat=1, qbd=2, v_sb=2, s_psum=2, smax=2, sshift=2, prob=2, pt_psum=2, pt_sb=2, av=1, recip=1,
        onorm=1, ot_psum=1, ot_sb=1, out_psum=1))
    ctx_loaded = k.transfers(T, "ctx_loaded")
    preset = k.sem("L0_preset")
    ctx_dram = k.a["ctx_1024"].rearrange("(t b) s d -> t (b s) d", b=PAIR)
    cosT = k.konst[:, C_COS:C_COS + SEQ].unsqueeze(1).broadcast_to([P, 8, SEQ])
    sinT = k.konst[:, C_SIN:C_SIN + SEQ].unsqueeze(1).broadcast_to([P, 8, SEQ])

    def sync(sp):
        k.ready(sp)

        def body(at):
            if t := at(3):
                if t.has(2):
                    sp.wait_ge(*f["xT_psum"](t.back(2)))
                sp.dma_start(cin[t.par], ctx_dram[t.idx]).then_inc(ctx_loaded.at(t), 16)
            if t := at(1):
                sp.wait_ge(*s["z_ready"](t))
                sp.dma_start(k.z1T_dram[t.idx], z1o[t.par]).then_inc(k.z1T_stored.at(t), 16)
                sp.wait_ge(*s["ctxT_sb"](t))
                sp.dma_start(k.ctxT_dram[t.idx], cto[t.par]).then_inc(k.ctxT_stored.at(t), 16)
        steps(sp, T, 3, 1, body)

    def gpsimd(pool):
        k.ready(pool)
        pool.memset(V[0][:, :, :, HD0:VW], 1.0).then_inc(preset, 1)
        pool.memset(V[1][:, :, :, HD0:VW], 1.0).then_inc(preset, 1)
        pool.memset(QBD, 0.0).then_inc(preset, 1)
        pool.wait_ge(preset, 3)

        def body(at):
            if t := at(2):
                sl = t.par
                pool.wait_ge(*f["aggr"](t))
                k.hold(pool)
                pool.tensor_scalar(k.ve[:, sl, 0:1], k.mv[:, sl, 0, 1:2], 1.0 + EPS, EPS * EPS, ALU.mult, ALU.add)
                pool.tensor_scalar(k.ve[:, sl, 1:2], k.mv[:, sl, 1, 1:2], 1.0, EPS, ALU.mult, ALU.add)\
                    .then_inc(f["vareps"].sem, 1)
                pool.wait_ge(*f["vareps"](t))
                pool.tensor_tensor(k.rstd[:, sl, :], k.ve[:, sl, :],
                                   k.konst[:, C_MHALF:C_MHALF + 2], ALU.pow).then_inc(f["rstd_ready"].sem, 1)
            if t := at(1):
                pool.wait_ge(*s["kcos"](t))
                k.hold(pool)
                pool.wait_ge(*s["ksin"](t))
                pool.tensor_tensor(KT[:, :, 0], rotA.rearrange("p (c b i) -> p c b i", c=HPAIRS, b=PAIR),
                                   rotB.rearrange("p (c b i) -> p c b i", c=HPAIRS, b=PAIR), ALU.add)\
                    .then_inc(s["krot"].sem, 1)
        steps(pool, T, 2, 0, body)

    def tensor(pe):
        k.ready(pe)
        pe.wait_ge(preset, 3)

        def body(at):
            if t := at(0):
                pe.wait_ge(*s["krot"](t))
                pe.wait_ge(*s["klat"](t))
                pe.wait_ge(*s["qbd"](t))
                for b in range(PAIR):
                    for c in range(HPAIRS):
                        mm = pe.matmul(ps[:, 6 + b, c * P:(c + 1) * P], QBD[:, c, b].rearrange("p h i -> p (h i)"),
                                       KT[:, c, :, b, :], start=True, stop=True)
                    mm.then_inc(s["s_psum"].sem, 1)
            if t := at(1):
                pe.wait_ge(*s["z_ready"](t))
                if t.has(2):
                    pe.wait_ge(*s["pt_sb"](t.back(2)))
                for c in range(HPAIRS):
                    w = k.wk0[:, c * P:(c + 1) * P]
                    pe.matmul(ps[:, 0, c * P:(c + 1) * P], w, Z[t.par][:, :, 0], start=True, stop=True)
                    mm = pe.matmul(ps[:, 1, c * P:(c + 1) * P], w, Z[t.par][:, :, 1], start=True, stop=True)
                mm.then_inc(s["k_psum"].sem, 1)
                if t.has(2):
                    pe.wait_ge(*s["onorm"](t.back(2)))
                for c in range(HPAIRS):
                    mm = pe.matmul(ps[:, 2, c * P:(c + 1) * P], k.wr0[:, c * P:(c + 1) * P], Z[t.par][:, :, 0],
                                   start=True, stop=True)
                mm.then_inc(s["k2_psum"].sem, 1)
                for c in range(HPAIRS):
                    mm = pe.matmul(ps[:, 3, c * P:(c + 1) * P], k.wq0[:, c * P:(c + 1) * P], Z[t.par][:, :, 1],
                                   start=True, stop=True)
                mm.then_inc(s["q_psum"].sem, 1)
            if t := at(-1):
                pe.wait_ge(*s["onorm"](t))
                if at(0):
                    pe.wait_ge(*s["v_sb"](at(0)))
                for c in range(HPAIRS):
                    mm = pe.transpose(ps[:, 5, c * P:(c + 1) * P], on[:, c * P:(c + 1) * P], k.ident)
                mm.then_inc(s["ot_psum"].sem, 1)
            if t := at(2):
                pe.wait_ge(*f["xhat_ready"](t))
                pe.wait_ge(*s["zhat"](t))
                if t.has(1):
                    pe.wait_ge(*s["ctxT_sb"](t.back(1)))
                if t.has(2):
                    pe.wait_ge(*s["v_sb"](t.back(2)))
                pe.transpose(ps[:, 4, 0:P], k.xh[:, t.par, :], k.ident)
                pe.transpose(ps[:, 4, P:2 * P], zh[t.par], k.ident)
                pe.transpose(ps[:, 4, 2 * P:3 * P], cin[t.par], k.ident).then_inc(f["xT_psum"].sem, 1)
            if t := at(-1):
                pe.wait_ge(*s["ot_sb"](t))
                for c in range(HPAIRS):
                    mm = pe.matmul(ps[:, 5, 0:D], oT[:, c * P:(c + 1) * P], k.wo0[:, c, :],
                                   start=c == 0, stop=c == HPAIRS - 1)
                mm.then_inc(s["out_psum"].sem, 1)
            if t := at(0):
                if at(1):
                    pe.wait_ge(*s["kcos"](at(1)))
                    pe.wait_ge(*s["klat"](at(1)))
                for b in range(PAIR):
                    pe.wait_ge(*s["prob"](t, b + 1))
                    for c in range(HPAIRS):
                        mm = pe.transpose(ps[:, b, c * P:(c + 1) * P], prob[:, b, c * P:(c + 1) * P], k.ident)
                    mm.then_inc(s["pt_psum"].sem, 1)
            if t := at(1):
                if at(2):
                    pe.wait_ge(*s["z_ready"](at(2)))
                    pe.wait_ge(*s["ctxT_sb"](at(2)))
                if at(-1):
                    pe.wait_ge(*f["x_updated"](at(-1)))
                for b in range(PAIR):
                    mm = pe.matmul(ps[:, 4 + b, :], Z[t.par][:, b].rearrange("p s i -> p (s i)"), k.wv0[:, :],
                                   start=True, stop=True)
                    mm.then_inc(s["v_psum"].sem, 1)
            if t := at(0):
                pe.wait_ge(*s["pt_sb"](t))
                pe.wait_ge(*s["v_sb"](t))
                if at(1):
                    pe.wait_ge(*s["ksin"](at(1)))
                    pe.wait_ge(*s["qbd"](at(1)))
                for h in range(H0):
                    for b in range(PAIR):
                        mm = pe.matmul(ps[b * 64:b * 64 + 64, 2 + h // 4, (h % 4) * VW:(h % 4 + 1) * VW],
                                       probT[:, b, h // 2, (h % 2) * 64:(h % 2) * 64 + 64], V[t.par][:, b, h, :],
                                       start=True, stop=True)
                mm.then_inc(s["av"].sem, 1)
        steps(pe, T, 2, 1, body)

    def vector(dve):
        k.ready(dve)

        def body(at):
            if t := at(2):
                sl = t.par
                dve.wait_ge(*ctx_loaded(t))
                k.hold(dve)
                dve.bn_stats(k.st[:, sl, 1, :], cin[sl])
                dve.bn_stats(k.st[:, sl, 0, :], k.x[:, t.idx, :]).then_inc(f["stats"].sem, 1)
                dve.wait_ge(*f["stats"](t))
                k.hold(dve)
                dve.bn_aggr(k.mv[:, sl, 1, :], k.st[:, sl, 1, :])
                dve.bn_aggr(k.mv[:, sl, 0, :], k.st[:, sl, 0, :]).then_inc(f["aggr"].sem, 1)
            if t := at(-1):
                dve.wait_ge(*s["av"](t))
                heads = ps[:, 2:4, 0:4 * VW].rearrange("p k (h e) -> p k h e", e=VW)
                dve.reciprocal(rec.rearrange("p (k h) -> p k h", k=2), heads[:, :, :, HD0]).then_inc(s["recip"].sem, 1)
                dve.wait_ge(*s["recip"](t))
                dve.tensor_tensor(on.rearrange("p (k h e) -> p k h e", k=2, e=HD0), heads[:, :, :, 0:HD0],
                                  rec.rearrange("p (k h) -> p k h", k=2).unsqueeze(3).broadcast_to([P, 2, 4, HD0]),
                                  ALU.mult).then_inc(s["onorm"].sem, 1)
            if t := at(0):
                for b in range(PAIR):
                    sc = ps[:, 6 + b, :].rearrange("p (c n) -> p c n", c=HPAIRS)
                    m = mx[:, b * HPAIRS:(b + 1) * HPAIRS]
                    dve.wait_ge(*s["s_psum"](t, b + 1))
                    dve.tensor_reduce(m, sc, AX.X, ALU.max).then_inc(s["smax"].sem, 1)
                    dve.wait_ge(*s["smax"](t, b + 1))
                    dve.tensor_tensor(prob[:, b].rearrange("p (c n) -> p c n", c=HPAIRS), sc,
                                      m.unsqueeze(2).broadcast_to([P, HPAIRS, P]), ALU.subtract)\
                        .then_inc(s["sshift"].sem, 1)
            if t := at(1):
                kk = [ps[:, n, :].rearrange("p (c i) -> p c i", i=SEQ) for n in (0, 2)]
                if t.has(1):
                    dve.wait_ge(*s["krot"](t.back(1)))
                dve.wait_ge(*s["k_psum"](t))
                dve.tensor_tensor(rotA.rearrange("p (c i) -> p c i", i=SEQ), kk[0], cosT, ALU.mult)\
                    .then_inc(s["kcos"].sem, 1)
                dve.wait_ge(*s["k2_psum"](t))
                dve.tensor_tensor(rotB.rearrange("p (c i) -> p c i", i=SEQ), kk[1], sinT, ALU.mult)\
                    .then_inc(s["ksin"].sem, 1)
            if t := at(2):
                sl = t.par
                tile_xhat(k, f, dve, t, sl)
                dve.tensor_scalar(zh[sl], cin[sl], k.mv[:, sl, 1, 0:1], k.rstd[:, sl, 1:2],
                                  ALU.subtract, ALU.mult).then_inc(s["zhat"].sem, 1)
                if t.has(2):
                    dve.wait_ge(*k.z1T_stored(t.back(2)))
                dve.wait_ge(*f["xT_psum"](t))
                for dst, n, g in ((Z[sl][:, :, 1], 0, 2), (Z[sl][:, :, 0], 1, 0),
                                  (z1o[sl].rearrange("p (b i) -> p b i", b=PAIR), 1, 4)):
                    dve.tensor_scalar(dst, ps[:, 4, n * P:(n + 1) * P].rearrange("p (b i) -> p b i", b=PAIR), k.aff[:, g:g + 1], k.aff[:, g + 1:g + 2],
                                      ALU.mult, ALU.add).then_inc(s["z_ready"].sem, 1)
            if t := at(-1):
                dve.wait_ge(*s["out_psum"](t))
                dve.scalar_tensor_tensor(out=k.x[:, t.idx, :], in0=ps[:, 5, 0:D], scalar=k.gates[:, 0:1],
                                         in1=k.x[:, t.idx, :], op0=ALU.mult, op1=ALU.add)\
                    .then_inc(f["x_updated"].sem, 1)
        steps(dve, T, 2, 1, body)

    def scalar(act):
        k.ready(act)
        act.wait_ge(preset, 3)

        def body(at):
            if t := at(0):
                for b in range(PAIR):
                    act.wait_ge(*s["sshift"](t, b + 1))
                    act.activation(prob[:, b], prob[:, b], ACT.Exp, scale=HD0 ** -0.5).then_inc(s["prob"].sem, 1)
            if t := at(1):
                act.wait_ge(*s["k_psum"](t))
                act.activation(KT[:, :, 1], ps[:, 1, :].rearrange("p (c b i) -> p c b i", c=HPAIRS, b=PAIR),
                               ACT.Copy).then_inc(s["klat"].sem, 1)
                act.wait_ge(*s["q_psum"](t))
                for h in range(2):
                    rows = slice(64 * h, 64 * h + 64)
                    act.activation(QBD[rows, :, :, h, :],
                                   ps[rows, 3, :].rearrange("p (c b i) -> p c b i", c=HPAIRS, b=PAIR),
                                   ACT.Copy).then_inc(s["qbd"].sem, 1)
            if t := at(-1):
                act.wait_ge(*s["ot_psum"](t))
                act.activation(oT, ps[:, 5, :], ACT.Copy).then_inc(s["ot_sb"].sem, 1)
            if t := at(2):
                if t.has(2):
                    act.wait_ge(*k.ctxT_stored(t.back(2)))
                act.wait_ge(*s["z_ready"](t))
                act.activation(cto[t.par], ps[:, 4, 2 * P:3 * P], ACT.Copy).then_inc(s["ctxT_sb"].sem, 1)
            if t := at(0):
                for b in range(PAIR):
                    act.wait_ge(*s["pt_psum"](t, b + 1))
                    act.activation(probT[:, b].rearrange("p c n -> p (c n)"), ps[:, b, :], ACT.Copy)\
                        .then_inc(s["pt_sb"].sem, 1)
            if t := at(1):
                for b in range(PAIR):
                    act.wait_ge(*s["v_psum"](t, b + 1))
                    act.activation(V[t.par][:, b, :, 0:HD0], ps[:, 4 + b, :].rearrange("p (h e) -> p h e", e=HD0),
                                   ACT.Copy).then_inc(s["v_sb"].sem, 1)
        steps(act, T, 2, 1, body)

    return dict(sync=sync, gpsimd=gpsimd, tensor=tensor, vector=vector, scalar=scalar)


def sub(g, j):
    return Tile(g.idx * GROUP + j, j % 2)


class Route:

    OPS = 2 * GROUP + 3

    def __init__(self, k):
        self.k = k
        self.score = k.take(GROUP * EXPERTS).rearrange("p (j e) -> p j e", j=GROUP)
        self.best = k.take(GROUP * 8).rearrange("p (j e) -> p j e", j=GROUP)
        self.where = k.take(GROUP * 8).bitcast(U32).rearrange("p (j e) -> p j e", j=GROUP)
        self.wheref = k.take(GROUP * 2).rearrange("p (j e) -> p j e", j=GROUP)
        self.hit = [k.take(GROUP * EXPERTS).rearrange("p (j e) -> p j e", j=GROUP) for _ in range(2)]
        self.done = k.sig(k.T // GROUP, "routed", self.OPS)

    def run(self, dve, g):
        k, wide = self.k, [P, GROUP, EXPERTS]
        for j in range(GROUP):
            dve.max(self.best[:, j], self.score[:, j]).then_inc(self.done.sem, 1)
        dve.wait_ge(*self.done(g, GROUP))
        k.hold(dve)
        for j in range(GROUP):
            dve.max_index(self.where[:, j], self.best[:, j], self.score[:, j]).then_inc(self.done.sem, 1)
        dve.wait_ge(*self.done(g, 2 * GROUP))
        dve.tensor_copy(self.wheref, self.where[:, :, 0:2]).then_inc(self.done.sem, 1)
        dve.wait_ge(*self.done(g, 2 * GROUP + 1))
        for n in range(2):
            iota = k.konst[:, C_IOTA:C_IOTA + EXPERTS].unsqueeze(1).broadcast_to(wide)
            dve.tensor_tensor(self.hit[n], iota, self.wheref[:, :, n:n + 1].broadcast_to(wide), ALU.is_equal)\
                .then_inc(self.done.sem, 1)


def group_front(k, f, xTg, bank, twice=False):
    def dve_part(dve, g):
        for j in range(GROUP):
            tile_stats(k, f, dve, sub(g, j), j)
        for j in range(GROUP):
            if g.has(1):
                dve.wait_ge(*f["xT_psum"](g.back(1)))
            tile_xhat(k, f, dve, sub(g, j), j)

    def pool_part(pool, g):
        for j in range(GROUP):
            tile_rstd(k, f, pool, sub(g, j), j, twice)

    def pe_part(pe, g):
        pe.wait_ge(*f["xhat_ready"](sub(g, GROUP - 1)))
        if g.has(1):
            pe.wait_ge(*f["xT_sb"](g.back(1)))
        for j in range(GROUP):
            mm = pe.transpose(k.psum[:, bank, j * P:(j + 1) * P], k.xh[:, j, :], k.ident)
        mm.then_inc(f["xT_psum"].sem, 1)

    def act_part(act, g):
        act.wait_ge(*f["xT_psum"](g))
        act.activation(xTg[g.par], k.psum[:, bank, :], ACT.Copy).then_inc(f["xT_sb"].sem, 1)
    return dve_part, pool_part, pe_part, act_part


def group_signals(k, no):
    f = k.front(no)
    f.update(k.sigs(k.T // GROUP, dict(xT_psum=1, xT_sb=1)))
    return f


def experts0(k, no):
    ps, G = k.psum, k.T // GROUP
    f = group_signals(k, no)
    k.stage_memory()
    xTg = [k.take(GCOLS) for _ in range(2)]
    route = Route(k)
    gap, e, den, rden = (k.take(GROUP) for _ in range(4))
    w = [k.take(GROUP) for _ in range(2)]
    part = [k.take(GROUP * EXPERTS).rearrange("p (j e) -> p j e", j=GROUP) for _ in range(2)]
    coef = k.take(GROUP * EXPERTS).rearrange("p (j e) -> p j e", j=GROUP)
    s = k.sigs(G, dict(
        l_psum=1, l_sb=1, gap=1, e=1, w=4, part=2, coef=1, y_psum=GROUP, acc=GROUP * (EXPERTS - 1)))
    d_front, p_front, t_front, a_front = group_front(k, f, xTg, 0)
    wide = [P, GROUP, EXPERTS]

    def gpsimd(pool):
        steps(pool, G, 1, 0, lambda at: at(1) and p_front(pool, at(1)))

    def tensor(pe):
        def experts(g, j):
            bank = 2 + 2 * (j % 2)
            t = sub(g, j)
            if t.has(2):
                pe.wait_ge(*f["x_updated"](t.back(2)))
            for h in range(2):
                mm = pe.matmul(ps[:, bank + h, :], xTg[g.par][:, j * P:(j + 1) * P],
                               k.we0[:, 4 * h:4 * h + 4, :].rearrange("p e m -> p (e m)"), start=True, stop=True)
            mm.then_inc(s["y_psum"].sem, 1)

        def body(at):
            g, nxt = at(0), at(1)
            if g:
                pe.wait_ge(*f["xT_sb"](g))
                experts(g, 0)
                experts(g, 1)
            if nxt:
                t_front(pe, nxt)
            if g:
                experts(g, 2)
                experts(g, 3)
            if nxt:
                pe.wait_ge(*f["xT_sb"](nxt))
                if nxt.has(1):
                    pe.wait_ge(*s["l_sb"](nxt.back(1)))
                for j in range(GROUP):
                    mm = pe.matmul(ps[:, 1, j * EXPERTS:(j + 1) * EXPERTS], xTg[nxt.par][:, j * P:(j + 1) * P],
                                   k.wg0[:, :], start=True, stop=True)
                mm.then_inc(s["l_psum"].sem, 1)
        steps(pe, G, 1, 0, body)

    def vector(dve):
        def routing(g):
            dve.wait_ge(*s["l_psum"](g))
            dve.tensor_copy(route.score, ps[:, 1, 0:GROUP * EXPERTS].rearrange("p (j e) -> p j e", j=GROUP))\
                .then_inc(s["l_sb"].sem, 1)
            dve.wait_ge(*s["l_sb"](g))
            k.hold(dve)
            route.run(dve, g)
            dve.tensor_tensor(gap, route.best[:, :, 1], route.best[:, :, 0], ALU.subtract).then_inc(s["gap"].sem, 1)
            dve.wait_ge(*s["e"](g))
            dve.tensor_scalar(den, e, 1.0, None, ALU.add).then_inc(s["w"].sem, 1)
            dve.wait_ge(*s["w"](g, 1))
            dve.reciprocal(rden, den).then_inc(s["w"].sem, 1)
            dve.wait_ge(*s["w"](g, 2))
            dve.tensor_scalar(w[0], rden, k.gates[:, 4:5], None, ALU.mult).then_inc(s["w"].sem, 1)
            dve.wait_ge(*s["w"](g, 3))
            dve.tensor_tensor(w[1], e, w[0], ALU.mult).then_inc(s["w"].sem, 1)
            dve.wait_ge(*s["w"](g, 4))
            dve.wait_ge(*route.done(g))
            for n in range(2):
                dve.tensor_tensor(part[n], route.hit[n], w[n].unsqueeze(2).broadcast_to(wide), ALU.mult)\
                    .then_inc(s["part"].sem, 1)
            dve.wait_ge(*s["part"](g))
            dve.tensor_tensor(coef, part[0], part[1], ALU.add).then_inc(s["coef"].sem, 1)

        def body(at):
            if g := at(0):
                routing(g)
            if g := at(1):
                d_front(dve, g)
            if g := at(0):
                dve.wait_ge(*s["coef"](g))
                for j in range(GROUP):
                    t = sub(g, j)
                    bank = 2 + 2 * (j % 2)
                    dve.wait_ge(*s["y_psum"](g, j + 1))
                    for n in range(EXPERTS):
                        y = ps[:, bank + n // 4, (n % 4) * D:(n % 4 + 1) * D]
                        x = k.x[:, t.idx, :]
                        if n:
                            dve.wait_ge(*s["acc"](g, j * (EXPERTS - 1) + n))
                        dve.scalar_tensor_tensor(out=x, in0=y, scalar=coef[:, j, n:n + 1], in1=x, op0=ALU.mult,
                                                 op1=ALU.add)\
                            .then_inc(s["acc"].sem if n < EXPERTS - 1 else f["x_updated"].sem, 1)
        steps(dve, G, 1, 0, body)

    def scalar(act):
        def body(at):
            if g := at(0):
                act.wait_ge(*s["gap"](g))
                act.activation(e, gap, ACT.Exp).then_inc(s["e"].sem, 1)
            if g := at(1):
                a_front(act, g)
        steps(act, G, 1, 0, body)

    return dict(gpsimd=gpsimd, tensor=tensor, vector=vector, scalar=scalar)


def attention1(k, no):
    ps, T = k.psum, k.T
    f = k.front(no)
    f["xT_psum"] = k.sig(T, "xT_psum")
    k.stage_memory()
    two = lambda n: [k.take(n) for _ in range(2)]
    zt = two(P)
    zs = [z.rearrange("p (b u i) -> p b u i", b=PAIR, u=2) for z in two(4 * SEQ)]
    QM = k.take(512).rearrange("p (b h i) -> p b h i", b=PAIR, h=4)
    KT = k.take(P)
    NV = HD1 + 1
    VB = [v.rearrange("p (n m h e) -> p n m h e", m=2, h=2, e=NV) for v in two(PAIR * ROWS4 * 4 * NV)]
    mx = k.take(16).rearrange("p (r n) -> p r n", r=ROWS4)
    prob = k.take(1024).rearrange("p (r n) -> p r n", r=ROWS4)
    probT = k.take(1024).rearrange("p (b n) -> p b n", b=PAIR)
    rec = k.take(PAIR * 16).rearrange("p (b n) -> p b n", b=PAIR)
    on, oT = k.take(D), k.take(D)
    loads = [k.transfers(T, f"z_loaded{u}") for u in range(2)]
    s = k.sigs(T, dict(
        zt=1, q_psum=1, kv_psum=1, qm=1, kt=1, vb=2, s_psum=2, smax=2, sshift=2, prob=1, pt_psum=2, pt_sb=2,
        av=1, recip=1, onorm=4, ot_psum=1, ot_sb=1, out_psum=1))
    preset = k.sem("A1_preset")

    def sync(sp):
        k.z1T_stored.wait_all(sp, T)

        def body(at):
            if t := at(2):
                if t.has(2):
                    sp.wait_ge(*s["kv_psum"](t.back(2)))
                for u in range(2):
                    sp.dma_start(zs[t.par][:, :, u, :], k.z1T_dram[t.idx].rearrange("p (b i) -> p b i", b=PAIR))\
                        .then_inc(loads[u].at(t), 16)
        steps(sp, T, 2, 0, body)

    def gpsimd(pool):
        for n in range(2):
            pool.memset(VB[n], 0.0).then_inc(preset, 1)
        pool.wait_ge(preset, 2)
        for n in range(2):
            for m in range(2):
                pool.memset(VB[n][64 * m:64 * m + 64, :, m, :, HD1:NV], 1.0).then_inc(preset, 1)
        pool.wait_ge(preset, 6)

        def body(at):
            if t := at(2):
                tile_rstd(k, f, pool, t, t.par, True)
        steps(pool, T, 2, 0, body)

    def tensor(pe):
        def body(at):
            if t := at(0):
                pe.wait_ge(*s["qm"](t))
                pe.wait_ge(*s["kt"](t))
                if t.has(1):
                    pe.wait_ge(*s["onorm"](t.back(1)))
                for r in range(ROWS4):
                    rows = slice(32 * r, 32 * r + 32)
                    for b in range(PAIR):
                        for m in range(2):
                            n = 2 * b + m
                            mm = pe.matmul(ps[:, r, n * SEQ:(n + 1) * SEQ],
                                           QM[rows, b, 2 * m:2 * m + 2, :].rearrange("p h i -> p (h i)"),
                                           KT[rows, b * SEQ:(b + 1) * SEQ], start=True, stop=True)
                    if r % 2:
                        mm.then_inc(s["s_psum"].sem, 1)
            if t := at(1):
                pe.wait_ge(*s["zt"](t))
                pe.matmul(ps[:, 4, 0:P], k.w1a[:, 0, :], zt[t.par], start=True, stop=True).then_inc(s["q_psum"].sem, 1)
                for u in range(2):
                    pe.wait_ge(*loads[u](t))
                if t.has(1):
                    pe.wait_ge(*s["kt"](t.back(1)))
                    pe.wait_ge(*s["vb"](t.back(1)))
                pe.matmul(ps[:, 5, 0:P], k.w1a[:, 1, :], zs[t.par][:, :, 0, :], start=True, stop=True)
                for b in range(PAIR):
                    mm = pe.matmul(ps[:, 5, (b + 1) * D:(b + 2) * D], zs[t.par][:, b].rearrange("p u i -> p (u i)"),
                                   k.w1a[:, 2, :], start=True, stop=True)
                mm.then_inc(s["kv_psum"].sem, 1)
            if t := at(-1):
                pe.wait_ge(*s["onorm"](t))
                pe.transpose(ps[:, 6, 0:D], on, k.ident).then_inc(s["ot_psum"].sem, 1)
            if t := at(2):
                pe.wait_ge(*f["xhat_ready"](t))
                if at(1):
                    pe.wait_ge(*s["qm"](at(1)))
                if t.has(1):
                    pe.wait_ge(*s["zt"](t.back(1)))
                pe.transpose(ps[:, 4, 0:P], k.xh[:, t.par, :], k.ident).then_inc(f["xT_psum"].sem, 1)
            if t := at(-1):
                pe.wait_ge(*s["ot_sb"](t))
                pe.matmul(ps[:, 7, 0:D], oT, k.w1a[:, 3, :], start=True, stop=True).then_inc(s["out_psum"].sem, 1)
            if t := at(0):
                pe.wait_ge(*s["prob"](t))
                if t.has(1):
                    pe.wait_ge(*f["x_updated"](t.back(1)))
                for b in range(PAIR):
                    for r in range(ROWS4):
                        mm = pe.transpose(ps[:, 6 + b, r * P:(r + 1) * P], prob[:, r, b * P:(b + 1) * P], k.ident)
                    mm.then_inc(s["pt_psum"].sem, 1)
                pe.wait_ge(*s["vb"](t))
                for b in range(PAIR):
                    pe.wait_ge(*s["pt_sb"](t, b + 1))
                    for r in range(ROWS4):
                        mm = pe.matmul(ps[:, b, r * 4 * NV:(r + 1) * 4 * NV], probT[:, b, r * P:(r + 1) * P],
                                       VB[t.par][:, b * ROWS4 + r].rearrange("p m h e -> p (m h e)"),
                                       start=True, stop=True)
                mm.then_inc(s["av"].sem, 1)
        steps(pe, T, 2, 1, body)

    def vector(dve):
        def body(at):
            if t := at(2):
                tile_stats(k, f, dve, t, t.par)
            if t := at(-1):
                dve.wait_ge(*s["av"](t))
                heads = ps[:, 0:2, 0:ROWS4 * 4 * NV].rearrange("p b (n e) -> p b n e", e=NV)
                dve.reciprocal(rec, heads[:, :, :, HD1]).then_inc(s["recip"].sem, 1)
                dve.wait_ge(*s["recip"](t))
                for h in range(2):
                    rows = slice(64 * h, 64 * h + 64)
                    for b in range(PAIR):
                        src = ps[rows, b, 0:ROWS4 * 4 * NV].rearrange("p (n h e) -> p n h e", h=2, e=NV)[:, :, h, 0:HD1]
                        r = rec[rows, b].rearrange("p (n h) -> p n h", h=2)[:, :, h:h + 1].broadcast_to([64, 8, HD1])
                        dst = on[64 * b:64 * b + 64, :].rearrange("p (n h e) -> p n h e", h=2, e=HD1)[:, :, h, :]
                        dve.tensor_tensor(dst, src, r, ALU.mult).then_inc(s["onorm"].sem, 1)
            if t := at(0):
                for c in range(2):
                    sc = ps[:, 2 * c:2 * c + 2, 0:4 * SEQ].rearrange("p r (n i) -> p r n i", i=SEQ)
                    m = mx[:, 2 * c:2 * c + 2]
                    dve.wait_ge(*s["s_psum"](t, c + 1))
                    dve.tensor_reduce(m, sc, AX.X, ALU.max).then_inc(s["smax"].sem, 1)
                    dve.wait_ge(*s["smax"](t, c + 1))
                    dve.tensor_tensor(prob[:, 2 * c:2 * c + 2].rearrange("p r (n i) -> p r n i", i=SEQ), sc,
                                      m.unsqueeze(3).broadcast_to([P, 2, 4, SEQ]), ALU.subtract)\
                        .then_inc(s["sshift"].sem, 1)
            if t := at(1):
                dve.wait_ge(*s["q_psum"](t))
                q = ps[:, 4, 0:P].rearrange("p (b i) -> p b i", b=PAIR)
                mask = k.konst[:, C_MASK4:C_MASK4 + 4]
                dve.tensor_tensor(QM, q.unsqueeze(2).broadcast_to([P, PAIR, 4, SEQ]),
                                  mask.unsqueeze(1).unsqueeze(3).broadcast_to([P, PAIR, 4, SEQ]), ALU.mult)\
                    .then_inc(s["qm"].sem, 1)
            if t := at(2):
                tile_xhat(k, f, dve, t, t.par)
                dve.wait_ge(*f["xT_psum"](t))
                dve.tensor_scalar(zt[t.par], ps[:, 4, 0:P], k.aff[:, 6:7], k.aff[:, 7:8], ALU.mult, ALU.add)\
                    .then_inc(s["zt"].sem, 1)
            if t := at(-1):
                dve.wait_ge(*s["out_psum"](t))
                dve.scalar_tensor_tensor(out=k.x[:, t.idx, :], in0=ps[:, 7, 0:D], scalar=k.gates[:, 1:2],
                                         in1=k.x[:, t.idx, :], op0=ALU.mult, op1=ALU.add)\
                    .then_inc(f["x_updated"].sem, 1)
        steps(dve, T, 2, 1, body)

    def scalar(act):
        act.wait_ge(preset, 6)

        def body(at):
            if t := at(0):
                act.wait_ge(*s["sshift"](t))
                act.activation(prob, prob, ACT.Exp, scale=HD1 ** -0.5).then_inc(s["prob"].sem, 1)
            if t := at(1):
                act.wait_ge(*s["kv_psum"](t))
                act.activation(KT, ps[:, 5, 0:P], ACT.Copy).then_inc(s["kt"].sem, 1)
                for m in range(2):
                    rows = slice(64 * m, 64 * m + 64)
                    act.activation(VB[t.par][rows, :, m, :, 0:HD1],
                                   ps[rows, 5, D:3 * D].rearrange("p (n m h e) -> p n m h e", m=2, h=2, e=HD1)[:, :, m],
                                   ACT.Copy).then_inc(s["vb"].sem, 1)
            if t := at(-1):
                act.wait_ge(*s["ot_psum"](t))
                act.activation(oT, ps[:, 6, 0:D], ACT.Copy).then_inc(s["ot_sb"].sem, 1)
            if t := at(0):
                for b in range(PAIR):
                    act.wait_ge(*s["pt_psum"](t, b + 1))
                    act.activation(probT[:, b], ps[:, 6 + b, :], ACT.Copy).then_inc(s["pt_sb"].sem, 1)
        steps(act, T, 2, 1, body)

    return dict(sync=sync, gpsimd=gpsimd, tensor=tensor, vector=vector, scalar=scalar)


def spiking1(k, no):
    ps, G = k.psum, k.T // GROUP
    f = group_signals(k, no)
    k.stage_memory()
    NC = FF1 // P
    xTg = [k.take(GCOLS) for _ in range(2)]
    relu = k.take(NC * GCOLS).rearrange("p (c n) -> p c n", c=NC)
    sq = [v.rearrange("p (c n) -> p c n", c=NC) for v in (k.take(NC * GCOLS) for _ in range(2))]
    mem, decayed, count = [k.take(GCOLS) for _ in range(2)], k.take(GCOLS), k.take(GCOLS)
    drive = k.take(GCOLS)
    s = k.sigs(G, dict(
        h_psum=NC, relu=NC, sq=NC, y_psum=1, drive=1, decayed=SPIKE_STEPS - 1, mem=SPIKE_STEPS - 1,
        count=SPIKE_STEPS))
    d_front, p_front, t_front, a_front = group_front(k, f, xTg, 0)

    def gpsimd(pool):
        steps(pool, G, 2, 0, lambda at: at(2) and p_front(pool, at(2)))

    def tensor(pe):
        def body(at):
            if g := at(2):
                t_front(pe, g)
            if g := at(1):
                pe.wait_ge(*f["xT_sb"](g))
                for c in range(NC):
                    if g.has(1):
                        pe.wait_ge(*s["sq"](g.back(1), c + 1))
                    pe.matmul(ps[:, 1 + c, :], k.wfc1[:, c * P:(c + 1) * P], xTg[g.par], start=True, stop=True)\
                        .then_inc(s["h_psum"].sem, 1)
            if g := at(0):
                pe.wait_ge(*s["sq"](g))
                if g.has(1):
                    pe.wait_ge(*s["drive"](g.back(1)))
                for j in range(GROUP):
                    for c in range(NC):
                        mm = pe.matmul(ps[:, 5, j * P:(j + 1) * P], sq[g.par][:, c, j * P:(j + 1) * P],
                                       k.wpr1[:, c, :], start=c == 0, stop=c == NC - 1)
                mm.then_inc(s["y_psum"].sem, 1)
        steps(pe, G, 2, 0, body)

    def vector(dve):
        def squares(g):
            for c in range(NC):
                dve.wait_ge(*s["relu"](g, c + 1))
                dve.tensor_tensor(sq[g.par][:, c, :], relu[:, c, :], ps[:, 1 + c, :], ALU.mult)\
                    .then_inc(s["sq"].sem, 1)

        def spikes(g):
            dve.wait_ge(*s["drive"](g))
            if g.has(1):
                dve.wait_ge(*f["x_updated"](sub(g.back(1), GROUP - 1)))
            dve.tensor_scalar(count, drive, 1.0, None, ALU.is_gt).then_inc(s["count"].sem, 1)
            m = drive
            for n in range(1, SPIKE_STEPS):
                if n > 1:
                    dve.wait_ge(*s["mem"](g, n - 1))
                dve.scalar_tensor_tensor(out=decayed, in0=m, scalar=BETA, in1=drive, op0=ALU.mult, op1=ALU.add)\
                    .then_inc(s["decayed"].sem, 1)
                dve.wait_ge(*s["decayed"](g, n))
                nxt = mem[n % 2]
                dve.scalar_tensor_tensor(out=nxt, in0=m, scalar=1.0, in1=decayed, op0=ALU.is_gt, op1=ALU.subtract,
                                         reverse1=True).then_inc(s["mem"].sem, 1)
                dve.wait_ge(*s["mem"](g, n))
                dve.wait_ge(*s["count"](g, n))
                dve.scalar_tensor_tensor(out=count, in0=nxt, scalar=1.0, in1=count, op0=ALU.is_gt, op1=ALU.add)\
                    .then_inc(s["count"].sem, 1)
                m = nxt
            dve.wait_ge(*s["count"](g))
            for j in range(GROUP):
                x = k.x[:, sub(g, j).idx, :]
                dve.scalar_tensor_tensor(out=x, in0=count[:, j * P:(j + 1) * P], scalar=k.spike_gate[:, :], in1=x,
                                         op0=ALU.mult, op1=ALU.add).then_inc(f["x_updated"].sem, 1)

        def body(at):
            if g := at(2):
                d_front(dve, g)
            if g := at(1):
                squares(g)
            if g := at(0):
                spikes(g)
        steps(dve, G, 2, 0, body)

    def scalar(act):
        def body(at):
            if g := at(2):
                a_front(act, g)
            if g := at(1):
                for c in range(NC):
                    act.wait_ge(*s["h_psum"](g, c + 1))
                    act.activation(relu[:, c, :], ps[:, 1 + c, :], ACT.Relu).then_inc(s["relu"].sem, 1)
            if g := at(0):
                act.wait_ge(*s["y_psum"](g))
                if g.has(1):
                    act.wait_ge(*s["count"](g.back(1)))
                act.activation(drive, ps[:, 5, :], ACT.Copy).then_inc(s["drive"].sem, 1)
        steps(act, G, 2, 0, body)

    return dict(gpsimd=gpsimd, tensor=tensor, vector=vector, scalar=scalar)


def context_attention(layer):
    biased, masked = layer == 2, layer == 3
    SCALE = D ** -0.5

    def stage(k, no):
        ps, T = k.psum, k.T
        f = k.front(no)
        f["xT_psum"] = k.sig(T, "xT_psum")
        k.stage_memory()
        two = lambda n: [k.take(n) for _ in range(2)]
        xT, qT, cT, cr, pT, uT = two(P), two(P), two(P), two(D), two(P), two(P)
        prob, xb, sm = two(P), two(D), two(SEQ)
        mx, nb, rs, rec = two(1), two(1), two(1), two(1)
        A, B = k.A[layer - 2], k.B[layer - 2]
        s = k.sigs(T, dict(
            xT_sb=1, q_psum=1, q_sb=1, s_psum=1, smax=1, nb=1, prob=2, pt_psum=1, pt_sb=1, u_psum=1,
            u_sb=1, recip=1, out_psum=1))
        s["biased" if biased else "masked"] = k.sig(T, "biased" if biased else "masked")
        cT_loaded, cr_loaded = k.transfers(T, "cT_loaded"), k.transfers(T, "cr_loaded")
        preset = k.sem(f"A{layer}_preset")
        ctx_dram = k.a["ctx_1024"].rearrange("(t b) s d -> t (b s) d", b=PAIR)

        def sync(sp):
            def body(at):
                if t := at(2):
                    if t.has(2):
                        sp.wait_ge(*s["s_psum"](t.back(2)))
                    sp.dma_start(cT[t.par], k.ctxT_dram[t.idx]).then_inc(cT_loaded.at(t), 16)
                if t := at(1):
                    if t.has(2):
                        sp.wait_ge(*s["u_psum"](t.back(2)))
                    sp.dma_start(cr[t.par], ctx_dram[t.idx]).then_inc(cr_loaded.at(t), 16)
            steps(sp, T, 2, 0, body)

        def gpsimd(pool):
            for n in range(2):
                pool.memset(prob[n], 0.0).then_inc(preset, 1)

            def body(at):
                if t := at(3):
                    tile_rstd(k, f, pool, t, t.par, False)
                if biased and (t := at(0)):
                    if t.has(2):
                        pool.wait_ge(*f["x_updated"](t.back(2)))
                        k.hold(pool)
                    pool.tensor_tensor(xb[t.par], k.x[:, t.idx, :], k.bout[:, :], ALU.add)\
                        .then_inc(s["biased"].sem, 1)
            steps(pool, T, 3, 0, body)

        def tensor(pe):
            def body(at):
                if t := at(-2):
                    pe.wait_ge(*s["u_sb"](t))
                    if t.has(2):
                        pe.wait_ge(*f["x_updated"](t.back(2)))
                    pe.matmul(ps[:, 6 + t.par, 0:D], uT[t.par], B[:, :], start=True, stop=True)\
                        .then_inc(s["out_psum"].sem, 1)
                if t := at(-1):
                    pe.wait_ge(*s["pt_sb"](t))
                    pe.wait_ge(*cr_loaded(t))
                    if t.has(1):
                        pe.wait_ge(*s["u_sb"](t.back(1)))
                    pe.matmul(ps[:, 5, 0:P], cr[t.par], pT[t.par], start=True, stop=True)\
                        .then_inc(s["u_psum"].sem, 1)
                if t := at(0):
                    pe.wait_ge(*s["prob"](t))
                    if t.has(1):
                        pe.wait_ge(*s["pt_sb"](t.back(1)))
                    pe.transpose(ps[:, 4, 0:P], prob[t.par], k.ident).then_inc(s["pt_psum"].sem, 1)
                if t := at(1):
                    pe.wait_ge(*s["q_sb"](t))
                    pe.wait_ge(*cT_loaded(t))
                    if t.has(2):
                        pe.wait_ge(*s["prob"](t.back(2)))
                    for b in range(PAIR):
                        cols = slice(b * SEQ, (b + 1) * SEQ)
                        mm = pe.matmul(ps[64 * b:64 * b + 64, 2 + t.par, 0:SEQ], qT[t.par][:, cols],
                                       cT[t.par][:, cols], start=True, stop=True)
                    mm.then_inc(s["s_psum"].sem, 1)
                if t := at(2):
                    pe.wait_ge(*s["xT_sb"](t))
                    if t.has(1):
                        pe.wait_ge(*s["q_sb"](t.back(1)))
                    pe.matmul(ps[:, 1, 0:P], A[:, :], xT[t.par], start=True, stop=True).then_inc(s["q_psum"].sem, 1)
                if t := at(3):
                    pe.wait_ge(*f["xhat_ready"](t))
                    if t.has(1):
                        pe.wait_ge(*s["xT_sb"](t.back(1)))
                    pe.transpose(ps[:, 0, 0:P], k.xh[:, t.par, :], k.ident).then_inc(f["xT_psum"].sem, 1)
            steps(pe, T, 3, 2, body)

        def vector(dve):
            def body(at):
                if t := at(3):
                    tile_stats(k, f, dve, t, t.par)
                if t := at(-2):
                    dve.wait_ge(*s["out_psum"](t))
                    if biased:
                        dve.wait_ge(*s["biased"](t))
                    dve.scalar_tensor_tensor(out=k.x[:, t.idx, :], in0=ps[:, 6 + t.par, 0:D], scalar=rec[t.par],
                                             in1=xb[t.par] if biased else k.x[:, t.idx, :], op0=ALU.mult,
                                             op1=ALU.add).then_inc(f["x_updated"].sem, 1)
                if t := at(0):
                    dve.wait_ge(*s["prob"](t))
                    if t.has(2):
                        dve.wait_ge(*f["x_updated"](t.back(2)))
                        k.hold(dve)
                    dve.reciprocal(rec[t.par], rs[t.par]).then_inc(s["recip"].sem, 1)
                if t := at(-1):
                    dve.wait_ge(*s["u_psum"](t))
                    dve.tensor_copy(uT[t.par], ps[:, 5, 0:P]).then_inc(s["u_sb"].sem, 1)
                if t := at(1):
                    dve.wait_ge(*s["s_psum"](t))
                    src = ps[:, 2 + t.par, 0:SEQ]
                    if masked:
                        dve.tensor_tensor(sm[t.par], src, k.konst[:, C_CAUSAL:C_CAUSAL + SEQ], ALU.mult)\
                            .then_inc(s["masked"].sem, 1)
                        dve.wait_ge(*s["masked"](t))
                        src = sm[t.par]
                    dve.tensor_reduce(mx[t.par], src, AX.X, ALU.max).then_inc(s["smax"].sem, 1)
                    dve.wait_ge(*s["smax"](t))
                    dve.tensor_scalar(nb[t.par], mx[t.par], -SCALE, None, ALU.mult).then_inc(s["nb"].sem, 1)
                if t := at(3):
                    tile_xhat(k, f, dve, t, t.par)
            steps(dve, T, 3, 2, body)

        def scalar(act):
            act.wait_ge(preset, 2)

            def body(at):
                if t := at(0):
                    act.wait_ge(*s["pt_psum"](t))
                    act.activation(pT[t.par], ps[:, 4, 0:P], ACT.Copy).then_inc(s["pt_sb"].sem, 1)
                if t := at(1):
                    act.wait_ge(*s["nb"](t))
                    for b in range(PAIR):
                        rows = slice(64 * b, 64 * b + 64)
                        src = sm[t.par][rows] if masked else ps[rows, 2 + t.par, 0:SEQ]
                        act.activation(prob[t.par][rows, b * SEQ:(b + 1) * SEQ], src, ACT.Exp, scale=SCALE,
                                       bias=nb[t.par][rows], accum_out=rs[t.par][rows]).then_inc(s["prob"].sem, 1)
                if t := at(2):
                    act.wait_ge(*s["q_psum"](t))
                    if biased:
                        act.activation(qT[t.par], ps[:, 1, 0:P], ACT.Identity, bias=k.bqk[:, :])\
                            .then_inc(s["q_sb"].sem, 1)
                    else:
                        act.activation(qT[t.par], ps[:, 1, 0:P], ACT.Copy).then_inc(s["q_sb"].sem, 1)
                if t := at(3):
                    act.wait_ge(*f["xT_psum"](t))
                    act.activation(xT[t.par], ps[:, 0, 0:P], ACT.Copy).then_inc(s["xT_sb"].sem, 1)
            steps(act, T, 3, 0, body)

        return dict(sync=sync, gpsimd=gpsimd, tensor=tensor, vector=vector, scalar=scalar)
    return stage


def experts2(k, no):
    ps, G = k.psum, k.T // GROUP
    f = group_signals(k, no)
    k.stage_memory()
    xTg = [k.take(GCOLS) for _ in range(2)]
    hT = [v.rearrange("p (c n) -> p c n", c=CHUNKS2) for v in (k.take(CHUNKS2 * GCOLS) for _ in range(2))]
    small = lambda: k.take(GROUP * EXPERTS).rearrange("p (j e) -> p j e", j=GROUP)
    score, shifted, expd, hits = small(), small(), small(), small()
    route = Route(k)
    smax, ssum, srec = k.take(GROUP), k.take(GROUP), k.take(GROUP)
    coef, coefT = small(), k.take(GCOLS)
    s = k.sigs(G, dict(
        l_psum=1, score=1, smax=1, shifted=1, expd=1, ssum=1, srec=1, routing_prob=1, hits=1, coef=1, ct_psum=1, ct_sb=1,
        h_psum=CHUNKS2, h_sb=CHUNKS2, y_psum=GROUP, acc=GROUP * EXPERTS))
    d_front, p_front, t_front, a_front = group_front(k, f, xTg, 0)
    wide = [P, GROUP, EXPERTS]

    def gpsimd(pool):
        steps(pool, G, 1, 0, lambda at: at(1) and p_front(pool, at(1)))

    def tensor(pe):
        def hidden(g, c):
            if c >= 2:
                pe.wait_ge(*s["h_sb"](g, c - 1))
            elif g.has(1):
                pe.wait_ge(*s["h_sb"](g.back(1), CHUNKS2 - 1 + c))
            w = k.w1s[:, c, 0:P] if c < EXPERTS else k.w1tail[:, c - EXPERTS, :]
            pe.matmul(ps[:, 2 + c % 2, :], w, xTg[g.par], start=True, stop=True).then_inc(s["h_psum"].sem, 1)

        def outputs(g, j):
            bank, cols = 4 + 2 * (j % 2), slice(j * P, (j + 1) * P)
            t = sub(g, j)
            if t.has(2):
                pe.wait_ge(*f["x_updated"](t.back(2)))
            for e in range(EXPERTS):
                dst = ps[:, bank + e % 2, (e // 2) * D:(e // 2 + 1) * D]
                rows = slice(64 * (e % 2), 64 * (e % 2) + 64)
                pe.matmul(dst, hT[g.par][:, e, cols], k.w2a[:, e, :], start=True, stop=False)
                mm = pe.matmul(dst, hT[g.par][rows, EXPERTS + e // 2, cols], k.w2b[rows, e // 2, :],
                               start=False, stop=True)
            mm.then_inc(s["y_psum"].sem, 1)

        def body(at):
            g, nxt = at(0), at(1)
            if g:
                pe.wait_ge(*s["h_sb"](g))
                outputs(g, 0)
            if nxt:
                t_front(pe, nxt)
            if g:
                outputs(g, 1)
            if nxt:
                pe.wait_ge(*f["xT_sb"](nxt))
                if g:
                    pe.wait_ge(*s["b2_sb"](g))
                for j in range(GROUP):
                    mm = pe.matmul(ps[:, 1, j * EXPERTS:(j + 1) * EXPERTS], xTg[nxt.par][:, j * P:(j + 1) * P],
                                   k.wr2[:, :], start=True, stop=True)
                mm.then_inc(s["l_psum"].sem, 1)
                for c in range(0, 4):
                    hidden(nxt, c)
            if g:
                outputs(g, 2)
            if nxt:
                for c in range(4, 8):
                    hidden(nxt, c)
            if g:
                outputs(g, 3)
            if nxt:
                for c in range(8, 12):
                    hidden(nxt, c)
                pe.wait_ge(*s["coef"](nxt))
                for j in range(GROUP):
                    mm = pe.transpose(ps[0:EXPERTS, 1, j * P:(j + 1) * P], coef[:, j], k.ident)
                mm.then_inc(s["ct_psum"].sem, 1)
                pe.wait_ge(*s["ct_sb"](nxt))
                for j in range(GROUP):
                    mm = pe.matmul(ps[:, 1, j * D:(j + 1) * D], coefT[0:EXPERTS, j * P:(j + 1) * P], k.b2r[:, :],
                                   start=True, stop=True)
                mm.then_inc(s["b2_psum"].sem, 1)
        steps(pe, G, 1, 0, body)

    s["b2_psum"], s["b2_sb"] = k.sig(G, "b2_psum"), k.sig(G, "b2_sb")
    b2sum = [k.take(GCOLS) for _ in range(2)]

    def vector(dve):
        def routing(g):
            dve.wait_ge(*s["l_psum"](g))
            dve.tensor_tensor(score, ps[:, 1, 0:GROUP * EXPERTS].rearrange("p (j e) -> p j e", j=GROUP),
                              k.br2[:, :].unsqueeze(1).broadcast_to(wide), ALU.add).then_inc(s["score"].sem, 1)
            dve.wait_ge(*s["score"](g))
            dve.tensor_reduce(smax, score, AX.X, ALU.max).then_inc(s["smax"].sem, 1)
            dve.wait_ge(*s["smax"](g))
            dve.tensor_tensor(shifted, score, smax.unsqueeze(2).broadcast_to(wide), ALU.subtract)\
                .then_inc(s["shifted"].sem, 1)
            dve.wait_ge(*s["expd"](g))
            dve.tensor_reduce(ssum, expd, AX.X, ALU.add).then_inc(s["ssum"].sem, 1)
            dve.wait_ge(*s["ssum"](g))
            dve.reciprocal(srec, ssum).then_inc(s["srec"].sem, 1)
            dve.wait_ge(*s["srec"](g))
            dve.tensor_tensor(route.score, expd, srec.unsqueeze(2).broadcast_to(wide), ALU.mult)\
                .then_inc(s["routing_prob"].sem, 1)
            dve.wait_ge(*s["routing_prob"](g))
            k.hold(dve)
            route.run(dve, g)
            dve.wait_ge(*route.done(g))
            dve.tensor_tensor(hits, route.hit[0], route.hit[1], ALU.add).then_inc(s["hits"].sem, 1)
            dve.wait_ge(*s["hits"](g))
            dve.scalar_tensor_tensor(out=coef, in0=hits, scalar=k.gates[:, 6:7], in1=route.score,
                                     op0=ALU.mult, op1=ALU.mult).then_inc(s["coef"].sem, 1)

        def combine(g, j):
            t = sub(g, j)
            bank = 4 + 2 * (j % 2)
            x = k.x[:, t.idx, :]
            dve.tensor_tensor(x, x, b2sum[g.par][:, j * D:(j + 1) * D], ALU.add).then_inc(s["acc"].sem, 1)
            dve.wait_ge(*s["y_psum"](g, j + 1))
            for e in range(EXPERTS):
                dve.wait_ge(*s["acc"](g, j * EXPERTS + e + 1))
                dve.scalar_tensor_tensor(out=x, in0=ps[:, bank + e % 2, (e // 2) * D:(e // 2 + 1) * D],
                                         scalar=coefs[:, j, e:e + 1], in1=x, op0=ALU.mult, op1=ALU.add)\
                    .then_inc(s["acc"].sem if e < EXPERTS - 1 else f["x_updated"].sem, 1)

        def body(at):
            g, nxt = at(0), at(1)
            if nxt:
                d_front(dve, nxt)
            if g:
                dve.wait_ge(*s["b2_sb"](g))
                if g.has(1):
                    dve.wait_ge(*f["x_updated"](sub(g.back(1), GROUP - 1)))
                    k.hold(dve)
                dve.tensor_copy(coefs, coef).then_inc(s["coefs"].sem, 1)
                dve.wait_ge(*s["coefs"](g))
                combine(g, 0)
                combine(g, 1)
            if nxt:
                routing(nxt)
            if g:
                combine(g, 2)
                combine(g, 3)
        steps(dve, G, 1, 0, body)

    coefs = small()
    s["coefs"] = k.sig(G, "coefs")

    def scalar(act):
        def body(at):
            if g := at(1):
                a_front(act, g)
                for c in range(4):
                    hidden_out(act, g, c)
                act.wait_ge(*s["shifted"](g))
                act.activation(expd, shifted, ACT.Exp).then_inc(s["expd"].sem, 1)
                for c in range(4, CHUNKS2):
                    hidden_out(act, g, c)
                act.wait_ge(*s["ct_psum"](g))
                act.activation(coefT[0:EXPERTS, :], ps[0:EXPERTS, 1, :], ACT.Copy).then_inc(s["ct_sb"].sem, 1)
                act.wait_ge(*s["b2_psum"](g))
                act.activation(b2sum[g.par], ps[:, 1, :], ACT.Copy).then_inc(s["b2_sb"].sem, 1)
        steps(act, G, 1, 0, body)

    def hidden_out(act, g, c):
        act.wait_ge(*s["h_psum"](g, c + 1))
        act.activation(hT[g.par][:, c, :], ps[:, 2 + c % 2, :], ACT.Gelu, bias=k.b1c[:, c:c + 1])\
            .then_inc(s["h_sb"].sem, 1)

    return dict(gpsimd=gpsimd, tensor=tensor, vector=vector, scalar=scalar)


def quantised3(k, no):
    ps, T, G = k.psum, k.T, k.T // GROUP
    f = k.front(no)
    k.stage_memory()
    W = CHUNKS3 * GCOLS
    half = lambda n: k.take(n // 2).bitcast(I16)
    upq = half(G * W).rearrange("p (g n) -> p g n", g=G)
    xdT = k.take(T * P).rearrange("p (g n) -> p g n", g=G)
    xhs = k.take(T * P).rearrange("p (g n) -> p g n", g=G)
    mark = k.taken
    gq2 = k.arena[:, mark - 2 * T * P:mark - 2 * T * P + G * W // 2].bitcast(I16).rearrange("p (g n) -> p g n", g=G)
    k.taken = mark - T * P
    gq, sig, sigq = half(W), k.take(W), k.take(W // 2).bitcast(U16)
    gs = [k.take(W) for _ in range(2)]
    k.taken = max(mark - 2 * T * P + G * W // 2, mark - T * P)
    gin, prod = [k.take(W) for _ in range(2)], k.take(W)
    k.taken = mark - 2 * T * P + G * W // 2
    oprod, oq, of = k.take(W), half(W), k.take(W)
    sb = k.sb
    xq, xd = sb("xq", [P, GCOLS], I16), sb("xd", [P, GCOLS])
    xmax, ugmax = sb("xmax", [P, T]), sb("ugmax", [P, 2, G, CHUNKS3])
    gsmax, omax = sb("gsmax", [P, G]), sb("omax", [P, G])
    local, wide = sb("local_max", [P, 2]), sb("wide_max", [2, P])
    top = sb("top_max", [2, 1])
    scale = {n: sb(f"scale_{n}", [P, w]) for n, w in dict(x=1, ug=2, gs=1, o=1).items()}
    inv = {n: sb(f"inv_{n}", [P, w]) for n, w in dict(x=1, ug=2, gs=1, o=1).items()}
    sprod, down = sb("scale_product", [P, 1]), sb("scale_down", [P, 1])
    gs_dram = k.nc.dram_tensor("gated_scratch", [G, P, W], F32, kind="Internal").ap()
    gs_stored, gs_loaded = k.transfers(G, "gated_stored"), k.transfers(G, "gated_loaded")
    s = k.sigs(G, dict(
        xmax=1, xq=1, xd=1, t_psum=1, xdT=1, p_psum=2 * CHUNKS3, pmax=2 * CHUNKS3, c_psum=2 * CHUNKS3, upq=CHUNKS3,
        gq=CHUNKS3, sig=1, sigq=1, gs=1, gsmax=1, gq2=1, prod=1, omax=1, oprod=1, oq=1, of=1, y_psum=1))
    SCALES = ("x", "ug", "gs", "o")
    found, spread = k.sem("Q3_scale_found"), k.sem("Q3_scale_spread")
    final = k.sem("Q3_final_scales")

    def scale_vector(dve, name, columns, factor):
        n, w = SCALES.index(name), scale[name].shape[1]
        dve.tensor_reduce(local[:, 0:w], columns, AX.X, ALU.max).then_inc(found, 1)
        dve.wait_ge(spread, 2 * n + 1)
        dve.tensor_reduce(top[0:w, :], ps[0:w, 7, 0:P], AX.X, ALU.max).then_inc(found, 1)
        dve.wait_ge(found, 5 * n + 2)
        dve.tensor_scalar(wide[0:w, :], k.konst[0:w, C_ONES:C_ONES + P], top[0:w, :], None, ALU.mult)\
            .then_inc(found, 1)
        dve.wait_ge(spread, 2 * n + 2)
        dve.tensor_scalar(scale[name][:, :], ps[:, 7, P:P + w], factor / QMAX_A, 1e-12, ALU.mult, ALU.max)\
            .then_inc(found, 1)
        dve.wait_ge(found, 5 * n + 4)
        dve.reciprocal(inv[name][:, :], scale[name][:, :]).then_inc(found, 1)
        dve.wait_ge(found, 5 * n + 5)

    def scale_tensor(pe, name):
        n, w = SCALES.index(name), scale[name].shape[1]
        pe.wait_ge(found, 5 * n + 1)
        pe.transpose(ps[0:w, 7, 0:P], local[:, 0:w], k.ident).then_inc(spread, 1)
        pe.wait_ge(found, 5 * n + 3)
        pe.matmul(ps[:, 7, P:P + w], wide[0:w, :], k.konst[0:w, C_IDENT:C_IDENT + w], start=True, stop=True)\
            .then_inc(spread, 1)

    def scale_known(eng, name):
        eng.wait_ge(found, 5 * SCALES.index(name) + 5)

    def sync(sp):
        def store(at):
            if g := at(0):
                sp.wait_ge(*s["gs"](g))
                sp.dma_start(gs_dram[g.idx], gs[g.par]).then_inc(gs_stored.at(g), 16)
        steps(sp, G, 0, 0, store)
        gs_stored.wait_all(sp, G)
        sp.wait_ge(*s["gsmax"].all(G))

        def load(at):
            if g := at(0):
                if g.has(2):
                    sp.wait_ge(*s["gq2"](g.back(2)))
                sp.dma_start(gin[g.par], gs_dram[g.idx]).then_inc(gs_loaded.at(g), 16)
        steps(sp, G, 0, 2, load)

    def gpsimd(pool):
        steps(pool, T, 1, 0, lambda at: at(1) and tile_rstd(k, f, pool, at(1), at(1).par, False))

    def project(pe, g, psum_signal, freed):
        for n, w in enumerate((k.wup3, k.wgt3)):
            for c in range(CHUNKS3):
                if g.has(1):
                    freed(g.back(1), n, c)
                pe.matmul(ps[:, 1 + CHUNKS3 * n + c, :], w[:, c, :], xdT[:, g.idx, :], start=True, stop=True)\
                    .then_inc(psum_signal.sem, 1)

    def tensor(pe):
        scale_tensor(pe, "x")

        def first(at):
            if g := at(1):
                pe.wait_ge(*s["xd"](g))
                if g.has(1):
                    pe.wait_ge(*s["xdT"](g.back(1)))
                for j in range(GROUP):
                    mm = pe.transpose(ps[:, 0, j * P:(j + 1) * P], xd[:, j * P:(j + 1) * P], k.ident)
                mm.then_inc(s["t_psum"].sem, 1)
            if g := at(0):
                pe.wait_ge(*s["xdT"](g))
                project(pe, g, s["p_psum"], lambda b, n, c: pe.wait_ge(*s["pmax"](b, CHUNKS3 * n + c + 1)))
        steps(pe, G, 1, 0, first)
        scale_tensor(pe, "ug")

        def second(at):
            if g := at(0):
                project(pe, g, s["c_psum"],
                        lambda b, n, c: pe.wait_ge(*s["gq" if n else "upq"](b, c + 1)))
        pe.wait_ge(*s["pmax"].all(G))
        steps(pe, G, 0, 0, second)
        scale_tensor(pe, "gs")
        scale_tensor(pe, "o")

        def last(at):
            if g := at(0):
                pe.wait_ge(*s["of"](g))
                if g.has(2):
                    pe.wait_ge(*f["x_updated"](sub(g.back(2), GROUP - 1)))
                for j in range(GROUP):
                    for c in range(CHUNKS3):
                        mm = pe.matmul(ps[:, g.par, j * P:(j + 1) * P],
                                       of[:, c * GCOLS + j * P:c * GCOLS + (j + 1) * P], k.wdn3[:, c, :],
                                       start=c == 0, stop=c == CHUNKS3 - 1)
                mm.then_inc(s["y_psum"].sem, 1)
        steps(pe, G, 0, 0, last)

    def vector(dve):
        xflat = xhs.rearrange("p g (j n) -> p (g j) n", j=GROUP)

        def normalise(at):
            if t := at(1):
                tile_stats(k, f, dve, t, t.par)
            if t := at(0):
                tile_xhat(k, f, dve, t, t.par, out=xflat[:, t.idx, :])
                dve.wait_ge(*f["xhat_ready"](t))
                k.hold(dve)
                dve.tensor_reduce(xmax[:, bass.ds(t.idx, 1)], xflat[:, t.idx, :], AX.X, ALU.max,
                                  apply_absolute_value=True).then_inc(s["xmax"].sem, 1)
        steps(dve, T, 1, 0, normalise)
        dve.wait_ge(*s["xmax"].all(T))
        scale_vector(dve, "x", xmax[:, :], 1.0)

        def first(at):
            if g := at(1):
                if g.has(1):
                    dve.wait_ge(*s["xd"](g.back(1)))
                dve.tensor_scalar(xq[:, :], xhs[:, g.idx, :], inv["x"][:, :], None, ALU.mult).then_inc(s["xq"].sem, 1)
                dve.wait_ge(*s["xq"](g))
                if g.has(1):
                    dve.wait_ge(*s["t_psum"](g.back(1)))
                dve.tensor_scalar(xd[:, :], xq[:, :], scale["x"][:, :], None, ALU.mult).then_inc(s["xd"].sem, 1)
            if g := at(0):
                for n in range(2 * CHUNKS3):
                    dve.wait_ge(*s["p_psum"](g, n + 1))
                    k.hold(dve)
                    dve.tensor_reduce(ugmax[:, n // CHUNKS3, g.idx, n % CHUNKS3:n % CHUNKS3 + 1], ps[:, 1 + n, :],
                                      AX.X, ALU.max, apply_absolute_value=True).then_inc(s["pmax"].sem, 1)
        steps(dve, G, 1, 0, first)
        dve.wait_ge(*s["pmax"].all(G))
        scale_vector(dve, "ug", ugmax[:, :, :, :].rearrange("p w g c -> p w (g c)"), 1.0)

        def second(at):
            if g := at(0):
                dve.wait_ge(*s["sig"](g))
                dve.tensor_scalar(sigq, sig, QSIG, QSIG - 1.0, ALU.mult, ALU.min).then_inc(s["sigq"].sem, 1)
                dve.wait_ge(*s["sigq"](g))
                if g.has(2):
                    dve.wait_ge(*gs_stored(g.back(2)))
                dve.scalar_tensor_tensor(out=gs[g.par], in0=gq, scalar=scale["ug"][:, 1:2], in1=sigq, op0=ALU.mult,
                                         op1=ALU.mult).then_inc(s["gs"].sem, 1)
                dve.wait_ge(*s["gs"](g))
                k.hold(dve)
                dve.tensor_reduce(gsmax[:, bass.ds(g.idx, 1)], gs[g.par], AX.X, ALU.max, apply_absolute_value=True)\
                    .then_inc(s["gsmax"].sem, 1)
        steps(dve, G, 0, 0, second)
        dve.wait_ge(*s["gsmax"].all(G))
        scale_vector(dve, "gs", gsmax[:, :], 1.0)
        dve.tensor_scalar(sprod[:, :], scale["gs"][:, :], scale["ug"][:, 0:1], 1.0 / QSIG, ALU.mult, ALU.mult)\
            .then_inc(final, 1)
        dve.wait_ge(final, 1)

        def product(g, out, signal):
            dve.scalar_tensor_tensor(out=out, in0=gq2[:, g.idx, :], scalar=sprod[:, :], in1=upq[:, g.idx, :],
                                     op0=ALU.mult, op1=ALU.mult).then_inc(signal.sem, 1)

        def third(at):
            if g := at(0):
                dve.wait_ge(*s["gq2"](g))
                if g.has(1):
                    dve.wait_ge(*s["omax"](g.back(1)))
                product(g, prod, s["prod"])
                dve.wait_ge(*s["prod"](g))
                k.hold(dve)
                dve.tensor_reduce(omax[:, bass.ds(g.idx, 1)], prod, AX.X, ALU.max, apply_absolute_value=True)\
                    .then_inc(s["omax"].sem, 1)
        steps(dve, G, 0, 0, third)
        dve.wait_ge(*s["omax"].all(G))
        scale_vector(dve, "o", omax[:, :], 1.0)
        dve.tensor_scalar(down[:, :], scale["o"][:, :], k.gates[:, 7:8], None, ALU.mult).then_inc(final, 1)
        dve.wait_ge(final, 2)

        def last(at):
            if g := at(1):
                if g.has(1):
                    dve.wait_ge(*s["oq"](g.back(1)))
                product(g, oprod, s["oprod"])
            if g := at(0):
                dve.wait_ge(*s["y_psum"](g))
                for j in range(GROUP):
                    x = k.x[:, sub(g, j).idx, :]
                    dve.scalar_tensor_tensor(out=x, in0=ps[:, g.par, j * P:(j + 1) * P], scalar=down[:, :], in1=x,
                                             op0=ALU.mult, op1=ALU.add).then_inc(f["x_updated"].sem, 1)
        steps(dve, G, 1, 0, last)

    def scalar(act):
        scale_known(act, "x")

        def first(at):
            if g := at(1):
                act.wait_ge(*s["t_psum"](g))
                k.hold(act)
                act.activation(xdT[:, g.idx, :], ps[:, 0, :], ACT.Copy).then_inc(s["xdT"].sem, 1)
        steps(act, G, 1, 0, first)
        scale_known(act, "ug")

        def second(at):
            if g := at(0):
                for c in range(CHUNKS3):
                    act.wait_ge(*s["c_psum"](g, c + 1))
                    k.hold(act)
                    act.activation(upq[:, g.idx, c * GCOLS:(c + 1) * GCOLS], ps[:, 1 + c, :], ACT.Copy,
                                   scale=inv["ug"][:, 0:1]).then_inc(s["upq"].sem, 1)
                if g.has(1):
                    act.wait_ge(*s["gs"](g.back(1)))
                for c in range(CHUNKS3):
                    act.wait_ge(*s["c_psum"](g, CHUNKS3 + c + 1))
                    act.activation(gq[:, c * GCOLS:(c + 1) * GCOLS], ps[:, 1 + CHUNKS3 + c, :], ACT.Copy,
                                   scale=inv["ug"][:, 1:2]).then_inc(s["gq"].sem, 1)
                act.wait_ge(*s["gq"](g))
                act.activation(sig, gq, ACT.Sigmoid, scale=scale["ug"][:, 1:2]).then_inc(s["sig"].sem, 1)
        steps(act, G, 0, 0, second)
        scale_known(act, "gs")
        act.wait_ge(gs_stored.sems[0], G // 2 * 16)
        act.wait_ge(gs_stored.sems[1], G // 2 * 16)

        def third(at):
            if g := at(0):
                act.wait_ge(*gs_loaded(g))
                k.hold(act)
                act.activation(gq2[:, g.idx, :], gin[g.par], ACT.Copy, scale=inv["gs"][:, :])\
                    .then_inc(s["gq2"].sem, 1)
        steps(act, G, 0, 0, third)
        scale_known(act, "o")

        def last(at):
            if g := at(0):
                act.wait_ge(*s["oprod"](g))
                if g.has(1):
                    act.wait_ge(*s["of"](g.back(1)))
                act.activation(oq, oprod, ACT.Copy, scale=inv["o"][:, :]).then_inc(s["oq"].sem, 1)
                act.wait_ge(*s["oq"](g))
                if g.has(1):
                    act.wait_ge(*s["y_psum"](g.back(1)))
                act.activation(of, oq, ACT.Copy).then_inc(s["of"].sem, 1)
        steps(act, G, 0, 0, last)

    return dict(sync=sync, gpsimd=gpsimd, tensor=tensor, vector=vector, scalar=scalar)


STAGES = [attention0, experts0, attention1, spiking1, context_attention(2), experts2, context_attention(3), quantised3]


def flamingo(nc, args, out, last=8):
    with ExitStack() as ctx:
        k = Kit(nc, ctx, args, out)
        parts = [prepare(k)]
        for no, stage in enumerate(STAGES[:last]):
            parts.append(stage(k, no))
        stored = k.sem("x_stored")
        ov = out.rearrange("(t b) s d -> (b s) t d", b=PAIR)
        QUARTERS = 4
        block = ctx.enter_context(nc.Block())

        def run(engine, name):
            for no, part in enumerate(parts):
                if name in part:
                    if no > 1:
                        stage_start(engine, k, no - 1)
                    part[name](engine)

        @block.sync
        def _(sp):
            run(sp, "sync")
            updated = k.front(last - 1)["x_updated"]
            for j in range(QUARTERS):
                n = k.T // QUARTERS
                sp.wait_ge(*updated.all((j + 1) * n))
                sp.dma_start(ov[:, j * n:(j + 1) * n, :], k.x[:, j * n:(j + 1) * n, :]).then_inc(stored, 16)
            sp.wait_ge(stored, 16 * QUARTERS)
            k.ctxT_stored.wait_all(sp, k.T)
            k.z1T_stored.wait_all(sp, k.T)

        @block.gpsimd
        def _(pool):
            run(pool, "gpsimd")

        @block.tensor
        def _(pe):
            run(pe, "tensor")

        @block.vector
        def _(dve):
            run(dve, "vector")

        @block.scalar
        def _(act):
            run(act, "scalar")


def shape_constants():
    import numpy as np
    c = np.zeros((P, C_END), np.float32)
    c[:, C_IDENT:C_IDENT + P] = np.eye(P)
    freq = (np.float32(1.0) / np.float32(10000.0) ** (np.arange(0, HD0, 2, dtype=np.float32) / np.float32(HD0)))
    theta = np.arange(SEQ, dtype=np.float32)[:, None] * freq.astype(np.float32)[None, :]
    angles = np.concatenate([theta, theta] * 2, axis=1).T
    c[:, C_COS:C_COS + SEQ], c[:, C_SIN:C_SIN + SEQ] = np.cos(angles), np.sin(angles)
    c[:, C_IOTA:C_IOTA + EXPERTS] = np.arange(EXPERTS)
    rows = np.arange(P)
    c[:, C_MASK4:C_MASK4 + 4] = (rows[:, None] // HD1) % 4 == np.arange(4)
    c[:, C_CAUSAL:C_CAUSAL + SEQ] = np.arange(SEQ) <= rows[:, None] % SEQ
    c[:, C_MHALF:C_MHALF + 4] = -0.5
    c[:, C_ONES:C_ONES + P] = 1.0
    return c


def kernel(**inputs):
    import numpy as np
    import concourse.bacc as bacc
    from concourse.bass_utils import run_bass_kernel_spmd

    nc = bacc.Bacc("TRN2", target_bir_lowering=False, num_devices=1)
    arrays, args = {}, {}
    for name, a in list(inputs.items()) + [("shape_constants", shape_constants())]:
        a = np.ascontiguousarray(a)
        arrays[f"in_{name}"] = a
        args[name] = nc.dram_tensor(f"in_{name}", a.shape, mybir.dt.from_np(a.dtype), kind="ExternalInput").ap()
    out = nc.dram_tensor("out_x", inputs["x"].shape, F32, kind="ExternalOutput").ap()
    flamingo(nc, args, out)
    r = run_bass_kernel_spmd(nc, [arrays], core_ids=[0])
    return r.results[0]["out_x"]
```

```python
from contextlib import ExitStack

import concourse.bass as bass
from concourse import mybir

ALU = mybir.AluOpType
ACT = mybir.ActivationFunctionType
AX = mybir.AxisListType
F32 = mybir.dt.float32
I16 = mybir.dt.int16
U16 = mybir.dt.uint16
U32 = mybir.dt.uint32

P = 128
SEQ = 64
D = 128
PAIR = P // SEQ
EPS = 1e-5
EXPERTS = 8
GROUP = 4
GCOLS = GROUP * P
DUO = 2
H0, HD0 = 8, 64
INNER = H0 * HD0
HPAIRS = H0 // 2
VW = HD0 + 1
H1, HD1 = 16, 8
FF1 = 512
SPIKE_STEPS, BETA = 5, 0.9
HID2 = 192
CHUNKS2 = EXPERTS * HID2 // P
FF3 = 384
CHUNKS3 = FF3 // P
BLOCK = 32
QMAX_A, QMAX_W, QSIG = 32767.0, 7.0, 65536.0

C_IDENT, C_COS, C_SIN, C_IOTA, C_MASK8, C_CAUSAL, C_MHALF, C_ONES = 0, 128, 192, 256, 264, 272, 336, 340
C_END = C_ONES + 128


class Tile:

    def __init__(self, idx, par):
        self.idx, self.par = idx, par

    def has(self, k):
        return not isinstance(self.idx, int) or self.idx >= k

    def back(self, k):
        return Tile(self.idx - k, (self.par - k) % 2)


class Signal:

    def __init__(self, sem, per=1, base=0):
        self.sem, self.per, self.base = sem, per, base

    def __call__(self, t, k=None):
        return self.sem, self.base + self.per * t.idx + (self.per if k is None else k)

    def all(self, n):
        return self.sem, self.base + self.per * n


class Transfers:

    def __init__(self, even, odd, base):
        self.sems, self.base = (even, odd), base

    def at(self, t):
        return self.sems[t.par]

    def __call__(self, t):
        return self.sems[t.par], self.base + (t.idx - t.par) * 8 + 16

    def wait_all(self, eng, n):
        for sem in self.sems:
            eng.wait_ge(sem, self.base + n // 2 * 16)


def steps(eng, n, lead, lag, body):
    def fixed(s):
        body(lambda k: Tile(s + k, (s + k) % 2) if 0 <= s + k < n else None)

    first = (lag + 3) // 2 * 2
    end = first + (n - lead - first) // 2 * 2
    if end - first < 4:
        for s in range(-lead, n + lag):
            fixed(s)
        return
    for s in range(-lead, first):
        fixed(s)
    with eng.Fori(first // 2, end // 2) as i:
        for u in range(2):
            body(lambda k, u=u: Tile(i * 2 + (u + k), (u + k) % 2))
    for s in range(end, n + lag):
        fixed(s)


class Kit:

    def __init__(self, nc, ctx, args, out):
        self.nc, self.ctx, self.a, self.out = nc, ctx, args, out
        self.T = args["x"].shape[0] // PAIR
        self.psum = ctx.enter_context(nc.psum_tensor("banks", [P, 8, 512], F32))
        self.x = self.sb("x_tiles", [P, self.T, D])
        self.konst = self.sb("konst", [P, C_END])
        self.arena = self.sb("arena", [P, 30500])
        self.taken, self.fronts, self.sems, self.counted = 0, {}, {}, {}
        self.ident = self.konst[:, C_IDENT:C_IDENT + P]
        self.st = self.sb("bn_parts", [P, GROUP, 2, 6])
        self.mv = self.sb("mean_var", [P, GROUP, 2, 2])
        self.ve = self.sb("var_eps", [P, GROUP, 2])
        self.rstd = self.sb("rstd", [P, GROUP, 2])
        self.xh = self.sb("xhat", [P, GROUP, D])
        self.gate_pass = self.sem("form_has_no_register_wait")
        names = ("stats", "aggr", "vareps", "rstd_ready", "xhat_ready", "x_updated")
        self.shared = {n: self.sem(n) for n in names}
        self.ctxT_dram = nc.dram_tensor("ctxT_scratch", [self.T, P, P], F32, kind="Internal").ap()
        self.z1T_dram = nc.dram_tensor("z1T_scratch", [self.T, P, P], F32, kind="Internal").ap()
        self.ctxT_stored, self.z1T_stored = (
            self.transfers(self.T, n) for n in ("ctxT_stored", "z1T_stored"))

    def sb(self, name, shape, dt=F32):
        return self.ctx.enter_context(self.nc.sbuf_tensor(name, shape, dt))

    def sem(self, name):
        return self.ctx.enter_context(self.nc.semaphore(name))

    def shared_sem(self, name):
        if name not in self.sems:
            self.sems[name], self.counted[name] = self.sem(name), 0
        return self.sems[name], self.counted[name]

    def sig(self, n, name, per=1):
        sem, base = self.shared_sem(name)
        self.counted[name] = base + per * n
        return Signal(sem, per, base)

    def sigs(self, n, names):
        return {name: self.sig(n, name, per) for name, per in names.items()}

    def transfers(self, n, name):
        (even, base), (odd, _) = (self.shared_sem(name + side) for side in ("_even", "_odd"))
        for side in ("_even", "_odd"):
            self.counted[name + side] = base + n // 2 * 16
        return Transfers(even, odd, base)

    def stage_memory(self):
        self.taken = 0

    def take(self, cols):
        a = self.arena[:, self.taken:self.taken + cols]
        self.taken += cols
        assert self.taken <= 30500, self.taken
        return a

    def front(self, no):
        if no not in self.fronts:
            self.fronts[no] = {n: Signal(s, 1, no * self.T) for n, s in self.shared.items()}
        return self.fronts[no]

    def hold(self, eng):
        eng.sem_inc(self.gate_pass, 1)


def tile_stats(k, f, dve, t, slot):
    dve.bn_stats(k.st[:, slot, 0, :], k.x[:, t.idx, :]).then_inc(f["stats"].sem, 1)
    dve.wait_ge(*f["stats"](t))
    k.hold(dve)
    dve.bn_aggr(k.mv[:, slot, 0, :], k.st[:, slot, 0, :]).then_inc(f["aggr"].sem, 1)


def tile_rstd(k, f, pool, t, slot, twice):
    pool.wait_ge(*f["aggr"](t))
    k.hold(pool)
    pool.tensor_scalar(k.ve[:, slot, 0:1], k.mv[:, slot, 0, 1:2], 1.0 + EPS if twice else 1.0,
                       EPS * EPS if twice else EPS, ALU.mult, ALU.add).then_inc(f["vareps"].sem, 1)
    pool.wait_ge(*f["vareps"](t))
    pool.tensor_tensor(k.rstd[:, slot, 0:1], k.ve[:, slot, 0:1], k.konst[:, C_MHALF:C_MHALF + 1],
                       ALU.pow).then_inc(f["rstd_ready"].sem, 1)


def tile_xhat(k, f, dve, t, slot, out=None):
    dve.wait_ge(*f["rstd_ready"](t))
    dve.tensor_scalar(k.xh[:, slot, :] if out is None else out, k.x[:, t.idx, :], k.mv[:, slot, 0, 0:1],
                      k.rstd[:, slot, 0:1], ALU.subtract, ALU.mult).then_inc(f["xhat_ready"].sem, 1)


def stage_start(eng, k, no):
    if no:
        eng.wait_ge(*k.front(no)["x_updated"].all(0))
    if no == 1:
        k.ctxT_stored.wait_all(eng, k.T)
        k.z1T_stored.wait_all(eng, k.T)


def prepare(k):
    nc, a, ps = k.nc, k.a, k.psum
    sb = k.sb
    raw = k.take
    k.gates, k.spike_gate = sb("gates", [P, 8]), sb("spike_gate", [P, 1])
    gates_raw = raw(8)
    k.wq0, k.wk0, k.wv0, k.wr0 = (sb(n, [P, INNER]) for n in ("wq0", "wk0", "wv0", "wk0_rotated"))
    k.wo0 = sb("wo0", [P, HPAIRS, D])
    k.aff = sb("affine_columns", [P, 8])
    k.we0, k.wg0 = sb("we0", [P, EXPERTS, D]), sb("wg0", [P, EXPERTS])
    gw_raw = raw(D)
    k.w1a = sb("w1a", [P, 4, D])
    k.wfc1, k.wpr1 = sb("wfc1", [P, FF1]), sb("wpr1", [P, 4, D])
    fc_raw, pr_raw = raw(4 * D), raw(FF1)
    w2_raw, w3_raw = raw(4 * D), raw(3 * D)
    woT = raw(D)
    bcol = raw(2)
    bo_row = raw(D)
    bv_wide, b1_raw = raw(D), raw(P)
    k.A = [sb("A2", [P, D]), sb("A3", [P, D])]
    k.B = [sb("B2", [P, D]), sb("B3", [P, D])]
    k.bqk, k.bout = sb("bqk", [P, 1]), sb("bout", [P, D])
    k.wr2, k.br2 = sb("wr2", [P, EXPERTS]), sb("br2", [P, EXPERTS])
    k.w1s, k.w1tail = sb("w1s", [P, EXPERTS, P]), sb("w1tail", [P, EXPERTS // 2, P])
    k.w2a, k.w2b = sb("w2a", [P, EXPERTS, D]), sb("w2b", [P, EXPERTS // 2, D])
    k.b1c, k.b2r = sb("b1c", [P, CHUNKS2]), sb("b2r", [EXPERTS, D])
    q_raw = raw(3 * FF3).rearrange("p (w b i) -> p w b i", w=3, i=BLOCK)
    q_max, q_inv = raw(36).rearrange("p (w b) -> p w b", w=3), raw(36).rearrange("p (w b) -> p w b", w=3)
    q_int = raw(3 * FF3 // 2).bitcast(I16).rearrange("p (w b i) -> p w b i", w=3, i=BLOCK)
    q_clip = raw(3 * FF3 // 2).bitcast(I16).rearrange("p (w b i) -> p w b i", w=3, i=BLOCK)
    q_deq = raw(3 * FF3).rearrange("p (w b i) -> p w b i", w=3, i=BLOCK)
    k.wup3, k.wgt3, k.wdn3 = (sb(n, [P, CHUNKS3, D]) for n in ("wup3", "wgt3", "wdn3"))

    loaded, x_loaded = k.sem("weights_loaded"), k.sem("x_loaded")
    gates_ready, built, dequant = k.sem("gates_ready"), k.sem("weights_built"), k.sem("dequantised")
    turned, turned_sb, folded, folded_sb = (k.sem(n) for n in ("turned", "turned_sb", "folded", "folded_sb"))
    wkv = a["L0_xattn_Wkv"]
    loads = [
        (k.konst[:, :], a["shape_constants"]),
        (gates_raw[:, 0:4], a["g_xattn"].partition_broadcast(P)),
        (gates_raw[:, 4:8], a["g_ffn"].partition_broadcast(P)),
        (k.wq0[:, :], a["L0_xattn_Wq"]), (k.wk0[:, :], wkv[:, 0:INNER]), (k.wv0[:, :], wkv[:, INNER:2 * INNER]),
        (k.wo0[:, :, :], a["L0_xattn_Wo"].rearrange("(c p) d -> p c d", p=P)),
        (k.we0[:, :, :], a["L0_ffn_We"].rearrange("e d m -> d e m")),
        (gw_raw[0:EXPERTS, :], a["L0_ffn_gate_w"]),
        (fc_raw.rearrange("p (c d) -> p c d", c=4), a["L1_ffn_W_fc"].rearrange("(c p) d -> p c d", p=P)),
        (pr_raw, a["L1_ffn_W_proj"]),
        (bo_row[0:1, :], a["L2_xattn_bo"].rearrange("(a n) -> a n", a=1)),
        (k.wr2[:, :], a["L2_ffn_Wr"]), (k.br2[:, :], a["L2_ffn_br"].partition_broadcast(P)),
        (k.w1s[:, :, :], a["L2_ffn_W1"][:, :, 0:P].rearrange("e d h -> d e h")),
        (k.w2a[:, :, :], a["L2_ffn_W2"][:, 0:P, :].rearrange("e h d -> h e d")),
        (q_raw[:, 0].rearrange("p (c b) i -> p c (b i)", c=CHUNKS3), a["L3_ffn_w_up"].rearrange("(c p) d -> p c d", p=P)),
        (q_raw[:, 1].rearrange("p (c b) i -> p c (b i)", c=CHUNKS3), a["L3_ffn_w_gate"].rearrange("(c p) d -> p c d", p=P)),
        (q_raw[:, 2].rearrange("p b i -> p (b i)"), a["L3_ffn_w_down"]),
    ]
    for i, n in enumerate(("L0_xattn_gamma_x", "L0_xattn_beta_x", "L0_xattn_gamma_l", "L0_xattn_beta_l",
                           "L1_xattn_ln1_g", "L1_xattn_ln1_b", "L1_xattn_ln2_g", "L1_xattn_ln2_b")):
        loads.append((k.aff[:, i:i + 1], a[n].rearrange("(p a) -> p a", a=1)))
    for i, n in enumerate(("Wq", "Wk", "Wv", "Wfc")):
        loads.append((k.w1a[:, i, :], a["L1_xattn_" + n]))
    for i, n in enumerate(("Wk", "Wv", "Wq", "Wo")):
        loads.append((w2_raw[:, i * D:(i + 1) * D], a["L2_xattn_" + n]))
    for i, n in enumerate(("WQ", "WK", "WV")):
        loads.append((w3_raw[:, i * D:(i + 1) * D], a["L3_xattn_" + n]))
    for i, n in enumerate(("bv", "bq")):
        loads.append((bcol[:, i:i + 1], a["L2_xattn_" + n].rearrange("(p a) -> p a", a=1)))
    for h in range(2):
        w2 = a["L2_ffn_W2"].rearrange("(k h) n d -> h n k d", h=2)
        b1 = a["L2_ffn_b1"].rearrange("(k h) n -> h k n", h=2)[:, :, P:HID2]
        w1 = a["L2_ffn_W1"].rearrange("(k h) d n -> h d k n", h=2)
        loads.append((k.w1tail[:, :, h * 64:h * 64 + 64], w1[h][:, :, P:HID2]))
        loads.append((k.w2b[h * 64:h * 64 + 64, :, :], w2[h, P:HID2]))
        loads.append((b1_raw[EXPERTS:CHUNKS2, h * 64:h * 64 + 64], b1[h]))
    loads.append((b1_raw[0:EXPERTS, :], a["L2_ffn_b1"][:, 0:P]))
    loads.append((k.b2r[:, :], a["L2_ffn_b2"]))
    xv = a["x"].rearrange("(t b) s d -> (b s) t d", b=PAIR)
    XPARTS = 4

    def sync(sp):
        for j in range(XPARTS):
            n = k.T // XPARTS
            sp.dma_start(k.x[:, j * n:(j + 1) * n, :], xv[:, j * n:(j + 1) * n, :]).then_inc(x_loaded, 16)
        for dst, src in loads[0::2]:
            sp.dma_start(dst, src).then_inc(loaded, 16)

    def all_loaded(eng):
        eng.wait_ge(loaded, 16 * len(loads))

    def scalar(act):
        for dst, src in loads[1::2]:
            act.dma_start(dst, src).then_inc(loaded, 16)
        all_loaded(act)
        act.activation(k.gates[:, :], gates_raw, ACT.Tanh).then_inc(gates_ready, 1)
        act.wait_ge(gates_ready, 1)
        act.activation(k.spike_gate[:, :], k.gates[:, 5:6], ACT.Copy, scale=1.0 / SPIKE_STEPS).then_inc(gates_ready, 1)
        act.wait_ge(turned, 1)
        for dst, src in ((k.wfc1[:, :], ps[:, 0, :]), (k.wpr1[:, :, :].rearrange("p c d -> p (c d)"), ps[:, 1, :]),
                         (woT, ps[:, 2, 0:D]), (k.wg0[:, :], ps[:, 2, 2 * D:2 * D + EXPERTS]),
                         (k.b1c[:, :], ps[:, 2, 3 * D:3 * D + CHUNKS2])):
            act.activation(dst, src, ACT.Copy).then_inc(turned_sb, 1)
        act.wait_ge(gates_ready, 1)
        act.activation(k.B[1][:, :], ps[:, 2, D:2 * D], ACT.Copy, scale=k.gates[:, 3:4]).then_inc(turned_sb, 1)
        act.wait_ge(turned, 2)
        for i, w in enumerate((k.wup3, k.wgt3, k.wdn3)):
            act.activation(w[:, :, :].rearrange("p c d -> p (c d)"), ps[:, 3 + i, 0:3 * D], ACT.Copy).then_inc(turned_sb, 1)
        act.wait_ge(folded, 1)
        act.activation(k.A[0][:, :], ps[:, 6, 0:D], ACT.Copy).then_inc(folded_sb, 1)
        act.activation(k.A[1][:, :], ps[:, 6, D:2 * D], ACT.Copy).then_inc(folded_sb, 1)
        act.activation(k.bqk[:, :], ps[:, 6, 2 * D:2 * D + 1], ACT.Copy).then_inc(folded_sb, 1)
        act.wait_ge(folded, 2)
        act.activation(k.B[0][:, :], ps[:, 7, 0:D], ACT.Copy, scale=k.gates[:, 2:3]).then_inc(folded_sb, 1)
        act.activation(k.bout[:, :], ps[:, 7, D:2 * D], ACT.Copy, scale=k.gates[:, 2:3]).then_inc(folded_sb, 1)

    def vector(dve):
        all_loaded(dve)
        src = k.wk0[:, :].rearrange("p (h s i) -> p h s i", s=2, i=HD0 // 2)
        dst = k.wr0[:, :].rearrange("p (h s i) -> p h s i", s=2, i=HD0 // 2)
        dve.tensor_scalar(dst[:, :, 0], src[:, :, 1], -1.0, None, ALU.mult).then_inc(built, 1)
        dve.tensor_copy(dst[:, :, 1], src[:, :, 0]).then_inc(built, 1)
        dve.tensor_scalar(bv_wide, k.konst[:, C_ONES:C_ONES + P], bcol[:, 0:1], None, ALU.mult).then_inc(built, 1)
        blocks = [P, 3, 12, BLOCK]
        dve.tensor_reduce(q_max, q_raw, AX.X, ALU.max, apply_absolute_value=True).then_inc(dequant, 1)
        dve.wait_ge(dequant, 1)
        dve.tensor_scalar(q_max, q_max, 1.0 / QMAX_W, 1e-12, ALU.mult, ALU.max).then_inc(dequant, 1)
        dve.wait_ge(dequant, 2)
        dve.reciprocal(q_inv, q_max).then_inc(dequant, 1)
        dve.wait_ge(dequant, 3)
        for w in range(3):
            dve.tensor_tensor(q_int[:, w], q_raw[:, w], q_inv[:, w].unsqueeze(2).broadcast_to(blocks[:1] + blocks[2:]),
                              ALU.mult).then_inc(dequant, 1)
        dve.wait_ge(dequant, 6)
        dve.tensor_scalar(q_clip, q_int, -QMAX_W - 1.0, QMAX_W, ALU.max, ALU.min).then_inc(dequant, 1)
        dve.wait_ge(dequant, 7)
        for w in range(3):
            dve.tensor_tensor(q_deq[:, w], q_clip[:, w], q_max[:, w].unsqueeze(2).broadcast_to(blocks[:1] + blocks[2:]),
                              ALU.mult).then_inc(dequant, 1)

    def tensor(pe):
        all_loaded(pe)
        for c in range(4):
            pe.transpose(ps[:, 0, c * P:(c + 1) * P], fc_raw[:, c * D:(c + 1) * D], k.ident)
            pe.transpose(ps[:, 1, c * P:(c + 1) * P], pr_raw[:, c * P:(c + 1) * P], k.ident)
        pe.transpose(ps[:, 2, 0:D], w2_raw[:, 3 * D:4 * D], k.ident)
        pe.transpose(ps[:, 2, D:2 * D], w3_raw[:, 2 * D:3 * D], k.ident)
        pe.transpose(ps[:, 2, 2 * D:2 * D + EXPERTS], gw_raw[0:EXPERTS, :],
                     k.konst[0:EXPERTS, C_IDENT:C_IDENT + EXPERTS])
        pe.transpose(ps[:, 2, 3 * D:3 * D + CHUNKS2], b1_raw[0:CHUNKS2, :],
                     k.konst[0:CHUNKS2, C_IDENT:C_IDENT + CHUNKS2]).then_inc(turned, 1)
        pe.matmul(ps[:, 6, 0:D], w2_raw[:, 2 * D:3 * D], w2_raw[:, 0:D], start=True, stop=True)
        pe.matmul(ps[:, 6, D:2 * D], w3_raw[:, 0:D], w3_raw[:, D:2 * D], start=True, stop=True)
        pe.matmul(ps[:, 6, 2 * D:2 * D + 1], w2_raw[:, 0:D], bcol[:, 1:2], start=True, stop=True).then_inc(folded, 1)
        pe.wait_ge(dequant, 10)
        for w in range(3):
            for c in range(3):
                flat = q_deq[:, w].rearrange("p b i -> p (b i)")[:, c * P:(c + 1) * P]
                mm = pe.transpose(ps[:, 3 + w, c * P:(c + 1) * P], flat, k.ident)
        mm.then_inc(turned, 1)
        pe.wait_ge(turned_sb, 6)
        pe.wait_ge(built, 3)
        pe.matmul(ps[:, 7, 0:D], w2_raw[:, D:2 * D], woT, start=True, stop=True)
        pe.matmul(ps[:, 7, D:2 * D], bv_wide, woT, start=True, stop=False)
        pe.matmul(ps[:, 7, D:2 * D], k.konst[0:1, C_ONES:C_ONES + P], bo_row[0:1, :], start=False, stop=True)\
            .then_inc(folded, 1)

    def ready(eng):
        eng.wait_ge(x_loaded, 16 * XPARTS)
        all_loaded(eng)
        eng.wait_ge(gates_ready, 2)
        eng.wait_ge(built, 3)
        eng.wait_ge(turned_sb, 9)
        eng.wait_ge(folded_sb, 5)

    k.ready = ready
    return dict(sync=sync, scalar=scalar, vector=vector, tensor=tensor)


def attention0(k, no):
    nc, ps, T = k.nc, k.psum, k.T
    f = k.front(no)
    f["xT_psum"] = k.sig(T, "xT_psum")
    k.stage_memory()
    two = lambda n: [k.take(n) for _ in range(2)]
    cin, zh = two(D), two(D)
    Z = [z.rearrange("p (b s i) -> p b s i", b=PAIR, s=2) for z in two(2 * P)]
    z1o, cto = two(P), two(P)
    KT = k.take(HPAIRS * 4 * SEQ).rearrange("p (c s b i) -> p c s b i", c=HPAIRS, s=2, b=PAIR)
    rotA, rotB = k.take(512), k.take(512)
    QBD = k.take(HPAIRS * PAIR * P).rearrange("p (c b h i) -> p c b h i", c=HPAIRS, b=PAIR, h=2)
    V = [v.rearrange("p (b h e) -> p b h e", b=PAIR, e=VW) for v in two(PAIR * H0 * VW)]
    mx = k.take(PAIR * HPAIRS)
    prob = k.take(PAIR * 512).rearrange("p (b n) -> p b n", b=PAIR)
    probT = k.take(PAIR * 512).rearrange("p (b c n) -> p b c n", b=PAIR, c=HPAIRS)
    rec = k.take(H0)
    on = k.take(INNER)
    oT = k.take(INNER)
    s = k.sigs(T, dict(
        zhat=1, z_ready=3, ctxT_sb=1, k_psum=1, k2_psum=1, q_psum=1, v_psum=2, kcos=1, ksin=1,
        krot=1, klat=1, qbd=2, v_sb=2, s_psum=2, smax=2, sshift=2, prob=2, pt_psum=2, pt_sb=2, av=1, recip=1,
        onorm=1, ot_psum=1, ot_sb=1, out_psum=1))
    ctx_loaded = k.transfers(T, "ctx_loaded")
    preset = k.sem("L0_preset")
    ctx_dram = k.a["ctx_1024"].rearrange("(t b) s d -> t (b s) d", b=PAIR)
    cosT = k.konst[:, C_COS:C_COS + SEQ].unsqueeze(1).broadcast_to([P, 8, SEQ])
    sinT = k.konst[:, C_SIN:C_SIN + SEQ].unsqueeze(1).broadcast_to([P, 8, SEQ])

    def sync(sp):
        k.ready(sp)

        def body(at):
            if t := at(3):
                if t.has(2):
                    sp.wait_ge(*f["xT_psum"](t.back(2)))
                sp.dma_start(cin[t.par], ctx_dram[t.idx]).then_inc(ctx_loaded.at(t), 16)
            if t := at(1):
                sp.wait_ge(*s["z_ready"](t))
                sp.dma_start(k.z1T_dram[t.idx], z1o[t.par]).then_inc(k.z1T_stored.at(t), 16)
                sp.wait_ge(*s["ctxT_sb"](t))
                sp.dma_start(k.ctxT_dram[t.idx], cto[t.par]).then_inc(k.ctxT_stored.at(t), 16)
        steps(sp, T, 3, 1, body)

    def gpsimd(pool):
        k.ready(pool)
        pool.memset(V[0][:, :, :, HD0:VW], 1.0).then_inc(preset, 1)
        pool.memset(V[1][:, :, :, HD0:VW], 1.0).then_inc(preset, 1)
        pool.memset(QBD, 0.0).then_inc(preset, 1)
        pool.wait_ge(preset, 3)

        def body(at):
            if t := at(2):
                sl = t.par
                pool.wait_ge(*f["aggr"](t))
                k.hold(pool)
                pool.tensor_scalar(k.ve[:, sl, 0:1], k.mv[:, sl, 0, 1:2], 1.0 + EPS, EPS * EPS, ALU.mult, ALU.add)
                pool.tensor_scalar(k.ve[:, sl, 1:2], k.mv[:, sl, 1, 1:2], 1.0, EPS, ALU.mult, ALU.add)\
                    .then_inc(f["vareps"].sem, 1)
                pool.wait_ge(*f["vareps"](t))
                pool.tensor_tensor(k.rstd[:, sl, :], k.ve[:, sl, :],
                                   k.konst[:, C_MHALF:C_MHALF + 2], ALU.pow).then_inc(f["rstd_ready"].sem, 1)
            if t := at(1):
                pool.wait_ge(*s["kcos"](t))
                k.hold(pool)
                pool.wait_ge(*s["ksin"](t))
                pool.tensor_tensor(KT[:, :, 0], rotA.rearrange("p (c b i) -> p c b i", c=HPAIRS, b=PAIR),
                                   rotB.rearrange("p (c b i) -> p c b i", c=HPAIRS, b=PAIR), ALU.add)\
                    .then_inc(s["krot"].sem, 1)
        steps(pool, T, 2, 0, body)

    def tensor(pe):
        k.ready(pe)
        pe.wait_ge(preset, 3)

        def body(at):
            if t := at(0):
                pe.wait_ge(*s["krot"](t))
                pe.wait_ge(*s["klat"](t))
                pe.wait_ge(*s["qbd"](t))
                for b in range(PAIR):
                    for c in range(HPAIRS):
                        mm = pe.matmul(ps[:, 6 + b, c * P:(c + 1) * P], QBD[:, c, b].rearrange("p h i -> p (h i)"),
                                       KT[:, c, :, b, :], start=True, stop=True)
                    mm.then_inc(s["s_psum"].sem, 1)
            if t := at(1):
                pe.wait_ge(*s["z_ready"](t))
                if t.has(2):
                    pe.wait_ge(*s["pt_sb"](t.back(2)))
                for c in range(HPAIRS):
                    w = k.wk0[:, c * P:(c + 1) * P]
                    pe.matmul(ps[:, 0, c * P:(c + 1) * P], w, Z[t.par][:, :, 0], start=True, stop=True)
                    mm = pe.matmul(ps[:, 1, c * P:(c + 1) * P], w, Z[t.par][:, :, 1], start=True, stop=True)
                mm.then_inc(s["k_psum"].sem, 1)
                if t.has(2):
                    pe.wait_ge(*s["onorm"](t.back(2)))
                for c in range(HPAIRS):
                    mm = pe.matmul(ps[:, 2, c * P:(c + 1) * P], k.wr0[:, c * P:(c + 1) * P], Z[t.par][:, :, 0],
                                   start=True, stop=True)
                mm.then_inc(s["k2_psum"].sem, 1)
                for c in range(HPAIRS):
                    mm = pe.matmul(ps[:, 3, c * P:(c + 1) * P], k.wq0[:, c * P:(c + 1) * P], Z[t.par][:, :, 1],
                                   start=True, stop=True)
                mm.then_inc(s["q_psum"].sem, 1)
            if t := at(-1):
                pe.wait_ge(*s["onorm"](t))
                if at(0):
                    pe.wait_ge(*s["v_sb"](at(0)))
                for c in range(HPAIRS):
                    mm = pe.transpose(ps[:, 5, c * P:(c + 1) * P], on[:, c * P:(c + 1) * P], k.ident)
                mm.then_inc(s["ot_psum"].sem, 1)
            if t := at(2):
                pe.wait_ge(*f["xhat_ready"](t))
                pe.wait_ge(*s["zhat"](t))
                if t.has(1):
                    pe.wait_ge(*s["ctxT_sb"](t.back(1)))
                if t.has(2):
                    pe.wait_ge(*s["v_sb"](t.back(2)))
                pe.transpose(ps[:, 4, 0:P], k.xh[:, t.par, :], k.ident)
                pe.transpose(ps[:, 4, P:2 * P], zh[t.par], k.ident)
                pe.transpose(ps[:, 4, 2 * P:3 * P], cin[t.par], k.ident).then_inc(f["xT_psum"].sem, 1)
            if t := at(-1):
                pe.wait_ge(*s["ot_sb"](t))
                for c in range(HPAIRS):
                    mm = pe.matmul(ps[:, 5, 0:D], oT[:, c * P:(c + 1) * P], k.wo0[:, c, :],
                                   start=c == 0, stop=c == HPAIRS - 1)
                mm.then_inc(s["out_psum"].sem, 1)
            if t := at(0):
                if at(1):
                    pe.wait_ge(*s["kcos"](at(1)))
                    pe.wait_ge(*s["klat"](at(1)))
                for b in range(PAIR):
                    pe.wait_ge(*s["prob"](t, b + 1))
                    for c in range(HPAIRS):
                        mm = pe.transpose(ps[:, b, c * P:(c + 1) * P], prob[:, b, c * P:(c + 1) * P], k.ident)
                    mm.then_inc(s["pt_psum"].sem, 1)
            if t := at(1):
                if at(2):
                    pe.wait_ge(*s["z_ready"](at(2)))
                    pe.wait_ge(*s["ctxT_sb"](at(2)))
                if at(-1):
                    pe.wait_ge(*f["x_updated"](at(-1)))
                for b in range(PAIR):
                    mm = pe.matmul(ps[:, 4 + b, :], Z[t.par][:, b].rearrange("p s i -> p (s i)"), k.wv0[:, :],
                                   start=True, stop=True)
                    mm.then_inc(s["v_psum"].sem, 1)
            if t := at(0):
                pe.wait_ge(*s["pt_sb"](t))
                pe.wait_ge(*s["v_sb"](t))
                if at(1):
                    pe.wait_ge(*s["ksin"](at(1)))
                    pe.wait_ge(*s["qbd"](at(1)))
                for h in range(H0):
                    for b in range(PAIR):
                        mm = pe.matmul(ps[b * 64:b * 64 + 64, 2 + h // 4, (h % 4) * VW:(h % 4 + 1) * VW],
                                       probT[:, b, h // 2, (h % 2) * 64:(h % 2) * 64 + 64], V[t.par][:, b, h, :],
                                       start=True, stop=True)
                mm.then_inc(s["av"].sem, 1)
        steps(pe, T, 2, 1, body)

    def vector(dve):
        k.ready(dve)

        def body(at):
            if t := at(2):
                sl = t.par
                dve.wait_ge(*ctx_loaded(t))
                k.hold(dve)
                dve.bn_stats(k.st[:, sl, 1, :], cin[sl])
                dve.bn_stats(k.st[:, sl, 0, :], k.x[:, t.idx, :]).then_inc(f["stats"].sem, 1)
                dve.wait_ge(*f["stats"](t))
                k.hold(dve)
                dve.bn_aggr(k.mv[:, sl, 1, :], k.st[:, sl, 1, :])
                dve.bn_aggr(k.mv[:, sl, 0, :], k.st[:, sl, 0, :]).then_inc(f["aggr"].sem, 1)
            if t := at(-1):
                dve.wait_ge(*s["av"](t))
                heads = ps[:, 2:4, 0:4 * VW].rearrange("p k (h e) -> p k h e", e=VW)
                dve.reciprocal(rec.rearrange("p (k h) -> p k h", k=2), heads[:, :, :, HD0]).then_inc(s["recip"].sem, 1)
                dve.wait_ge(*s["recip"](t))
                dve.tensor_tensor(on.rearrange("p (k h e) -> p k h e", k=2, e=HD0), heads[:, :, :, 0:HD0],
                                  rec.rearrange("p (k h) -> p k h", k=2).unsqueeze(3).broadcast_to([P, 2, 4, HD0]),
                                  ALU.mult).then_inc(s["onorm"].sem, 1)
            if t := at(0):
                for b in range(PAIR):
                    sc = ps[:, 6 + b, :].rearrange("p (c n) -> p c n", c=HPAIRS)
                    m = mx[:, b * HPAIRS:(b + 1) * HPAIRS]
                    dve.wait_ge(*s["s_psum"](t, b + 1))
                    dve.tensor_reduce(m, sc, AX.X, ALU.max).then_inc(s["smax"].sem, 1)
                    dve.wait_ge(*s["smax"](t, b + 1))
                    dve.tensor_tensor(prob[:, b].rearrange("p (c n) -> p c n", c=HPAIRS), sc,
                                      m.unsqueeze(2).broadcast_to([P, HPAIRS, P]), ALU.subtract)\
                        .then_inc(s["sshift"].sem, 1)
            if t := at(1):
                kk = [ps[:, n, :].rearrange("p (c i) -> p c i", i=SEQ) for n in (0, 2)]
                if t.has(1):
                    dve.wait_ge(*s["krot"](t.back(1)))
                dve.wait_ge(*s["k_psum"](t))
                dve.tensor_tensor(rotA.rearrange("p (c i) -> p c i", i=SEQ), kk[0], cosT, ALU.mult)\
                    .then_inc(s["kcos"].sem, 1)
                dve.wait_ge(*s["k2_psum"](t))
                dve.tensor_tensor(rotB.rearrange("p (c i) -> p c i", i=SEQ), kk[1], sinT, ALU.mult)\
                    .then_inc(s["ksin"].sem, 1)
            if t := at(2):
                sl = t.par
                tile_xhat(k, f, dve, t, sl)
                dve.tensor_scalar(zh[sl], cin[sl], k.mv[:, sl, 1, 0:1], k.rstd[:, sl, 1:2],
                                  ALU.subtract, ALU.mult).then_inc(s["zhat"].sem, 1)
                if t.has(2):
                    dve.wait_ge(*k.z1T_stored(t.back(2)))
                dve.wait_ge(*f["xT_psum"](t))
                for dst, n, g in ((Z[sl][:, :, 1], 0, 2), (Z[sl][:, :, 0], 1, 0),
                                  (z1o[sl].rearrange("p (b i) -> p b i", b=PAIR), 1, 4)):
                    dve.tensor_scalar(dst, ps[:, 4, n * P:(n + 1) * P].rearrange("p (b i) -> p b i", b=PAIR), k.aff[:, g:g + 1], k.aff[:, g + 1:g + 2],
                                      ALU.mult, ALU.add).then_inc(s["z_ready"].sem, 1)
            if t := at(-1):
                dve.wait_ge(*s["out_psum"](t))
                dve.scalar_tensor_tensor(out=k.x[:, t.idx, :], in0=ps[:, 5, 0:D], scalar=k.gates[:, 0:1],
                                         in1=k.x[:, t.idx, :], op0=ALU.mult, op1=ALU.add)\
                    .then_inc(f["x_updated"].sem, 1)
        steps(dve, T, 2, 1, body)

    def scalar(act):
        k.ready(act)
        act.wait_ge(preset, 3)

        def body(at):
            if t := at(0):
                for b in range(PAIR):
                    act.wait_ge(*s["sshift"](t, b + 1))
                    act.activation(prob[:, b], prob[:, b], ACT.Exp, scale=HD0 ** -0.5).then_inc(s["prob"].sem, 1)
            if t := at(1):
                act.wait_ge(*s["k_psum"](t))
                act.activation(KT[:, :, 1], ps[:, 1, :].rearrange("p (c b i) -> p c b i", c=HPAIRS, b=PAIR),
                               ACT.Copy).then_inc(s["klat"].sem, 1)
                act.wait_ge(*s["q_psum"](t))
                for h in range(2):
                    rows = slice(64 * h, 64 * h + 64)
                    act.activation(QBD[rows, :, :, h, :],
                                   ps[rows, 3, :].rearrange("p (c b i) -> p c b i", c=HPAIRS, b=PAIR),
                                   ACT.Copy).then_inc(s["qbd"].sem, 1)
            if t := at(-1):
                act.wait_ge(*s["ot_psum"](t))
                act.activation(oT, ps[:, 5, :], ACT.Copy).then_inc(s["ot_sb"].sem, 1)
            if t := at(2):
                if t.has(2):
                    act.wait_ge(*k.ctxT_stored(t.back(2)))
                act.wait_ge(*s["z_ready"](t))
                act.activation(cto[t.par], ps[:, 4, 2 * P:3 * P], ACT.Copy).then_inc(s["ctxT_sb"].sem, 1)
            if t := at(0):
                for b in range(PAIR):
                    act.wait_ge(*s["pt_psum"](t, b + 1))
                    act.activation(probT[:, b].rearrange("p c n -> p (c n)"), ps[:, b, :], ACT.Copy)\
                        .then_inc(s["pt_sb"].sem, 1)
            if t := at(1):
                for b in range(PAIR):
                    act.wait_ge(*s["v_psum"](t, b + 1))
                    act.activation(V[t.par][:, b, :, 0:HD0], ps[:, 4 + b, :].rearrange("p (h e) -> p h e", e=HD0),
                                   ACT.Copy).then_inc(s["v_sb"].sem, 1)
        steps(act, T, 2, 1, body)

    return dict(sync=sync, gpsimd=gpsimd, tensor=tensor, vector=vector, scalar=scalar)


def sub(g, j):
    return Tile(g.idx * GROUP + j, j % 2)


class Route:

    OPS = 2 * GROUP + 3

    def __init__(self, k):
        self.k = k
        self.score = k.take(GROUP * EXPERTS).rearrange("p (j e) -> p j e", j=GROUP)
        self.best = k.take(GROUP * 8).rearrange("p (j e) -> p j e", j=GROUP)
        self.where = k.take(GROUP * 8).bitcast(U32).rearrange("p (j e) -> p j e", j=GROUP)
        self.wheref = k.take(GROUP * 2).rearrange("p (j e) -> p j e", j=GROUP)
        self.hit = [k.take(GROUP * EXPERTS).rearrange("p (j e) -> p j e", j=GROUP) for _ in range(2)]
        self.done = k.sig(k.T // GROUP, "routed", self.OPS)

    def run(self, dve, g):
        k, wide = self.k, [P, GROUP, EXPERTS]
        for j in range(GROUP):
            dve.max(self.best[:, j], self.score[:, j]).then_inc(self.done.sem, 1)
        dve.wait_ge(*self.done(g, GROUP))
        k.hold(dve)
        for j in range(GROUP):
            dve.max_index(self.where[:, j], self.best[:, j], self.score[:, j]).then_inc(self.done.sem, 1)
        dve.wait_ge(*self.done(g, 2 * GROUP))
        dve.tensor_copy(self.wheref, self.where[:, :, 0:2]).then_inc(self.done.sem, 1)
        dve.wait_ge(*self.done(g, 2 * GROUP + 1))
        for n in range(2):
            iota = k.konst[:, C_IOTA:C_IOTA + EXPERTS].unsqueeze(1).broadcast_to(wide)
            dve.tensor_tensor(self.hit[n], iota, self.wheref[:, :, n:n + 1].broadcast_to(wide), ALU.is_equal)\
                .then_inc(self.done.sem, 1)


def group_front(k, f, xTg, bank, twice=False):
    def dve_stats(dve, g, j):
        dve.bn_stats(k.st[:, j, 0, :], k.x[:, sub(g, j).idx, :]).then_inc(f["stats"].sem, 1)

    def dve_aggr(dve, g):
        dve.wait_ge(*f["stats"](sub(g, GROUP - 1)))
        k.hold(dve)
        for j in range(GROUP):
            dve.bn_aggr(k.mv[:, j, 0, :], k.st[:, j, 0, :]).then_inc(f["aggr"].sem, 1)

    def dve_xhat(dve, g, j):
        if g.has(1) and j == 0:
            dve.wait_ge(*f["xT_psum"](g.back(1)))
        tile_xhat(k, f, dve, sub(g, j), j)

    def dve_part(dve, g):
        for j in range(GROUP):
            dve_stats(dve, g, j)
        dve_aggr(dve, g)
        for j in range(GROUP):
            dve_xhat(dve, g, j)

    dve_part.stats, dve_part.aggr, dve_part.xhat = dve_stats, dve_aggr, dve_xhat

    def pool_part(pool, g):
        last = sub(g, GROUP - 1)
        pool.wait_ge(*f["aggr"](last))
        k.hold(pool)
        pool.tensor_scalar(k.ve[:, :, 0], k.mv[:, :, 0, 1], 1.0 + EPS if twice else 1.0,
                           EPS * EPS if twice else EPS, ALU.mult, ALU.add).then_inc(f["vareps"].sem, GROUP)
        pool.wait_ge(*f["vareps"](last))
        pool.tensor_tensor(k.rstd[:, :, 0], k.ve[:, :, 0], k.konst[:, C_MHALF:C_MHALF + GROUP],
                           ALU.pow).then_inc(f["rstd_ready"].sem, GROUP)

    def pe_part(pe, g):
        pe.wait_ge(*f["xhat_ready"](sub(g, GROUP - 1)))
        if g.has(1):
            pe.wait_ge(*f["xT_sb"](g.back(1)))
        for j in range(GROUP):
            mm = pe.transpose(k.psum[:, bank, j * P:(j + 1) * P], k.xh[:, j, :], k.ident)
        mm.then_inc(f["xT_psum"].sem, 1)

    def act_part(act, g):
        act.wait_ge(*f["xT_psum"](g))
        act.activation(xTg[g.par], k.psum[:, bank, :], ACT.Copy).then_inc(f["xT_sb"].sem, 1)
    return dve_part, pool_part, pe_part, act_part


def group_signals(k, no):
    f = k.front(no)
    f.update(k.sigs(k.T // GROUP, dict(xT_psum=1, xT_sb=1)))
    return f


def experts0(k, no):
    ps, G = k.psum, k.T // GROUP
    f = group_signals(k, no)
    k.stage_memory()
    xTg = [k.take(GCOLS) for _ in range(2)]
    route = Route(k)
    gap, e, den, rden = (k.take(GROUP) for _ in range(4))
    w = [k.take(GROUP) for _ in range(2)]
    part = [k.take(GROUP * EXPERTS).rearrange("p (j e) -> p j e", j=GROUP) for _ in range(2)]
    coef = k.take(GROUP * EXPERTS).rearrange("p (j e) -> p j e", j=GROUP)
    s = k.sigs(G, dict(
        l_psum=1, l_sb=1, gap=1, e=1, w=4, part=2, coef=1, y_psum=GROUP, acc=GROUP * (EXPERTS - 1)))
    d_front, p_front, t_front, a_front = group_front(k, f, xTg, 0)
    wide = [P, GROUP, EXPERTS]

    def gpsimd(pool):
        steps(pool, G, 1, 0, lambda at: at(1) and p_front(pool, at(1)))

    def tensor(pe):
        def experts(g, j):
            bank = 2 + 2 * (j % 2)
            t = sub(g, j)
            if t.has(2):
                pe.wait_ge(*f["x_updated"](t.back(2)))
            for h in range(2):
                mm = pe.matmul(ps[:, bank + h, :], xTg[g.par][:, j * P:(j + 1) * P],
                               k.we0[:, 4 * h:4 * h + 4, :].rearrange("p e m -> p (e m)"), start=True, stop=True)
            mm.then_inc(s["y_psum"].sem, 1)

        def body(at):
            g, nxt = at(0), at(1)
            if g:
                pe.wait_ge(*f["xT_sb"](g))
                experts(g, 0)
                experts(g, 1)
            if nxt:
                t_front(pe, nxt)
            if g:
                experts(g, 2)
                experts(g, 3)
            if nxt:
                pe.wait_ge(*f["xT_sb"](nxt))
                if nxt.has(1):
                    pe.wait_ge(*s["l_sb"](nxt.back(1)))
                for j in range(GROUP):
                    mm = pe.matmul(ps[:, 1, j * EXPERTS:(j + 1) * EXPERTS], xTg[nxt.par][:, j * P:(j + 1) * P],
                                   k.wg0[:, :], start=True, stop=True)
                mm.then_inc(s["l_psum"].sem, 1)
        steps(pe, G, 1, 0, body)

    def vector(dve):
        def routing(g):
            dve.wait_ge(*s["l_psum"](g))
            dve.tensor_copy(route.score, ps[:, 1, 0:GROUP * EXPERTS].rearrange("p (j e) -> p j e", j=GROUP))\
                .then_inc(s["l_sb"].sem, 1)
            dve.wait_ge(*s["l_sb"](g))
            k.hold(dve)
            route.run(dve, g)
            dve.tensor_tensor(gap, route.best[:, :, 1], route.best[:, :, 0], ALU.subtract).then_inc(s["gap"].sem, 1)
            dve.wait_ge(*s["e"](g))
            dve.tensor_scalar(den, e, 1.0, None, ALU.add).then_inc(s["w"].sem, 1)
            dve.wait_ge(*s["w"](g, 1))
            dve.reciprocal(rden, den).then_inc(s["w"].sem, 1)
            dve.wait_ge(*s["w"](g, 2))
            dve.tensor_scalar(w[0], rden, k.gates[:, 4:5], None, ALU.mult).then_inc(s["w"].sem, 1)
            dve.wait_ge(*s["w"](g, 3))
            dve.tensor_tensor(w[1], e, w[0], ALU.mult).then_inc(s["w"].sem, 1)
            dve.wait_ge(*s["w"](g, 4))
            dve.wait_ge(*route.done(g))
            for n in range(2):
                dve.tensor_tensor(part[n], route.hit[n], w[n].unsqueeze(2).broadcast_to(wide), ALU.mult)\
                    .then_inc(s["part"].sem, 1)
            dve.wait_ge(*s["part"](g))
            dve.tensor_tensor(coef, part[0], part[1], ALU.add).then_inc(s["coef"].sem, 1)

        def body(at):
            if g := at(0):
                routing(g)
            if g := at(1):
                d_front(dve, g)
            if g := at(0):
                dve.wait_ge(*s["coef"](g))
                for j in range(GROUP):
                    t = sub(g, j)
                    bank = 2 + 2 * (j % 2)
                    dve.wait_ge(*s["y_psum"](g, j + 1))
                    for n in range(EXPERTS):
                        y = ps[:, bank + n // 4, (n % 4) * D:(n % 4 + 1) * D]
                        x = k.x[:, t.idx, :]
                        if n:
                            dve.wait_ge(*s["acc"](g, j * (EXPERTS - 1) + n))
                        dve.scalar_tensor_tensor(out=x, in0=y, scalar=coef[:, j, n:n + 1], in1=x, op0=ALU.mult,
                                                 op1=ALU.add)\
                            .then_inc(s["acc"].sem if n < EXPERTS - 1 else f["x_updated"].sem, 1)
        steps(dve, G, 1, 0, body)

    def scalar(act):
        def body(at):
            if g := at(0):
                act.wait_ge(*s["gap"](g))
                act.activation(e, gap, ACT.Exp).then_inc(s["e"].sem, 1)
            if g := at(1):
                a_front(act, g)
        steps(act, G, 1, 0, body)

    return dict(gpsimd=gpsimd, tensor=tensor, vector=vector, scalar=scalar)


def attention1(k, no):
    ps, T = k.psum, k.T
    f = k.front(no)
    f["xT_psum"] = k.sig(T, "xT_psum")
    k.stage_memory()
    two = lambda n: [k.take(n) for _ in range(2)]
    HALF = H1 // 2
    zt = two(P)
    zs = [z.rearrange("p (b u i) -> p b u i", b=PAIR, u=2) for z in two(4 * SEQ)]
    QB = [q.rearrange("p (n b i) -> p n b i", n=2, b=PAIR) for q in two(4 * SEQ)]
    KM = [v.rearrange("p (n h i) -> p n h i", n=2, h=HALF) for v in two(2 * HALF * SEQ)]
    NV = HD1 + 1
    VB = [v.rearrange("p (b n h e) -> p b n h e", b=PAIR, h=2, e=NV) for v in two(PAIR * H1 * NV)]
    mx = k.take(H1).rearrange("p (n h) -> p n h", n=2)
    prob = [v.rearrange("p (n h i) -> p n h i", n=2, h=HALF) for v in two(H1 * SEQ)]
    probT = k.take(H1 * SEQ).rearrange("p (n i) -> p n i", n=2)
    rec = k.take(H1)
    on, oT = k.take(D), k.take(D)
    loads = [k.transfers(T, f"z_loaded{u}") for u in range(2)]
    s = k.sigs(T, dict(
        zt=1, k_psum=1, vq_psum=1, qb=2, km=1, vb=2, s_psum=2, smax=2, sshift=2, prob=2, pt_psum=2, pt_sb=2,
        av=1, recip=1, onorm=1, ot_psum=1, ot_sb=1, out_psum=1))
    preset = k.sem("A1_preset")

    def sync(sp):
        def body(at):
            if t := at(3):
                if t.has(2):
                    sp.wait_ge(*s["vq_psum"](t.back(2)))
                for u in range(2):
                    sp.dma_start(zs[t.par][:, :, u, :], k.z1T_dram[t.idx].rearrange("p (b i) -> p b i", b=PAIR))\
                        .then_inc(loads[u].at(t), 16)
        steps(sp, T, 3, 0, body)

    def gpsimd(pool):
        for n in range(2):
            pool.memset(VB[n], 0.0).then_inc(preset, 1)
            pool.memset(QB[n], 0.0).then_inc(preset, 1)
        pool.wait_ge(preset, 4)
        for n in range(2):
            for h in range(2):
                pool.memset(VB[n][64 * h:64 * h + 64, :, :, h, HD1:NV], 1.0).then_inc(preset, 1)
        pool.wait_ge(preset, 8)

        def body(at):
            if t := at(3):
                tile_rstd(k, f, pool, t, t.par, True)
        steps(pool, T, 3, 0, body)

    def tensor(pe):
        def body(at):
            if t := at(0):
                pe.wait_ge(*s["qb"](t))
                pe.wait_ge(*s["km"](t))
                for n in range(2):
                    pe.matmul(ps[:, 3 + n, :], QB[t.par][:, n].rearrange("p b i -> p (b i)"),
                              KM[t.par][:, n].rearrange("p h i -> p (h i)"), start=True, stop=True)\
                        .then_inc(s["s_psum"].sem, 1)
            if t := at(-2):
                pe.wait_ge(*s["ot_sb"](t))
                pe.matmul(ps[:, 0, D:2 * D], oT, k.w1a[:, 3, :], start=True, stop=True).then_inc(s["out_psum"].sem, 1)
            if t := at(-1):
                pe.wait_ge(*s["vb"](t))
                for n in range(2):
                    pe.wait_ge(*s["pt_sb"](t, n + 1))
                    for c in range(4):
                        for b in range(PAIR):
                            m = 4 * n + c
                            mm = pe.matmul(ps[64 * b:64 * b + 64, 7, m * 2 * NV:(m + 1) * 2 * NV],
                                           probT[:, n, c * P + b * SEQ:c * P + (b + 1) * SEQ],
                                           VB[t.par][:, b, m].rearrange("p h e -> p (h e)"), start=True, stop=True)
                mm.then_inc(s["av"].sem, 1)
            if t := at(2):
                for u in range(2):
                    pe.wait_ge(*loads[u](t))
                if t.has(1):
                    pe.wait_ge(*s["km"](t.back(1)))
                for n in range(2):
                    for b in range(PAIR):
                        mm = pe.matmul(ps[64 * b:64 * b + 64, 2, n * SEQ:(n + 1) * SEQ],
                                       k.w1a[:, 1, 64 * n:64 * n + 64], zs[t.par][:, b, 0, :], start=True, stop=True)
                mm.then_inc(s["k_psum"].sem, 1)
            if t := at(1):
                pe.wait_ge(*s["zt"](t))
                for b in range(PAIR):
                    pe.matmul(ps[:, 1, (b + 1) * D:(b + 2) * D], zs[t.par][:, b].rearrange("p u i -> p (u i)"),
                              k.w1a[:, 2, :], start=True, stop=True)
                for n in range(2):
                    for b in range(PAIR):
                        mm = pe.matmul(ps[64 * b:64 * b + 64, 1, n * SEQ:(n + 1) * SEQ],
                                       k.w1a[:, 0, 64 * n:64 * n + 64], zt[t.par][:, b * SEQ:(b + 1) * SEQ],
                                       start=True, stop=True)
                mm.then_inc(s["vq_psum"].sem, 1)
            if t := at(0):
                for n in range(2):
                    pe.wait_ge(*s["prob"](t, n + 1))
                    for c in range(4):
                        mm = pe.transpose(ps[:, 5 + n, c * P:(c + 1) * P],
                                          prob[t.par][:, n, 2 * c:2 * c + 2].rearrange("p h i -> p (h i)"), k.ident)
                    mm.then_inc(s["pt_psum"].sem, 1)
            if t := at(-1):
                pe.wait_ge(*s["onorm"](t))
                if t.has(1):
                    pe.wait_ge(*f["x_updated"](t.back(1)))
                pe.transpose(ps[:, 0, 0:D], on, k.ident).then_inc(s["ot_psum"].sem, 1)
            if t := at(2):
                pe.wait_ge(*f["xhat_ready"](t))
                if t.has(1):
                    pe.wait_ge(*s["vb"](t.back(1)))
                pe.transpose(ps[:, 1, 3 * D:4 * D], k.xh[:, t.par, :], k.ident).then_inc(f["xT_psum"].sem, 1)
        steps(pe, T, 2, 2, body)

    def vector(dve):
        def maxima(t, n):
            dve.wait_ge(*s["s_psum"](t, n + 1))
            dve.tensor_reduce(mx[:, n], ps[:, 3 + n, :].rearrange("p (h i) -> p h i", i=SEQ), AX.X, ALU.max)\
                .then_inc(s["smax"].sem, 1)

        def shift(t, n):
            dve.wait_ge(*s["smax"](t, n + 1))
            dve.tensor_tensor(prob[t.par][:, n], ps[:, 3 + n, :].rearrange("p (h i) -> p h i", i=SEQ),
                              mx[:, n].unsqueeze(2).broadcast_to([P, HALF, SEQ]), ALU.subtract)\
                .then_inc(s["sshift"].sem, 1)

        def body(at):
            if t := at(0):
                maxima(t, 0)
            if t := at(3):
                dve.bn_stats(k.st[:, t.par, 0, :], k.x[:, t.idx, :]).then_inc(f["stats"].sem, 1)
            if t := at(0):
                shift(t, 0)
                maxima(t, 1)
            if t := at(3):
                dve.wait_ge(*f["stats"](t))
                k.hold(dve)
                dve.bn_aggr(k.mv[:, t.par, 0, :], k.st[:, t.par, 0, :]).then_inc(f["aggr"].sem, 1)
            if t := at(0):
                shift(t, 1)
            heads = ps[:, 7, 0:H1 * NV].rearrange("p (n e) -> p n e", e=NV)
            if t := at(-1):
                dve.wait_ge(*s["av"](t))
                dve.reciprocal(rec, heads[:, :, HD1]).then_inc(s["recip"].sem, 1)
            if t := at(-2):
                dve.wait_ge(*s["out_psum"](t))
                dve.scalar_tensor_tensor(out=k.x[:, t.idx, :], in0=ps[:, 0, D:2 * D], scalar=k.gates[:, 1:2],
                                         in1=k.x[:, t.idx, :], op0=ALU.mult, op1=ALU.add)\
                    .then_inc(f["x_updated"].sem, 1)
            if t := at(-1):
                dve.wait_ge(*s["recip"](t))
                dve.tensor_tensor(on.rearrange("p (n e) -> p n e", e=HD1), heads[:, :, 0:HD1],
                                  rec.unsqueeze(2).broadcast_to([P, H1, HD1]), ALU.mult).then_inc(s["onorm"].sem, 1)
            if t := at(2):
                dve.wait_ge(*s["k_psum"](t))
                dve.tensor_tensor(KM[t.par], ps[:, 2, 0:P].rearrange("p (n i) -> p n i", n=2).unsqueeze(2)
                                  .broadcast_to([P, 2, HALF, SEQ]),
                                  k.konst[:, C_MASK8:C_MASK8 + HALF].unsqueeze(1).unsqueeze(3)
                                  .broadcast_to([P, 2, HALF, SEQ]), ALU.mult).then_inc(s["km"].sem, 1)
            if t := at(3):
                tile_xhat(k, f, dve, t, t.par)
        steps(dve, T, 3, 2, body)

    def scalar(act):
        act.wait_ge(preset, 8)

        def body(at):
            if t := at(0):
                for n in range(2):
                    act.wait_ge(*s["sshift"](t, n + 1))
                    act.activation(prob[t.par][:, n], prob[t.par][:, n], ACT.Exp, scale=HD1 ** -0.5)\
                        .then_inc(s["prob"].sem, 1)
            if t := at(1):
                act.wait_ge(*s["vq_psum"](t))
                for b in range(PAIR):
                    rows = slice(64 * b, 64 * b + 64)
                    act.activation(QB[t.par][rows, :, b, :], ps[rows, 1, 0:P].rearrange("p (n i) -> p n i", n=2),
                                   ACT.Copy).then_inc(s["qb"].sem, 1)
                for h in range(2):
                    rows = slice(64 * h, 64 * h + 64)
                    act.activation(VB[t.par][rows, :, :, h, 0:HD1],
                                   ps[rows, 1, D:3 * D].rearrange("p (b n h e) -> p b n h e", b=PAIR, h=2,
                                                                  e=HD1)[:, :, :, h],
                                   ACT.Copy).then_inc(s["vb"].sem, 1)
            if t := at(0):
                for n in range(2):
                    act.wait_ge(*s["pt_psum"](t, n + 1))
                    act.activation(probT[:, n], ps[:, 5 + n, :], ACT.Copy).then_inc(s["pt_sb"].sem, 1)
            if t := at(-1):
                act.wait_ge(*s["ot_psum"](t))
                act.activation(oT, ps[:, 0, 0:D], ACT.Copy).then_inc(s["ot_sb"].sem, 1)
            if t := at(2):
                act.wait_ge(*f["xT_psum"](t))
                act.activation(zt[t.par], ps[:, 1, 3 * D:4 * D], ACT.Identity, scale=k.aff[:, 6:7],
                               bias=k.aff[:, 7:8]).then_inc(s["zt"].sem, 1)
        steps(act, T, 2, 1, body)

    return dict(sync=sync, gpsimd=gpsimd, tensor=tensor, vector=vector, scalar=scalar)


def spiking1(k, no):
    ps, G = k.psum, k.T // GROUP
    f = group_signals(k, no)
    k.stage_memory()
    NC = FF1 // P
    xTg = [k.take(GCOLS) for _ in range(2)]
    relu = k.take(NC * GCOLS).rearrange("p (c n) -> p c n", c=NC)
    sq = [v.rearrange("p (c n) -> p c n", c=NC) for v in (k.take(NC * GCOLS) for _ in range(2))]
    mem = [k.take(GCOLS) for _ in range(2)]
    spike = [k.take(GCOLS) for _ in range(SPIKE_STEPS)]
    decayed, drive, count = k.take(GCOLS), [k.take(GCOLS) for _ in range(2)], [k.take(GCOLS) for _ in range(2)]
    s = k.sigs(G, dict(h_psum=NC, relu=NC, sq=NC, y_psum=1, drive=1, decayed=SPIKE_STEPS - 1,
                       mem=SPIKE_STEPS - 1, spike=SPIKE_STEPS, count=SPIKE_STEPS - 1))
    d_front, p_front, t_front, a_front = group_front(k, f, xTg, 0)

    def gpsimd(pool):
        def body(at):
            if g := at(3):
                p_front(pool, g)
            if g := at(-1):
                c = count[g.par]
                if g.has(2):
                    pool.wait_ge(*f["x_updated"](sub(g.back(2), GROUP - 1)))
                for n in range(1, SPIKE_STEPS):
                    pool.wait_ge(*s["spike"](g, n + 1))
                    if n > 1:
                        pool.wait_ge(*s["count"](g, n - 1))
                    pool.tensor_tensor(c, spike[n], spike[0] if n == 1 else c, ALU.add).then_inc(s["count"].sem, 1)
        steps(pool, G, 3, 1, body)

    def tensor(pe):
        def body(at):
            if g := at(2):
                t_front(pe, g)
            if g := at(1):
                pe.wait_ge(*f["xT_sb"](g))
                for c in range(NC):
                    if g.has(1):
                        pe.wait_ge(*s["relu"](g.back(1), c + 1))
                    pe.matmul(ps[:, 1 + c, :], k.wfc1[:, c * P:(c + 1) * P], xTg[g.par], start=True, stop=True)\
                        .then_inc(s["h_psum"].sem, 1)
            if g := at(0):
                pe.wait_ge(*s["sq"](g))
                if g.has(1):
                    pe.wait_ge(*s["drive"](g.back(1)))
                for j in range(GROUP):
                    for c in range(NC):
                        mm = pe.matmul(ps[:, 5, j * P:(j + 1) * P], sq[g.par][:, c, j * P:(j + 1) * P],
                                       k.wpr1[:, c, :], start=c == 0, stop=c == NC - 1)
                mm.then_inc(s["y_psum"].sem, 1)
        steps(pe, G, 2, 0, body)

    def vector(dve):
        def spikes(g, n, m):
            dve.tensor_scalar(spike[n], m, 1.0, None, ALU.is_gt).then_inc(s["spike"].sem, 1)

        def body(at):
            g, new = at(-1), at(3)
            if g:
                dve.wait_ge(*s["drive"](g))
                if g.has(1):
                    dve.wait_ge(*s["count"](g.back(1)))
                m = y = drive[g.par]
            for n in range(1, SPIKE_STEPS):
                if g:
                    if n > 1:
                        dve.wait_ge(*s["mem"](g, n - 1))
                    dve.scalar_tensor_tensor(out=decayed, in0=m, scalar=BETA, in1=y, op0=ALU.mult, op1=ALU.add)\
                        .then_inc(s["decayed"].sem, 1)
                    spikes(g, n - 1, m)
                    dve.wait_ge(*s["decayed"](g, n))
                    dve.scalar_tensor_tensor(out=mem[n % 2], in0=m, scalar=1.0, in1=decayed, op0=ALU.is_gt,
                                             op1=ALU.subtract, reverse1=True).then_inc(s["mem"].sem, 1)
                    m = mem[n % 2]
                if new and n < 3:
                    d_front.stats(dve, new, 2 * n - 2)
                    d_front.stats(dve, new, 2 * n - 1)
                if new and n == 3:
                    d_front.aggr(dve, new)
            old = at(-2)
            if old:
                update(old)
            if g:
                dve.wait_ge(*s["mem"](g))
                spikes(g, SPIKE_STEPS - 1, m)
            if new:
                for j in range(GROUP):
                    d_front.xhat(dve, new, j)

        def update(g):
            dve.wait_ge(*s["count"](g))
            for j in range(GROUP):
                x = k.x[:, sub(g, j).idx, :]
                dve.scalar_tensor_tensor(out=x, in0=count[g.par][:, j * P:(j + 1) * P], scalar=k.spike_gate[:, :],
                                         in1=x, op0=ALU.mult, op1=ALU.add).then_inc(f["x_updated"].sem, 1)
        steps(dve, G, 3, 2, body)

    def scalar(act):
        def body(at):
            if g := at(0):
                act.wait_ge(*s["y_psum"](g))
                if g.has(2):
                    act.wait_ge(*s["mem"](g.back(2)))
                act.activation(drive[g.par], ps[:, 5, :], ACT.Copy).then_inc(s["drive"].sem, 1)
            if g := at(2):
                a_front(act, g)
            if g := at(1):
                for c in range(NC):
                    act.wait_ge(*s["h_psum"](g, c + 1))
                    if g.has(1):
                        act.wait_ge(*s["sq"](g.back(1), c + 1))
                    act.activation(relu[:, c, :], ps[:, 1 + c, :], ACT.Relu).then_inc(s["relu"].sem, 1)
                for c in range(NC):
                    act.wait_ge(*s["relu"](g, c + 1))
                    act.activation(sq[g.par][:, c, :], relu[:, c, :], ACT.Square).then_inc(s["sq"].sem, 1)
        steps(act, G, 2, 0, body)

    return dict(gpsimd=gpsimd, tensor=tensor, vector=vector, scalar=scalar)


def context_attention(layer):
    biased, masked = layer == 2, layer == 3
    SCALE = D ** -0.5

    def stage(k, no):
        ps, N = k.psum, k.T // DUO
        f = k.front(no)
        f["xT_psum"] = k.sig(N, "xT_psum")
        k.stage_memory()
        two = lambda n: [k.take(n) for _ in range(2)]
        by_tile = lambda v: v.rearrange("p (j n) -> p j n", j=DUO)
        xT, qT = two(DUO * P), two(DUO * P)
        cT = [by_tile(v) for v in two(DUO * P)]
        cr = [by_tile(v) for v in two(DUO * D)]
        pT, uT = two(DUO * P), two(DUO * P)
        prob, sm = [by_tile(v) for v in two(DUO * P)], [by_tile(v) for v in two(DUO * SEQ)]
        xb = [by_tile(v) for v in two(DUO * D)]
        mx, nb, rs, rec = two(DUO), two(DUO), two(DUO), two(DUO)
        A, B = k.A[layer - 2], k.B[layer - 2]
        s = k.sigs(N, dict(
            xT_sb=1, q_psum=1, q_sb=1, s_psum=1, smax=1, nb=1, prob=DUO * PAIR, pt_psum=1, pt_sb=1, u_psum=1,
            u_sb=1, recip=1, out_psum=1))
        preset = k.sem(f"A{layer}_preset")
        s["biased" if biased else "masked"] = k.sig(N, "biased" if biased else "masked")
        cT_loaded, cr_loaded = k.transfers(N, "cT_loaded"), k.transfers(N, "cr_loaded")
        ctx_dram = k.a["ctx_1024"].rearrange("(n j b) s d -> n (b s) j d", j=DUO, b=PAIR)
        ctxT_dram = k.ctxT_dram.rearrange("(n j) p i -> n p j i", j=DUO)

        def tile(d, j):
            return Tile(d.idx * DUO + j, j)

        def slots(d):
            return slice(DUO * d.par, DUO * d.par + DUO)

        def sync(sp):
            def body(at):
                if d := at(2):
                    if d.has(2):
                        sp.wait_ge(*s["s_psum"](d.back(2)))
                    sp.dma_start(cT[d.par], ctxT_dram[d.idx]).then_inc(cT_loaded.at(d), 16)
                if d := at(1):
                    if d.has(2):
                        sp.wait_ge(*s["u_psum"](d.back(2)))
                    sp.dma_start(cr[d.par], ctx_dram[d.idx]).then_inc(cr_loaded.at(d), 16)
            steps(sp, N, 2, 0, body)

        def gpsimd(pool):
            for n in range(2):
                pool.memset(prob[n], 0.0).then_inc(preset, 1)

            def body(at):
                if d := at(4):
                    pool.wait_ge(*f["aggr"](tile(d, DUO - 1)))
                    k.hold(pool)
                    pool.tensor_scalar(k.ve[:, slots(d), 0], k.mv[:, slots(d), 0, 1], 1.0, EPS, ALU.mult, ALU.add)\
                        .then_inc(f["vareps"].sem, DUO)
                    pool.wait_ge(*f["vareps"](tile(d, DUO - 1)))
                    pool.tensor_tensor(k.rstd[:, slots(d), 0], k.ve[:, slots(d), 0],
                                       k.konst[:, C_MHALF:C_MHALF + DUO], ALU.pow).then_inc(f["rstd_ready"].sem, DUO)
                if biased and (d := at(0)):
                    if d.has(2):
                        pool.wait_ge(*f["x_updated"](tile(d.back(2), DUO - 1)))
                        k.hold(pool)
                    pool.tensor_tensor(xb[d.par], k.x[:, bass.ds(d.idx * DUO, DUO), :],
                                       k.bout[:, :].unsqueeze(1).broadcast_to([P, DUO, D]), ALU.add)\
                        .then_inc(s["biased"].sem, 1)
            steps(pool, N, 4, 0, body)

        def tensor(pe):
            def body(at):
                if d := at(-2):
                    pe.wait_ge(*s["u_sb"](d))
                    if d.has(2):
                        pe.wait_ge(*f["x_updated"](tile(d.back(2), DUO - 1)))
                    for j in range(DUO):
                        mm = pe.matmul(ps[:, 6 + d.par, j * D:(j + 1) * D], uT[d.par][:, j * P:(j + 1) * P], B[:, :],
                                       start=True, stop=True)
                    mm.then_inc(s["out_psum"].sem, 1)
                if d := at(-1):
                    pe.wait_ge(*s["pt_sb"](d))
                    pe.wait_ge(*cr_loaded(d))
                    if d.has(1):
                        pe.wait_ge(*s["u_sb"](d.back(1)))
                    for j in range(DUO):
                        cols = slice(j * P, (j + 1) * P)
                        mm = pe.matmul(ps[:, 5, cols], cr[d.par][:, j], pT[d.par][:, cols], start=True, stop=True)
                    mm.then_inc(s["u_psum"].sem, 1)
                if d := at(0):
                    pe.wait_ge(*s["prob"](d))
                    if d.has(1):
                        pe.wait_ge(*s["pt_sb"](d.back(1)))
                    for j in range(DUO):
                        mm = pe.transpose(ps[:, 4, j * P:(j + 1) * P], prob[d.par][:, j], k.ident)
                    mm.then_inc(s["pt_psum"].sem, 1)
                if d := at(1):
                    pe.wait_ge(*s["q_sb"](d))
                    pe.wait_ge(*cT_loaded(d))
                    if d.has(2):
                        pe.wait_ge(*s["prob"](d.back(2)))
                    for j in range(DUO):
                        for b in range(PAIR):
                            cols = slice(b * SEQ, (b + 1) * SEQ)
                            mm = pe.matmul(ps[64 * b:64 * b + 64, 2 + d.par, j * SEQ:(j + 1) * SEQ],
                                           qT[d.par][:, j * P + b * SEQ:j * P + (b + 1) * SEQ],
                                           cT[d.par][:, j, cols], start=True, stop=True)
                    mm.then_inc(s["s_psum"].sem, 1)
                if d := at(2):
                    pe.wait_ge(*s["xT_sb"](d))
                    if d.has(1):
                        pe.wait_ge(*s["q_sb"](d.back(1)))
                    pe.matmul(ps[:, 1, 0:DUO * P], A[:, :], xT[d.par], start=True, stop=True)\
                        .then_inc(s["q_psum"].sem, 1)
                if d := at(3):
                    pe.wait_ge(*f["xhat_ready"](tile(d, DUO - 1)))
                    if d.has(1):
                        pe.wait_ge(*s["xT_sb"](d.back(1)))
                    for j in range(DUO):
                        mm = pe.transpose(ps[:, 0, j * P:(j + 1) * P], k.xh[:, DUO * d.par + j, :], k.ident)
                    mm.then_inc(f["xT_psum"].sem, 1)
            steps(pe, N, 3, 2, body)

        def vector(dve):
            def body(at):
                if d := at(4):
                    for j in range(DUO):
                        dve.bn_stats(k.st[:, DUO * d.par + j, 0, :], k.x[:, tile(d, j).idx, :])\
                            .then_inc(f["stats"].sem, 1)
                if d := at(-1):
                    dve.wait_ge(*s["u_psum"](d))
                    dve.tensor_copy(uT[d.par], ps[:, 5, 0:DUO * P]).then_inc(s["u_sb"].sem, 1)
                if d := at(4):
                    dve.wait_ge(*f["stats"](tile(d, DUO - 1)))
                    k.hold(dve)
                    for j in range(DUO):
                        sl = DUO * d.par + j
                        dve.bn_aggr(k.mv[:, sl, 0, :], k.st[:, sl, 0, :]).then_inc(f["aggr"].sem, 1)
                if d := at(1):
                    dve.wait_ge(*s["s_psum"](d))
                    src = ps[:, 2 + d.par, 0:DUO * SEQ].rearrange("p (j n) -> p j n", j=DUO)
                    if masked:
                        dve.tensor_tensor(sm[d.par], src, k.konst[:, C_CAUSAL:C_CAUSAL + SEQ].unsqueeze(1)
                                          .broadcast_to([P, DUO, SEQ]), ALU.mult).then_inc(s["masked"].sem, 1)
                        dve.wait_ge(*s["masked"](d))
                        src = sm[d.par]
                    dve.tensor_reduce(mx[d.par], src, AX.X, ALU.max).then_inc(s["smax"].sem, 1)
                if d := at(1):
                    dve.wait_ge(*s["smax"](d))
                    dve.tensor_scalar(nb[d.par], mx[d.par], -SCALE, None, ALU.mult).then_inc(s["nb"].sem, 1)
                if d := at(-2):
                    dve.wait_ge(*s["out_psum"](d))
                    if biased:
                        dve.wait_ge(*s["biased"](d))
                    for j in range(DUO):
                        x = k.x[:, tile(d, j).idx, :]
                        dve.scalar_tensor_tensor(out=x, in0=ps[:, 6 + d.par, j * D:(j + 1) * D],
                                                 scalar=rec[d.par][:, j:j + 1], in1=xb[d.par][:, j] if biased else x,
                                                 op0=ALU.mult, op1=ALU.add).then_inc(f["x_updated"].sem, 1)
                if d := at(4):
                    if d.has(2):
                        dve.wait_ge(*f["xT_psum"](d.back(2)))
                    for j in range(DUO):
                        tile_xhat(k, f, dve, tile(d, j), DUO * d.par + j)
                if d := at(0):
                    dve.wait_ge(*s["prob"](d))
                    if d.has(2):
                        dve.wait_ge(*f["x_updated"](tile(d.back(2), DUO - 1)))
                        k.hold(dve)
                    dve.reciprocal(rec[d.par], rs[d.par]).then_inc(s["recip"].sem, 1)
            steps(dve, N, 4, 2, body)

        def scalar(act):
            act.wait_ge(preset, 2)

            def body(at):
                if d := at(0):
                    act.wait_ge(*s["pt_psum"](d))
                    act.activation(pT[d.par], ps[:, 4, 0:DUO * P], ACT.Copy).then_inc(s["pt_sb"].sem, 1)
                if d := at(1):
                    act.wait_ge(*s["nb"](d))
                    for j in range(DUO):
                        for b in range(PAIR):
                            rows = slice(64 * b, 64 * b + 64)
                            src = sm[d.par][rows, j] if masked else ps[rows, 2 + d.par, j * SEQ:(j + 1) * SEQ]
                            act.activation(prob[d.par][rows, j, b * SEQ:(b + 1) * SEQ], src, ACT.Exp, scale=SCALE,
                                           bias=nb[d.par][rows, j:j + 1], accum_out=rs[d.par][rows, j:j + 1])\
                                .then_inc(s["prob"].sem, 1)
                if d := at(2):
                    act.wait_ge(*s["q_psum"](d))
                    if biased:
                        act.activation(qT[d.par], ps[:, 1, 0:DUO * P], ACT.Identity, bias=k.bqk[:, :])\
                            .then_inc(s["q_sb"].sem, 1)
                    else:
                        act.activation(qT[d.par], ps[:, 1, 0:DUO * P], ACT.Copy).then_inc(s["q_sb"].sem, 1)
                if d := at(3):
                    act.wait_ge(*f["xT_psum"](d))
                    act.activation(xT[d.par], ps[:, 0, 0:DUO * P], ACT.Copy).then_inc(s["xT_sb"].sem, 1)
            steps(act, N, 3, 0, body)

        return dict(sync=sync, gpsimd=gpsimd, tensor=tensor, vector=vector, scalar=scalar)
    return stage


def experts2(k, no):
    ps, G = k.psum, k.T // GROUP
    f = group_signals(k, no)
    k.stage_memory()
    xTg = [k.take(GCOLS) for _ in range(2)]
    hT = [v.rearrange("p (c n) -> p c n", c=CHUNKS2) for v in (k.take(CHUNKS2 * GCOLS) for _ in range(2))]
    small = lambda: k.take(GROUP * EXPERTS).rearrange("p (j e) -> p j e", j=GROUP)
    score, shifted, expd, hits = small(), small(), small(), small()
    route = Route(k)
    smax, ssum, srec = k.take(GROUP), k.take(GROUP), k.take(GROUP)
    coef, coefT = small(), k.take(GCOLS)
    s = k.sigs(G, dict(
        l_psum=1, score=1, smax=1, shifted=1, expd=1, ssum=1, srec=1, routing_prob=1, hits=1, coef=1, ct_psum=1, ct_sb=1,
        h_psum=CHUNKS2, h_sb=CHUNKS2, y_psum=GROUP, acc=GROUP * EXPERTS))
    d_front, p_front, t_front, a_front = group_front(k, f, xTg, 0)
    wide = [P, GROUP, EXPERTS]

    def gpsimd(pool):
        steps(pool, G, 1, 0, lambda at: at(1) and p_front(pool, at(1)))

    def tensor(pe):
        def hidden(g, c):
            if c >= 2:
                pe.wait_ge(*s["h_sb"](g, c - 1))
            elif g.has(1):
                pe.wait_ge(*s["h_sb"](g.back(1), CHUNKS2 - 1 + c))
            w = k.w1s[:, c, 0:P] if c < EXPERTS else k.w1tail[:, c - EXPERTS, :]
            pe.matmul(ps[:, 2 + c % 2, :], w, xTg[g.par], start=True, stop=True).then_inc(s["h_psum"].sem, 1)

        def outputs(g, j):
            bank, cols = 4 + 2 * (j % 2), slice(j * P, (j + 1) * P)
            t = sub(g, j)
            if t.has(2):
                pe.wait_ge(*f["x_updated"](t.back(2)))
            for e in range(EXPERTS):
                dst = ps[:, bank + e % 2, (e // 2) * D:(e // 2 + 1) * D]
                rows = slice(64 * (e % 2), 64 * (e % 2) + 64)
                pe.matmul(dst, hT[g.par][:, e, cols], k.w2a[:, e, :], start=True, stop=False)
                mm = pe.matmul(dst, hT[g.par][rows, EXPERTS + e // 2, cols], k.w2b[rows, e // 2, :],
                               start=False, stop=True)
            mm.then_inc(s["y_psum"].sem, 1)

        def body(at):
            g, nxt = at(0), at(1)
            if g:
                pe.wait_ge(*s["h_sb"](g))
                outputs(g, 0)
            if nxt:
                t_front(pe, nxt)
            if g:
                outputs(g, 1)
            if nxt:
                pe.wait_ge(*f["xT_sb"](nxt))
                if g:
                    pe.wait_ge(*s["b2_sb"](g))
                for j in range(GROUP):
                    mm = pe.matmul(ps[:, 1, j * EXPERTS:(j + 1) * EXPERTS], xTg[nxt.par][:, j * P:(j + 1) * P],
                                   k.wr2[:, :], start=True, stop=True)
                mm.then_inc(s["l_psum"].sem, 1)
                for c in range(0, 4):
                    hidden(nxt, c)
            if g:
                outputs(g, 2)
            if nxt:
                for c in range(4, 8):
                    hidden(nxt, c)
            if g:
                outputs(g, 3)
            if nxt:
                for c in range(8, 12):
                    hidden(nxt, c)
                pe.wait_ge(*s["coef"](nxt))
                for j in range(GROUP):
                    mm = pe.transpose(ps[0:EXPERTS, 1, j * P:(j + 1) * P], coef[:, j], k.ident)
                mm.then_inc(s["ct_psum"].sem, 1)
                pe.wait_ge(*s["ct_sb"](nxt))
                for j in range(GROUP):
                    mm = pe.matmul(ps[:, 1, j * D:(j + 1) * D], coefT[0:EXPERTS, j * P:(j + 1) * P], k.b2r[:, :],
                                   start=True, stop=True)
                mm.then_inc(s["b2_psum"].sem, 1)
        steps(pe, G, 1, 0, body)

    s["b2_psum"], s["b2_sb"] = k.sig(G, "b2_psum"), k.sig(G, "b2_sb")
    b2sum = [k.take(GCOLS) for _ in range(2)]

    def vector(dve):
        def routing(g):
            dve.wait_ge(*s["l_psum"](g))
            dve.tensor_tensor(score, ps[:, 1, 0:GROUP * EXPERTS].rearrange("p (j e) -> p j e", j=GROUP),
                              k.br2[:, :].unsqueeze(1).broadcast_to(wide), ALU.add).then_inc(s["score"].sem, 1)
            dve.wait_ge(*s["score"](g))
            dve.tensor_reduce(smax, score, AX.X, ALU.max).then_inc(s["smax"].sem, 1)
            dve.wait_ge(*s["smax"](g))
            dve.tensor_tensor(shifted, score, smax.unsqueeze(2).broadcast_to(wide), ALU.subtract)\
                .then_inc(s["shifted"].sem, 1)
            dve.wait_ge(*s["expd"](g))
            dve.tensor_reduce(ssum, expd, AX.X, ALU.add).then_inc(s["ssum"].sem, 1)
            dve.wait_ge(*s["ssum"](g))
            dve.reciprocal(srec, ssum).then_inc(s["srec"].sem, 1)
            dve.wait_ge(*s["srec"](g))
            dve.tensor_tensor(route.score, expd, srec.unsqueeze(2).broadcast_to(wide), ALU.mult)\
                .then_inc(s["routing_prob"].sem, 1)
            dve.wait_ge(*s["routing_prob"](g))
            k.hold(dve)
            route.run(dve, g)
            dve.wait_ge(*route.done(g))
            dve.tensor_tensor(hits, route.hit[0], route.hit[1], ALU.add).then_inc(s["hits"].sem, 1)
            dve.wait_ge(*s["hits"](g))
            dve.scalar_tensor_tensor(out=coef, in0=hits, scalar=k.gates[:, 6:7], in1=route.score,
                                     op0=ALU.mult, op1=ALU.mult).then_inc(s["coef"].sem, 1)

        def combine(g, j):
            t = sub(g, j)
            bank = 4 + 2 * (j % 2)
            x = k.x[:, t.idx, :]
            dve.tensor_tensor(x, x, b2sum[g.par][:, j * D:(j + 1) * D], ALU.add).then_inc(s["acc"].sem, 1)
            dve.wait_ge(*s["y_psum"](g, j + 1))
            for e in range(EXPERTS):
                dve.wait_ge(*s["acc"](g, j * EXPERTS + e + 1))
                dve.scalar_tensor_tensor(out=x, in0=ps[:, bank + e % 2, (e // 2) * D:(e // 2 + 1) * D],
                                         scalar=coefs[:, j, e:e + 1], in1=x, op0=ALU.mult, op1=ALU.add)\
                    .then_inc(s["acc"].sem if e < EXPERTS - 1 else f["x_updated"].sem, 1)

        def body(at):
            g, nxt = at(0), at(1)
            if nxt:
                d_front(dve, nxt)
            if g:
                dve.wait_ge(*s["b2_sb"](g))
                if g.has(1):
                    dve.wait_ge(*f["x_updated"](sub(g.back(1), GROUP - 1)))
                    k.hold(dve)
                dve.tensor_copy(coefs, coef).then_inc(s["coefs"].sem, 1)
                dve.wait_ge(*s["coefs"](g))
                combine(g, 0)
                combine(g, 1)
            if nxt:
                routing(nxt)
            if g:
                combine(g, 2)
                combine(g, 3)
        steps(dve, G, 1, 0, body)

    coefs = small()
    s["coefs"] = k.sig(G, "coefs")

    def scalar(act):
        def body(at):
            if g := at(1):
                a_front(act, g)
                for c in range(4):
                    hidden_out(act, g, c)
                act.wait_ge(*s["shifted"](g))
                act.activation(expd, shifted, ACT.Exp).then_inc(s["expd"].sem, 1)
                for c in range(4, CHUNKS2):
                    hidden_out(act, g, c)
                act.wait_ge(*s["ct_psum"](g))
                act.activation(coefT[0:EXPERTS, :], ps[0:EXPERTS, 1, :], ACT.Copy).then_inc(s["ct_sb"].sem, 1)
                act.wait_ge(*s["b2_psum"](g))
                act.activation(b2sum[g.par], ps[:, 1, :], ACT.Copy).then_inc(s["b2_sb"].sem, 1)
        steps(act, G, 1, 0, body)

    def hidden_out(act, g, c):
        act.wait_ge(*s["h_psum"](g, c + 1))
        act.activation(hT[g.par][:, c, :], ps[:, 2 + c % 2, :], ACT.Gelu, bias=k.b1c[:, c:c + 1])\
            .then_inc(s["h_sb"].sem, 1)

    return dict(gpsimd=gpsimd, tensor=tensor, vector=vector, scalar=scalar)


def quantised3(k, no):
    ps, T, G = k.psum, k.T, k.T // GROUP
    f = k.front(no)
    k.stage_memory()
    W = CHUNKS3 * GCOLS
    half = lambda n: k.take(n // 2).bitcast(I16)
    upq = half(G * W).rearrange("p (g n) -> p g n", g=G)
    xdT = k.take(T * P).rearrange("p (g n) -> p g n", g=G)
    xhs = k.take(T * P).rearrange("p (g n) -> p g n", g=G)
    mark = k.taken
    gq2 = k.arena[:, mark - 2 * T * P:mark - 2 * T * P + G * W // 2].bitcast(I16).rearrange("p (g n) -> p g n", g=G)
    k.taken = mark - T * P
    gq, sig, sigq = half(W), k.take(W), k.take(W // 2).bitcast(U16)
    gs = [k.take(W) for _ in range(2)]
    k.taken = max(mark - 2 * T * P + G * W // 2, mark - T * P)
    gin, prod = [k.take(W) for _ in range(2)], k.take(W)
    k.taken = mark - 2 * T * P + G * W // 2
    oprod, oq, of = k.take(W), half(W), k.take(W)
    sb = k.sb
    xq, xd = sb("xq", [P, GCOLS], I16), sb("xd", [P, GCOLS])
    xmax, ugmax = sb("xmax", [P, T]), sb("ugmax", [P, 2, G, CHUNKS3])
    gsmax, omax = sb("gsmax", [P, G]), sb("omax", [P, G])
    local, wide = sb("local_max", [P, 2]), sb("wide_max", [2, P])
    top = sb("top_max", [2, 1])
    scale = {n: sb(f"scale_{n}", [P, w]) for n, w in dict(x=1, ug=2, gs=1, o=1).items()}
    inv = {n: sb(f"inv_{n}", [P, w]) for n, w in dict(x=1, ug=2, gs=1, o=1).items()}
    sprod, down = sb("scale_product", [P, 1]), sb("scale_down", [P, 1])
    gs_dram = k.nc.dram_tensor("gated_scratch", [G, P, W], F32, kind="Internal").ap()
    gs_stored, gs_loaded = k.transfers(G, "gated_stored"), k.transfers(G, "gated_loaded")
    s = k.sigs(G, dict(
        xmax=1, xq=1, xd=1, t_psum=1, xdT=1, p_psum=2 * CHUNKS3, pmax=2 * CHUNKS3, c_psum=2 * CHUNKS3, upq=CHUNKS3,
        gq=CHUNKS3, sig=1, sigq=1, gs=1, gsmax=1, gq2=1, prod=1, omax=1, oprod=1, oq=1, of=1, y_psum=1))
    SCALES = ("x", "ug", "gs", "o")
    found, spread = k.sem("Q3_scale_found"), k.sem("Q3_scale_spread")
    final = k.sem("Q3_final_scales")

    def scale_vector(dve, name, columns, factor):
        n, w = SCALES.index(name), scale[name].shape[1]
        dve.tensor_reduce(local[:, 0:w], columns, AX.X, ALU.max).then_inc(found, 1)
        dve.wait_ge(spread, 2 * n + 1)
        dve.tensor_reduce(top[0:w, :], ps[0:w, 7, 0:P], AX.X, ALU.max).then_inc(found, 1)
        dve.wait_ge(found, 5 * n + 2)
        dve.tensor_scalar(wide[0:w, :], k.konst[0:w, C_ONES:C_ONES + P], top[0:w, :], None, ALU.mult)\
            .then_inc(found, 1)
        dve.wait_ge(spread, 2 * n + 2)
        dve.tensor_scalar(scale[name][:, :], ps[:, 7, P:P + w], factor / QMAX_A, 1e-12, ALU.mult, ALU.max)\
            .then_inc(found, 1)
        dve.wait_ge(found, 5 * n + 4)
        dve.reciprocal(inv[name][:, :], scale[name][:, :]).then_inc(found, 1)
        dve.wait_ge(found, 5 * n + 5)

    def scale_tensor(pe, name):
        n, w = SCALES.index(name), scale[name].shape[1]
        pe.wait_ge(found, 5 * n + 1)
        pe.transpose(ps[0:w, 7, 0:P], local[:, 0:w], k.ident).then_inc(spread, 1)
        pe.wait_ge(found, 5 * n + 3)
        pe.matmul(ps[:, 7, P:P + w], wide[0:w, :], k.konst[0:w, C_IDENT:C_IDENT + w], start=True, stop=True)\
            .then_inc(spread, 1)

    def scale_known(eng, name):
        eng.wait_ge(found, 5 * SCALES.index(name) + 5)

    def sync(sp):
        def store(at):
            if g := at(0):
                sp.wait_ge(*s["gs"](g))
                sp.dma_start(gs_dram[g.idx], gs[g.par]).then_inc(gs_stored.at(g), 16)
        steps(sp, G, 0, 0, store)
        gs_stored.wait_all(sp, G)
        sp.wait_ge(*s["gsmax"].all(G))

        def load(at):
            if g := at(0):
                if g.has(2):
                    sp.wait_ge(*s["gq2"](g.back(2)))
                sp.dma_start(gin[g.par], gs_dram[g.idx]).then_inc(gs_loaded.at(g), 16)
        steps(sp, G, 0, 2, load)

    def gpsimd(pool):
        steps(pool, T, 1, 0, lambda at: at(1) and tile_rstd(k, f, pool, at(1), at(1).par, False))

    def project(pe, g, psum_signal, freed):
        for n, w in enumerate((k.wup3, k.wgt3)):
            for c in range(CHUNKS3):
                if g.has(1):
                    freed(g.back(1), n, c)
                pe.matmul(ps[:, 1 + CHUNKS3 * n + c, :], w[:, c, :], xdT[:, g.idx, :], start=True, stop=True)\
                    .then_inc(psum_signal.sem, 1)

    def tensor(pe):
        scale_tensor(pe, "x")

        def first(at):
            if g := at(1):
                pe.wait_ge(*s["xd"](g))
                if g.has(1):
                    pe.wait_ge(*s["xdT"](g.back(1)))
                for j in range(GROUP):
                    mm = pe.transpose(ps[:, 0, j * P:(j + 1) * P], xd[:, j * P:(j + 1) * P], k.ident)
                mm.then_inc(s["t_psum"].sem, 1)
            if g := at(0):
                pe.wait_ge(*s["xdT"](g))
                project(pe, g, s["p_psum"], lambda b, n, c: pe.wait_ge(*s["pmax"](b, CHUNKS3 * n + c + 1)))
        steps(pe, G, 1, 0, first)
        scale_tensor(pe, "ug")

        def second(at):
            if g := at(0):
                project(pe, g, s["c_psum"],
                        lambda b, n, c: pe.wait_ge(*s["gq" if n else "upq"](b, c + 1)))
        pe.wait_ge(*s["pmax"].all(G))
        steps(pe, G, 0, 0, second)
        scale_tensor(pe, "gs")
        scale_tensor(pe, "o")

        def last(at):
            if g := at(0):
                pe.wait_ge(*s["of"](g))
                if g.has(2):
                    pe.wait_ge(*f["x_updated"](sub(g.back(2), GROUP - 1)))
                for j in range(GROUP):
                    for c in range(CHUNKS3):
                        mm = pe.matmul(ps[:, g.par, j * P:(j + 1) * P],
                                       of[:, c * GCOLS + j * P:c * GCOLS + (j + 1) * P], k.wdn3[:, c, :],
                                       start=c == 0, stop=c == CHUNKS3 - 1)
                mm.then_inc(s["y_psum"].sem, 1)
        steps(pe, G, 0, 0, last)

    def vector(dve):
        xflat = xhs.rearrange("p g (j n) -> p (g j) n", j=GROUP)

        def normalise(at):
            if t := at(1):
                tile_stats(k, f, dve, t, t.par)
            if t := at(0):
                tile_xhat(k, f, dve, t, t.par, out=xflat[:, t.idx, :])
                dve.wait_ge(*f["xhat_ready"](t))
                k.hold(dve)
                dve.tensor_reduce(xmax[:, bass.ds(t.idx, 1)], xflat[:, t.idx, :], AX.X, ALU.max,
                                  apply_absolute_value=True).then_inc(s["xmax"].sem, 1)
        steps(dve, T, 1, 0, normalise)
        dve.wait_ge(*s["xmax"].all(T))
        scale_vector(dve, "x", xmax[:, :], 1.0)

        def first(at):
            if g := at(1):
                if g.has(1):
                    dve.wait_ge(*s["xd"](g.back(1)))
                dve.tensor_scalar(xq[:, :], xhs[:, g.idx, :], inv["x"][:, :], None, ALU.mult).then_inc(s["xq"].sem, 1)
                dve.wait_ge(*s["xq"](g))
                if g.has(1):
                    dve.wait_ge(*s["t_psum"](g.back(1)))
                dve.tensor_scalar(xd[:, :], xq[:, :], scale["x"][:, :], None, ALU.mult).then_inc(s["xd"].sem, 1)
            if g := at(0):
                for n in range(2 * CHUNKS3):
                    dve.wait_ge(*s["p_psum"](g, n + 1))
                    k.hold(dve)
                    dve.tensor_reduce(ugmax[:, n // CHUNKS3, g.idx, n % CHUNKS3:n % CHUNKS3 + 1], ps[:, 1 + n, :],
                                      AX.X, ALU.max, apply_absolute_value=True).then_inc(s["pmax"].sem, 1)
        steps(dve, G, 1, 0, first)
        dve.wait_ge(*s["pmax"].all(G))
        scale_vector(dve, "ug", ugmax[:, :, :, :].rearrange("p w g c -> p w (g c)"), 1.0)

        def second(at):
            if g := at(0):
                dve.wait_ge(*s["sig"](g))
                dve.tensor_scalar(sigq, sig, QSIG, QSIG - 1.0, ALU.mult, ALU.min).then_inc(s["sigq"].sem, 1)
                dve.wait_ge(*s["sigq"](g))
                if g.has(2):
                    dve.wait_ge(*gs_stored(g.back(2)))
                dve.scalar_tensor_tensor(out=gs[g.par], in0=gq, scalar=scale["ug"][:, 1:2], in1=sigq, op0=ALU.mult,
                                         op1=ALU.mult).then_inc(s["gs"].sem, 1)
                dve.wait_ge(*s["gs"](g))
                k.hold(dve)
                dve.tensor_reduce(gsmax[:, bass.ds(g.idx, 1)], gs[g.par], AX.X, ALU.max, apply_absolute_value=True)\
                    .then_inc(s["gsmax"].sem, 1)
        steps(dve, G, 0, 0, second)
        dve.wait_ge(*s["gsmax"].all(G))
        scale_vector(dve, "gs", gsmax[:, :], 1.0)
        dve.tensor_scalar(sprod[:, :], scale["gs"][:, :], scale["ug"][:, 0:1], 1.0 / QSIG, ALU.mult, ALU.mult)\
            .then_inc(final, 1)
        dve.wait_ge(final, 1)

        def product(g, out, signal):
            dve.scalar_tensor_tensor(out=out, in0=gq2[:, g.idx, :], scalar=sprod[:, :], in1=upq[:, g.idx, :],
                                     op0=ALU.mult, op1=ALU.mult).then_inc(signal.sem, 1)

        def third(at):
            if g := at(0):
                dve.wait_ge(*s["gq2"](g))
                if g.has(1):
                    dve.wait_ge(*s["omax"](g.back(1)))
                product(g, prod, s["prod"])
                dve.wait_ge(*s["prod"](g))
                k.hold(dve)
                dve.tensor_reduce(omax[:, bass.ds(g.idx, 1)], prod, AX.X, ALU.max, apply_absolute_value=True)\
                    .then_inc(s["omax"].sem, 1)
        steps(dve, G, 0, 0, third)
        dve.wait_ge(*s["omax"].all(G))
        scale_vector(dve, "o", omax[:, :], 1.0)
        dve.tensor_scalar(down[:, :], scale["o"][:, :], k.gates[:, 7:8], None, ALU.mult).then_inc(final, 1)
        dve.wait_ge(final, 2)

        def last(at):
            if g := at(1):
                if g.has(1):
                    dve.wait_ge(*s["oq"](g.back(1)))
                product(g, oprod, s["oprod"])
            if g := at(0):
                dve.wait_ge(*s["y_psum"](g))
                for j in range(GROUP):
                    x = k.x[:, sub(g, j).idx, :]
                    dve.scalar_tensor_tensor(out=x, in0=ps[:, g.par, j * P:(j + 1) * P], scalar=down[:, :], in1=x,
                                             op0=ALU.mult, op1=ALU.add).then_inc(f["x_updated"].sem, 1)
        steps(dve, G, 1, 0, last)

    def scalar(act):
        scale_known(act, "x")

        def first(at):
            if g := at(1):
                act.wait_ge(*s["t_psum"](g))
                k.hold(act)
                act.activation(xdT[:, g.idx, :], ps[:, 0, :], ACT.Copy).then_inc(s["xdT"].sem, 1)
        steps(act, G, 1, 0, first)
        scale_known(act, "ug")

        def second(at):
            if g := at(0):
                for c in range(CHUNKS3):
                    act.wait_ge(*s["c_psum"](g, c + 1))
                    k.hold(act)
                    act.activation(upq[:, g.idx, c * GCOLS:(c + 1) * GCOLS], ps[:, 1 + c, :], ACT.Copy,
                                   scale=inv["ug"][:, 0:1]).then_inc(s["upq"].sem, 1)
                if g.has(1):
                    act.wait_ge(*s["gs"](g.back(1)))
                for c in range(CHUNKS3):
                    act.wait_ge(*s["c_psum"](g, CHUNKS3 + c + 1))
                    act.activation(gq[:, c * GCOLS:(c + 1) * GCOLS], ps[:, 1 + CHUNKS3 + c, :], ACT.Copy,
                                   scale=inv["ug"][:, 1:2]).then_inc(s["gq"].sem, 1)
                act.wait_ge(*s["gq"](g))
                act.activation(sig, gq, ACT.Sigmoid, scale=scale["ug"][:, 1:2]).then_inc(s["sig"].sem, 1)
        steps(act, G, 0, 0, second)
        scale_known(act, "gs")
        act.wait_ge(gs_stored.sems[0], G // 2 * 16)
        act.wait_ge(gs_stored.sems[1], G // 2 * 16)

        def third(at):
            if g := at(0):
                act.wait_ge(*gs_loaded(g))
                k.hold(act)
                act.activation(gq2[:, g.idx, :], gin[g.par], ACT.Copy, scale=inv["gs"][:, :])\
                    .then_inc(s["gq2"].sem, 1)
        steps(act, G, 0, 0, third)
        scale_known(act, "o")

        def last(at):
            if g := at(0):
                act.wait_ge(*s["oprod"](g))
                if g.has(1):
                    act.wait_ge(*s["of"](g.back(1)))
                act.activation(oq, oprod, ACT.Copy, scale=inv["o"][:, :]).then_inc(s["oq"].sem, 1)
                act.wait_ge(*s["oq"](g))
                if g.has(1):
                    act.wait_ge(*s["y_psum"](g.back(1)))
                act.activation(of, oq, ACT.Copy).then_inc(s["of"].sem, 1)
        steps(act, G, 0, 0, last)

    return dict(sync=sync, gpsimd=gpsimd, tensor=tensor, vector=vector, scalar=scalar)


STAGES = [attention0, experts0, attention1, spiking1, context_attention(2), experts2, context_attention(3), quantised3]


def flamingo(nc, args, out, last=8):
    with ExitStack() as ctx:
        k = Kit(nc, ctx, args, out)
        parts = [prepare(k)]
        for no, stage in enumerate(STAGES[:last]):
            parts.append(stage(k, no))
        stored = k.sem("x_stored")
        ov = out.rearrange("(t b) s d -> (b s) t d", b=PAIR)
        QUARTERS = 4
        block = ctx.enter_context(nc.Block())

        def run(engine, name):
            for no, part in enumerate(parts):
                if name in part:
                    if no > 1:
                        stage_start(engine, k, no - 1)
                    part[name](engine)

        @block.sync
        def _(sp):
            run(sp, "sync")
            updated = k.front(last - 1)["x_updated"]
            for j in range(QUARTERS):
                n = k.T // QUARTERS
                sp.wait_ge(*updated.all((j + 1) * n))
                sp.dma_start(ov[:, j * n:(j + 1) * n, :], k.x[:, j * n:(j + 1) * n, :]).then_inc(stored, 16)
            sp.wait_ge(stored, 16 * QUARTERS)
            k.ctxT_stored.wait_all(sp, k.T)
            k.z1T_stored.wait_all(sp, k.T)

        @block.gpsimd
        def _(pool):
            run(pool, "gpsimd")

        @block.tensor
        def _(pe):
            run(pe, "tensor")

        @block.vector
        def _(dve):
            run(dve, "vector")

        @block.scalar
        def _(act):
            run(act, "scalar")


def shape_constants():
    import numpy as np
    c = np.zeros((P, C_END), np.float32)
    c[:, C_IDENT:C_IDENT + P] = np.eye(P)
    freq = (np.float32(1.0) / np.float32(10000.0) ** (np.arange(0, HD0, 2, dtype=np.float32) / np.float32(HD0)))
    theta = np.arange(SEQ, dtype=np.float32)[:, None] * freq.astype(np.float32)[None, :]
    angles = np.concatenate([theta, theta] * 2, axis=1).T
    c[:, C_COS:C_COS + SEQ], c[:, C_SIN:C_SIN + SEQ] = np.cos(angles), np.sin(angles)
    c[:, C_IOTA:C_IOTA + EXPERTS] = np.arange(EXPERTS)
    rows = np.arange(P)
    c[:, C_MASK8:C_MASK8 + 8] = (rows[:, None] // HD1) % 8 == np.arange(8)
    c[:, C_CAUSAL:C_CAUSAL + SEQ] = np.arange(SEQ) <= rows[:, None] % SEQ
    c[:, C_MHALF:C_MHALF + 4] = -0.5
    c[:, C_ONES:C_ONES + P] = 1.0
    return c


def kernel(**inputs):
    import numpy as np
    import concourse.bacc as bacc
    from concourse.bass_utils import run_bass_kernel_spmd

    nc = bacc.Bacc("TRN2", target_bir_lowering=False, num_devices=1)
    arrays, args = {}, {}
    for name, a in list(inputs.items()) + [("shape_constants", shape_constants())]:
        a = np.ascontiguousarray(a)
        arrays[f"in_{name}"] = a
        args[name] = nc.dram_tensor(f"in_{name}", a.shape, mybir.dt.from_np(a.dtype), kind="ExternalInput").ap()
    out = nc.dram_tensor("out_x", inputs["x"].shape, F32, kind="ExternalOutput").ap()
    flamingo(nc, args, out)
    r = run_bass_kernel_spmd(nc, [arrays], core_ids=[0])
    return r.results[0]["out_x"]
```

```python
from contextlib import ExitStack

import concourse.bass as bass
from concourse import mybir

ALU = mybir.AluOpType
ACT = mybir.ActivationFunctionType
AX = mybir.AxisListType
F32 = mybir.dt.float32
I16 = mybir.dt.int16
U16 = mybir.dt.uint16
U32 = mybir.dt.uint32

P = 128
SEQ = 64
D = 128
PAIR = P // SEQ
EPS = 1e-5
EXPERTS = 8
GROUP = 4
GCOLS = GROUP * P
DUO = 2
H0, HD0 = 8, 64
INNER = H0 * HD0
HPAIRS = H0 // 2
VW = HD0 + 1
H1, HD1 = 16, 8
FF1 = 512
SPIKE_STEPS, BETA = 5, 0.9
HID2 = 192
CHUNKS2 = EXPERTS * HID2 // P
FF3 = 384
CHUNKS3 = FF3 // P
BLOCK = 32
QMAX_A, QMAX_W, QSIG = 32767.0, 7.0, 65536.0

C_IDENT, C_COS, C_SIN, C_IOTA, C_MASK8, C_CAUSAL, C_MHALF, C_ONES = 0, 128, 192, 256, 264, 272, 336, 340
C_END = C_ONES + 128


class Tile:

    def __init__(self, idx, par):
        self.idx, self.par = idx, par

    def has(self, k):
        return not isinstance(self.idx, int) or self.idx >= k

    def back(self, k):
        return Tile(self.idx - k, (self.par - k) % 2)


class Signal:

    def __init__(self, sem, per=1, base=0):
        self.sem, self.per, self.base = sem, per, base

    def __call__(self, t, k=None):
        return self.sem, self.base + self.per * t.idx + (self.per if k is None else k)

    def all(self, n):
        return self.sem, self.base + self.per * n


class Transfers:

    def __init__(self, even, odd, base):
        self.sems, self.base = (even, odd), base

    def at(self, t):
        return self.sems[t.par]

    def __call__(self, t):
        return self.sems[t.par], self.base + (t.idx - t.par) * 8 + 16

    def wait_all(self, eng, n):
        for sem in self.sems:
            eng.wait_ge(sem, self.base + n // 2 * 16)


def steps(eng, n, lead, lag, body):
    def fixed(s):
        body(lambda k: Tile(s + k, (s + k) % 2) if 0 <= s + k < n else None)

    first = (lag + 3) // 2 * 2
    end = first + (n - lead - first) // 2 * 2
    if end - first < 4:
        for s in range(-lead, n + lag):
            fixed(s)
        return
    for s in range(-lead, first):
        fixed(s)
    with eng.Fori(first // 2, end // 2) as i:
        for u in range(2):
            body(lambda k, u=u: Tile(i * 2 + (u + k), (u + k) % 2))
    for s in range(end, n + lag):
        fixed(s)


class Kit:

    def __init__(self, nc, ctx, args, out):
        self.nc, self.ctx, self.a, self.out = nc, ctx, args, out
        self.T = args["x"].shape[0] // PAIR
        self.psum = ctx.enter_context(nc.psum_tensor("banks", [P, 8, 512], F32))
        self.x = self.sb("x_tiles", [P, self.T, D])
        self.konst = self.sb("konst", [P, C_END])
        self.arena = self.sb("arena", [P, 30720])
        self.taken, self.fronts, self.sems, self.counted = 0, {}, {}, {}
        self.ident = self.konst[:, C_IDENT:C_IDENT + P]
        self.st = self.sb("bn_parts", [P, GROUP, 2, 6])
        self.mv = self.sb("mean_var", [P, GROUP, 2, 2])
        self.ve = self.sb("var_eps", [P, GROUP, 2])
        self.rstd = self.sb("rstd", [P, GROUP, 2])
        self.xh = self.sb("xhat", [P, GROUP, D])
        self.gate_pass = self.sem("form_has_no_register_wait")
        names = ("stats", "aggr", "vareps", "rstd_ready", "xhat_ready", "x_updated")
        self.shared = {n: self.sem(n) for n in names}
        self.ctxT_dram = nc.dram_tensor("ctxT_scratch", [self.T, P, P], F32, kind="Internal").ap()
        self.z1T_dram = nc.dram_tensor("z1T_scratch", [self.T, P, P], F32, kind="Internal").ap()
        self.ctxT_stored, self.z1T_stored = (
            self.transfers(self.T, n) for n in ("ctxT_stored", "z1T_stored"))

    def sb(self, name, shape, dt=F32):
        return self.ctx.enter_context(self.nc.sbuf_tensor(name, shape, dt))

    def sem(self, name):
        return self.ctx.enter_context(self.nc.semaphore(name))

    def shared_sem(self, name):
        if name not in self.sems:
            self.sems[name], self.counted[name] = self.sem(name), 0
        return self.sems[name], self.counted[name]

    def sig(self, n, name, per=1):
        sem, base = self.shared_sem(name)
        self.counted[name] = base + per * n
        return Signal(sem, per, base)

    def sigs(self, n, names):
        return {name: self.sig(n, name, per) for name, per in names.items()}

    def transfers(self, n, name):
        (even, base), (odd, _) = (self.shared_sem(name + side) for side in ("_even", "_odd"))
        for side in ("_even", "_odd"):
            self.counted[name + side] = base + n // 2 * 16
        return Transfers(even, odd, base)

    def stage_memory(self):
        self.taken = 0

    def take(self, cols):
        a = self.arena[:, self.taken:self.taken + cols]
        self.taken += cols
        assert self.taken <= 30720, self.taken
        return a

    def front(self, no):
        if no not in self.fronts:
            self.fronts[no] = {n: Signal(s, 1, no * self.T) for n, s in self.shared.items()}
        return self.fronts[no]

    def hold(self, eng):
        eng.sem_inc(self.gate_pass, 1)


def tile_stats(k, f, dve, t, slot):
    dve.bn_stats(k.st[:, slot, 0, :], k.x[:, t.idx, :]).then_inc(f["stats"].sem, 1)
    dve.wait_ge(*f["stats"](t))
    k.hold(dve)
    dve.bn_aggr(k.mv[:, slot, 0, :], k.st[:, slot, 0, :]).then_inc(f["aggr"].sem, 1)


def tile_rstd(k, f, pool, t, slot, twice):
    pool.wait_ge(*f["aggr"](t))
    k.hold(pool)
    pool.tensor_scalar(k.ve[:, slot, 0:1], k.mv[:, slot, 0, 1:2], 1.0 + EPS if twice else 1.0,
                       EPS * EPS if twice else EPS, ALU.mult, ALU.add).then_inc(f["vareps"].sem, 1)
    pool.wait_ge(*f["vareps"](t))
    pool.tensor_tensor(k.rstd[:, slot, 0:1], k.ve[:, slot, 0:1], k.konst[:, C_MHALF:C_MHALF + 1],
                       ALU.pow).then_inc(f["rstd_ready"].sem, 1)


def tile_xhat(k, f, dve, t, slot, out=None):
    dve.wait_ge(*f["rstd_ready"](t))
    dve.tensor_scalar(k.xh[:, slot, :] if out is None else out, k.x[:, t.idx, :], k.mv[:, slot, 0, 0:1],
                      k.rstd[:, slot, 0:1], ALU.subtract, ALU.mult).then_inc(f["xhat_ready"].sem, 1)


def stage_start(eng, k, no):
    if no:
        eng.wait_ge(*k.front(no)["x_updated"].all(0))
    if no == 1:
        k.ctxT_stored.wait_all(eng, k.T)
        k.z1T_stored.wait_all(eng, k.T)


def prepare(k):
    nc, a, ps = k.nc, k.a, k.psum
    sb = k.sb
    raw = k.take
    k.gates, k.spike_gate = sb("gates", [P, 8]), sb("spike_gate", [P, 1])
    gates_raw = raw(8)
    k.wq0, k.wk0, k.wv0, k.wr0 = (sb(n, [P, INNER]) for n in ("wq0", "wk0", "wv0", "wk0_rotated"))
    k.wo0 = sb("wo0", [P, HPAIRS, D])
    k.aff = sb("affine_columns", [P, 8])
    k.we0, k.wg0 = sb("we0", [P, EXPERTS, D]), sb("wg0", [P, EXPERTS])
    gw_raw = raw(D)
    k.w1a = sb("w1a", [P, 4, D])
    k.wfc1, k.wpr1 = sb("wfc1", [P, FF1]), sb("wpr1", [P, 4, D])
    fc_raw, pr_raw = raw(4 * D), raw(FF1)
    w2_raw, w3_raw = raw(4 * D), raw(3 * D)
    woT = raw(D)
    bcol = raw(2)
    bo_row = raw(D)
    bv_wide, b1_raw = raw(D), raw(P)
    k.A = [sb("A2", [P, D]), sb("A3", [P, D])]
    k.B = [sb("B2", [P, D]), sb("B3", [P, D])]
    k.bqk, k.bout = sb("bqk", [P, 1]), sb("bout", [P, D])
    k.wr2, k.br2 = sb("wr2", [P, EXPERTS]), sb("br2", [P, EXPERTS])
    k.w1s, k.w1tail = sb("w1s", [P, EXPERTS, P]), sb("w1tail", [P, EXPERTS // 2, P])
    k.w2a, k.w2b = sb("w2a", [P, EXPERTS, D]), sb("w2b", [P, EXPERTS // 2, D])
    k.b1c, k.b2r = sb("b1c", [P, CHUNKS2]), sb("b2r", [EXPERTS, D])
    q_raw = raw(3 * FF3).rearrange("p (w b i) -> p w b i", w=3, i=BLOCK)
    q_max, q_inv = raw(36).rearrange("p (w b) -> p w b", w=3), raw(36).rearrange("p (w b) -> p w b", w=3)
    q_int = raw(3 * FF3 // 2).bitcast(I16).rearrange("p (w b i) -> p w b i", w=3, i=BLOCK)
    q_clip = raw(3 * FF3 // 2).bitcast(I16).rearrange("p (w b i) -> p w b i", w=3, i=BLOCK)
    q_deq = raw(3 * FF3).rearrange("p (w b i) -> p w b i", w=3, i=BLOCK)
    k.wup3, k.wgt3, k.wdn3 = (sb(n, [P, CHUNKS3, D]) for n in ("wup3", "wgt3", "wdn3"))

    loaded, x_loaded = k.sem("weights_loaded"), k.sem("x_loaded")
    gates_ready, built, dequant = k.sem("gates_ready"), k.sem("weights_built"), k.sem("dequantised")
    turned, turned_sb, folded, folded_sb = (k.sem(n) for n in ("turned", "turned_sb", "folded", "folded_sb"))
    wkv = a["L0_xattn_Wkv"]
    loads = [
        (k.konst[:, :], a["shape_constants"]),
        (gates_raw[:, 0:4], a["g_xattn"].partition_broadcast(P)),
        (gates_raw[:, 4:8], a["g_ffn"].partition_broadcast(P)),
        (k.wq0[:, :], a["L0_xattn_Wq"]), (k.wk0[:, :], wkv[:, 0:INNER]), (k.wv0[:, :], wkv[:, INNER:2 * INNER]),
        (k.wo0[:, :, :], a["L0_xattn_Wo"].rearrange("(c p) d -> p c d", p=P)),
        (k.we0[:, :, :], a["L0_ffn_We"].rearrange("e d m -> d e m")),
        (gw_raw[0:EXPERTS, :], a["L0_ffn_gate_w"]),
        (fc_raw.rearrange("p (c d) -> p c d", c=4), a["L1_ffn_W_fc"].rearrange("(c p) d -> p c d", p=P)),
        (pr_raw, a["L1_ffn_W_proj"]),
        (bo_row[0:1, :], a["L2_xattn_bo"].rearrange("(a n) -> a n", a=1)),
        (k.wr2[:, :], a["L2_ffn_Wr"]), (k.br2[:, :], a["L2_ffn_br"].partition_broadcast(P)),
        (k.w1s[:, :, :], a["L2_ffn_W1"][:, :, 0:P].rearrange("e d h -> d e h")),
        (k.w2a[:, :, :], a["L2_ffn_W2"][:, 0:P, :].rearrange("e h d -> h e d")),
        (q_raw[:, 0].rearrange("p (c b) i -> p c (b i)", c=CHUNKS3), a["L3_ffn_w_up"].rearrange("(c p) d -> p c d", p=P)),
        (q_raw[:, 1].rearrange("p (c b) i -> p c (b i)", c=CHUNKS3), a["L3_ffn_w_gate"].rearrange("(c p) d -> p c d", p=P)),
        (q_raw[:, 2].rearrange("p b i -> p (b i)"), a["L3_ffn_w_down"]),
    ]
    for i, n in enumerate(("L0_xattn_gamma_x", "L0_xattn_beta_x", "L0_xattn_gamma_l", "L0_xattn_beta_l",
                           "L1_xattn_ln1_g", "L1_xattn_ln1_b", "L1_xattn_ln2_g", "L1_xattn_ln2_b")):
        loads.append((k.aff[:, i:i + 1], a[n].rearrange("(p a) -> p a", a=1)))
    for i, n in enumerate(("Wq", "Wk", "Wv", "Wfc")):
        loads.append((k.w1a[:, i, :], a["L1_xattn_" + n]))
    for i, n in enumerate(("Wk", "Wv", "Wq", "Wo")):
        loads.append((w2_raw[:, i * D:(i + 1) * D], a["L2_xattn_" + n]))
    for i, n in enumerate(("WQ", "WK", "WV")):
        loads.append((w3_raw[:, i * D:(i + 1) * D], a["L3_xattn_" + n]))
    for i, n in enumerate(("bv", "bq")):
        loads.append((bcol[:, i:i + 1], a["L2_xattn_" + n].rearrange("(p a) -> p a", a=1)))
    for h in range(2):
        w2 = a["L2_ffn_W2"].rearrange("(k h) n d -> h n k d", h=2)
        b1 = a["L2_ffn_b1"].rearrange("(k h) n -> h k n", h=2)[:, :, P:HID2]
        w1 = a["L2_ffn_W1"].rearrange("(k h) d n -> h d k n", h=2)
        loads.append((k.w1tail[:, :, h * 64:h * 64 + 64], w1[h][:, :, P:HID2]))
        loads.append((k.w2b[h * 64:h * 64 + 64, :, :], w2[h, P:HID2]))
        loads.append((b1_raw[EXPERTS:CHUNKS2, h * 64:h * 64 + 64], b1[h]))
    loads.append((b1_raw[0:EXPERTS, :], a["L2_ffn_b1"][:, 0:P]))
    loads.append((k.b2r[:, :], a["L2_ffn_b2"]))
    xv = a["x"].rearrange("(t b) s d -> (b s) t d", b=PAIR)
    XPARTS = 4

    def sync(sp):
        for j in range(XPARTS):
            n = k.T // XPARTS
            sp.dma_start(k.x[:, j * n:(j + 1) * n, :], xv[:, j * n:(j + 1) * n, :]).then_inc(x_loaded, 16)
        for dst, src in loads[0::2]:
            sp.dma_start(dst, src).then_inc(loaded, 16)

    def all_loaded(eng):
        eng.wait_ge(loaded, 16 * len(loads))

    def scalar(act):
        for dst, src in loads[1::2]:
            act.dma_start(dst, src).then_inc(loaded, 16)
        all_loaded(act)
        act.activation(k.gates[:, :], gates_raw, ACT.Tanh).then_inc(gates_ready, 1)
        act.wait_ge(gates_ready, 1)
        act.activation(k.spike_gate[:, :], k.gates[:, 5:6], ACT.Copy, scale=1.0 / SPIKE_STEPS).then_inc(gates_ready, 1)
        act.wait_ge(turned, 1)
        for dst, src in ((k.wfc1[:, :], ps[:, 0, :]), (k.wpr1[:, :, :].rearrange("p c d -> p (c d)"), ps[:, 1, :]),
                         (woT, ps[:, 2, 0:D]), (k.wg0[:, :], ps[:, 2, 2 * D:2 * D + EXPERTS]),
                         (k.b1c[:, :], ps[:, 2, 3 * D:3 * D + CHUNKS2])):
            act.activation(dst, src, ACT.Copy).then_inc(turned_sb, 1)
        act.wait_ge(gates_ready, 1)
        act.activation(k.B[1][:, :], ps[:, 2, D:2 * D], ACT.Copy, scale=k.gates[:, 3:4]).then_inc(turned_sb, 1)
        act.wait_ge(turned, 2)
        for i, w in enumerate((k.wup3, k.wgt3, k.wdn3)):
            act.activation(w[:, :, :].rearrange("p c d -> p (c d)"), ps[:, 3 + i, 0:3 * D], ACT.Copy).then_inc(turned_sb, 1)
        act.wait_ge(folded, 1)
        act.activation(k.A[0][:, :], ps[:, 6, 0:D], ACT.Copy).then_inc(folded_sb, 1)
        act.activation(k.A[1][:, :], ps[:, 6, D:2 * D], ACT.Copy).then_inc(folded_sb, 1)
        act.activation(k.bqk[:, :], ps[:, 6, 2 * D:2 * D + 1], ACT.Copy).then_inc(folded_sb, 1)
        act.wait_ge(folded, 2)
        act.activation(k.B[0][:, :], ps[:, 7, 0:D], ACT.Copy, scale=k.gates[:, 2:3]).then_inc(folded_sb, 1)
        act.activation(k.bout[:, :], ps[:, 7, D:2 * D], ACT.Copy, scale=k.gates[:, 2:3]).then_inc(folded_sb, 1)

    def vector(dve):
        all_loaded(dve)
        src = k.wk0[:, :].rearrange("p (h s i) -> p h s i", s=2, i=HD0 // 2)
        dst = k.wr0[:, :].rearrange("p (h s i) -> p h s i", s=2, i=HD0 // 2)
        dve.tensor_scalar(dst[:, :, 0], src[:, :, 1], -1.0, None, ALU.mult).then_inc(built, 1)
        dve.tensor_copy(dst[:, :, 1], src[:, :, 0]).then_inc(built, 1)
        dve.tensor_scalar(bv_wide, k.konst[:, C_ONES:C_ONES + P], bcol[:, 0:1], None, ALU.mult).then_inc(built, 1)
        blocks = [P, 3, 12, BLOCK]
        dve.tensor_reduce(q_max, q_raw, AX.X, ALU.max, apply_absolute_value=True).then_inc(dequant, 1)
        dve.wait_ge(dequant, 1)
        dve.tensor_scalar(q_max, q_max, 1.0 / QMAX_W, 1e-12, ALU.mult, ALU.max).then_inc(dequant, 1)
        dve.wait_ge(dequant, 2)
        dve.reciprocal(q_inv, q_max).then_inc(dequant, 1)
        dve.wait_ge(dequant, 3)
        for w in range(3):
            dve.tensor_tensor(q_int[:, w], q_raw[:, w], q_inv[:, w].unsqueeze(2).broadcast_to(blocks[:1] + blocks[2:]),
                              ALU.mult).then_inc(dequant, 1)
        dve.wait_ge(dequant, 6)
        dve.tensor_scalar(q_clip, q_int, -QMAX_W - 1.0, QMAX_W, ALU.max, ALU.min).then_inc(dequant, 1)
        dve.wait_ge(dequant, 7)
        for w in range(3):
            dve.tensor_tensor(q_deq[:, w], q_clip[:, w], q_max[:, w].unsqueeze(2).broadcast_to(blocks[:1] + blocks[2:]),
                              ALU.mult).then_inc(dequant, 1)

    def tensor(pe):
        all_loaded(pe)
        for c in range(4):
            pe.transpose(ps[:, 0, c * P:(c + 1) * P], fc_raw[:, c * D:(c + 1) * D], k.ident)
            pe.transpose(ps[:, 1, c * P:(c + 1) * P], pr_raw[:, c * P:(c + 1) * P], k.ident)
        pe.transpose(ps[:, 2, 0:D], w2_raw[:, 3 * D:4 * D], k.ident)
        pe.transpose(ps[:, 2, D:2 * D], w3_raw[:, 2 * D:3 * D], k.ident)
        pe.transpose(ps[:, 2, 2 * D:2 * D + EXPERTS], gw_raw[0:EXPERTS, :],
                     k.konst[0:EXPERTS, C_IDENT:C_IDENT + EXPERTS])
        pe.transpose(ps[:, 2, 3 * D:3 * D + CHUNKS2], b1_raw[0:CHUNKS2, :],
                     k.konst[0:CHUNKS2, C_IDENT:C_IDENT + CHUNKS2]).then_inc(turned, 1)
        pe.matmul(ps[:, 6, 0:D], w2_raw[:, 2 * D:3 * D], w2_raw[:, 0:D], start=True, stop=True)
        pe.matmul(ps[:, 6, D:2 * D], w3_raw[:, 0:D], w3_raw[:, D:2 * D], start=True, stop=True)
        pe.matmul(ps[:, 6, 2 * D:2 * D + 1], w2_raw[:, 0:D], bcol[:, 1:2], start=True, stop=True).then_inc(folded, 1)
        pe.wait_ge(dequant, 10)
        for w in range(3):
            for c in range(3):
                flat = q_deq[:, w].rearrange("p b i -> p (b i)")[:, c * P:(c + 1) * P]
                mm = pe.transpose(ps[:, 3 + w, c * P:(c + 1) * P], flat, k.ident)
        mm.then_inc(turned, 1)
        pe.wait_ge(turned_sb, 6)
        pe.wait_ge(built, 3)
        pe.matmul(ps[:, 7, 0:D], w2_raw[:, D:2 * D], woT, start=True, stop=True)
        pe.matmul(ps[:, 7, D:2 * D], bv_wide, woT, start=True, stop=False)
        pe.matmul(ps[:, 7, D:2 * D], k.konst[0:1, C_ONES:C_ONES + P], bo_row[0:1, :], start=False, stop=True)\
            .then_inc(folded, 1)

    def ready(eng):
        eng.wait_ge(x_loaded, 16 * XPARTS)
        all_loaded(eng)
        eng.wait_ge(gates_ready, 2)
        eng.wait_ge(built, 3)
        eng.wait_ge(turned_sb, 9)
        eng.wait_ge(folded_sb, 5)

    k.ready = ready
    return dict(sync=sync, scalar=scalar, vector=vector, tensor=tensor)


def attention0(k, no):
    nc, ps, T = k.nc, k.psum, k.T
    f = k.front(no)
    f["xT_psum"] = k.sig(T, "xT_psum")
    k.stage_memory()
    two = lambda n: [k.take(n) for _ in range(2)]
    cin, zh = two(D), two(D)
    Z = [z.rearrange("p (b s i) -> p b s i", b=PAIR, s=2) for z in two(2 * P)]
    z1o, cto = two(P), two(P)
    KT = k.take(HPAIRS * 4 * SEQ).rearrange("p (c s b i) -> p c s b i", c=HPAIRS, s=2, b=PAIR)
    rotA, rotB = k.take(512), k.take(512)
    QBD = k.take(HPAIRS * PAIR * P).rearrange("p (c b h i) -> p c b h i", c=HPAIRS, b=PAIR, h=2)
    V = [v.rearrange("p (b h e) -> p b h e", b=PAIR, e=VW) for v in two(PAIR * H0 * VW)]
    mx = k.take(PAIR * HPAIRS)
    prob = k.take(PAIR * 512).rearrange("p (b n) -> p b n", b=PAIR)
    probT = k.take(PAIR * 512).rearrange("p (b c n) -> p b c n", b=PAIR, c=HPAIRS)
    rec = k.take(H0)
    on = k.take(INNER)
    oT = k.take(INNER)
    s = k.sigs(T, dict(
        zhat=1, z_ready=3, ctxT_sb=1, k_psum=1, k2_psum=1, q_psum=1, v_psum=2, kcos=1, ksin=1,
        krot=1, klat=1, qbd=2, v_sb=2, s_psum=2, smax=2, sshift=2, prob=2, pt_psum=2, pt_sb=2, av=1, recip=1,
        onorm=1, ot_psum=1, ot_sb=1, out_psum=1))
    ctx_loaded = k.transfers(T, "ctx_loaded")
    preset = k.sem("L0_preset")
    ctx_dram = k.a["ctx_1024"].rearrange("(t b) s d -> t (b s) d", b=PAIR)
    cosT = k.konst[:, C_COS:C_COS + SEQ].unsqueeze(1).broadcast_to([P, 8, SEQ])
    sinT = k.konst[:, C_SIN:C_SIN + SEQ].unsqueeze(1).broadcast_to([P, 8, SEQ])

    def sync(sp):
        k.ready(sp)

        def body(at):
            if t := at(3):
                if t.has(2):
                    sp.wait_ge(*f["xT_psum"](t.back(2)))
                sp.dma_start(cin[t.par], ctx_dram[t.idx]).then_inc(ctx_loaded.at(t), 16)
            if t := at(1):
                sp.wait_ge(*s["z_ready"](t))
                sp.dma_start(k.z1T_dram[t.idx], z1o[t.par]).then_inc(k.z1T_stored.at(t), 16)
                sp.wait_ge(*s["ctxT_sb"](t))
                sp.dma_start(k.ctxT_dram[t.idx], cto[t.par]).then_inc(k.ctxT_stored.at(t), 16)
        steps(sp, T, 3, 1, body)

    def gpsimd(pool):
        k.ready(pool)
        pool.memset(V[0][:, :, :, HD0:VW], 1.0).then_inc(preset, 1)
        pool.memset(V[1][:, :, :, HD0:VW], 1.0).then_inc(preset, 1)
        pool.memset(QBD, 0.0).then_inc(preset, 1)
        pool.wait_ge(preset, 3)

        def body(at):
            if t := at(2):
                sl = t.par
                pool.wait_ge(*f["aggr"](t))
                k.hold(pool)
                pool.tensor_scalar(k.ve[:, sl, 0:1], k.mv[:, sl, 0, 1:2], 1.0 + EPS, EPS * EPS, ALU.mult, ALU.add)
                pool.tensor_scalar(k.ve[:, sl, 1:2], k.mv[:, sl, 1, 1:2], 1.0, EPS, ALU.mult, ALU.add)\
                    .then_inc(f["vareps"].sem, 1)
                pool.wait_ge(*f["vareps"](t))
                pool.tensor_tensor(k.rstd[:, sl, :], k.ve[:, sl, :],
                                   k.konst[:, C_MHALF:C_MHALF + 2], ALU.pow).then_inc(f["rstd_ready"].sem, 1)
            if t := at(1):
                pool.wait_ge(*s["kcos"](t))
                k.hold(pool)
                pool.wait_ge(*s["ksin"](t))
                pool.tensor_tensor(KT[:, :, 0], rotA.rearrange("p (c b i) -> p c b i", c=HPAIRS, b=PAIR),
                                   rotB.rearrange("p (c b i) -> p c b i", c=HPAIRS, b=PAIR), ALU.add)\
                    .then_inc(s["krot"].sem, 1)
        steps(pool, T, 2, 0, body)

    def tensor(pe):
        k.ready(pe)
        pe.wait_ge(preset, 3)

        def body(at):
            if t := at(0):
                pe.wait_ge(*s["krot"](t))
                pe.wait_ge(*s["klat"](t))
                pe.wait_ge(*s["qbd"](t))
                for b in range(PAIR):
                    for c in range(HPAIRS):
                        mm = pe.matmul(ps[:, 6 + b, c * P:(c + 1) * P], QBD[:, c, b].rearrange("p h i -> p (h i)"),
                                       KT[:, c, :, b, :], start=True, stop=True)
                    mm.then_inc(s["s_psum"].sem, 1)
            if t := at(1):
                pe.wait_ge(*s["z_ready"](t))
                if t.has(2):
                    pe.wait_ge(*s["pt_sb"](t.back(2)))
                for c in range(HPAIRS):
                    w = k.wk0[:, c * P:(c + 1) * P]
                    pe.matmul(ps[:, 0, c * P:(c + 1) * P], w, Z[t.par][:, :, 0], start=True, stop=True)
                    mm = pe.matmul(ps[:, 1, c * P:(c + 1) * P], w, Z[t.par][:, :, 1], start=True, stop=True)
                mm.then_inc(s["k_psum"].sem, 1)
                if t.has(2):
                    pe.wait_ge(*s["onorm"](t.back(2)))
                for c in range(HPAIRS):
                    mm = pe.matmul(ps[:, 2, c * P:(c + 1) * P], k.wr0[:, c * P:(c + 1) * P], Z[t.par][:, :, 0],
                                   start=True, stop=True)
                mm.then_inc(s["k2_psum"].sem, 1)
                for c in range(HPAIRS):
                    mm = pe.matmul(ps[:, 3, c * P:(c + 1) * P], k.wq0[:, c * P:(c + 1) * P], Z[t.par][:, :, 1],
                                   start=True, stop=True)
                mm.then_inc(s["q_psum"].sem, 1)
            if t := at(-1):
                pe.wait_ge(*s["onorm"](t))
                if at(0):
                    pe.wait_ge(*s["v_sb"](at(0)))
                for c in range(HPAIRS):
                    mm = pe.transpose(ps[:, 5, c * P:(c + 1) * P], on[:, c * P:(c + 1) * P], k.ident)
                mm.then_inc(s["ot_psum"].sem, 1)
            if t := at(2):
                pe.wait_ge(*f["xhat_ready"](t))
                pe.wait_ge(*s["zhat"](t))
                if t.has(1):
                    pe.wait_ge(*s["ctxT_sb"](t.back(1)))
                if t.has(2):
                    pe.wait_ge(*s["v_sb"](t.back(2)))
                pe.transpose(ps[:, 4, 0:P], k.xh[:, t.par, :], k.ident)
                pe.transpose(ps[:, 4, P:2 * P], zh[t.par], k.ident)
                pe.transpose(ps[:, 4, 2 * P:3 * P], cin[t.par], k.ident).then_inc(f["xT_psum"].sem, 1)
            if t := at(-1):
                pe.wait_ge(*s["ot_sb"](t))
                for c in range(HPAIRS):
                    mm = pe.matmul(ps[:, 5, 0:D], oT[:, c * P:(c + 1) * P], k.wo0[:, c, :],
                                   start=c == 0, stop=c == HPAIRS - 1)
                mm.then_inc(s["out_psum"].sem, 1)
            if t := at(0):
                if at(1):
                    pe.wait_ge(*s["kcos"](at(1)))
                    pe.wait_ge(*s["klat"](at(1)))
                for b in range(PAIR):
                    pe.wait_ge(*s["prob"](t, b + 1))
                    for c in range(HPAIRS):
                        mm = pe.transpose(ps[:, b, c * P:(c + 1) * P], prob[:, b, c * P:(c + 1) * P], k.ident)
                    mm.then_inc(s["pt_psum"].sem, 1)
            if t := at(1):
                if at(2):
                    pe.wait_ge(*s["z_ready"](at(2)))
                    pe.wait_ge(*s["ctxT_sb"](at(2)))
                if at(-1):
                    pe.wait_ge(*f["x_updated"](at(-1)))
                for b in range(PAIR):
                    mm = pe.matmul(ps[:, 4 + b, :], Z[t.par][:, b].rearrange("p s i -> p (s i)"), k.wv0[:, :],
                                   start=True, stop=True)
                    mm.then_inc(s["v_psum"].sem, 1)
            if t := at(0):
                pe.wait_ge(*s["pt_sb"](t))
                pe.wait_ge(*s["v_sb"](t))
                if at(1):
                    pe.wait_ge(*s["ksin"](at(1)))
                    pe.wait_ge(*s["qbd"](at(1)))
                for h in range(H0):
                    for b in range(PAIR):
                        mm = pe.matmul(ps[b * 64:b * 64 + 64, 2 + h // 4, (h % 4) * VW:(h % 4 + 1) * VW],
                                       probT[:, b, h // 2, (h % 2) * 64:(h % 2) * 64 + 64], V[t.par][:, b, h, :],
                                       start=True, stop=True)
                mm.then_inc(s["av"].sem, 1)
        steps(pe, T, 2, 1, body)

    def vector(dve):
        k.ready(dve)

        def body(at):
            if t := at(2):
                sl = t.par
                dve.wait_ge(*ctx_loaded(t))
                k.hold(dve)
                dve.bn_stats(k.st[:, sl, 1, :], cin[sl])
                dve.bn_stats(k.st[:, sl, 0, :], k.x[:, t.idx, :]).then_inc(f["stats"].sem, 1)
                dve.wait_ge(*f["stats"](t))
                k.hold(dve)
                dve.bn_aggr(k.mv[:, sl, 1, :], k.st[:, sl, 1, :])
                dve.bn_aggr(k.mv[:, sl, 0, :], k.st[:, sl, 0, :]).then_inc(f["aggr"].sem, 1)
            if t := at(-1):
                dve.wait_ge(*s["av"](t))
                heads = ps[:, 2:4, 0:4 * VW].rearrange("p k (h e) -> p k h e", e=VW)
                dve.reciprocal(rec.rearrange("p (k h) -> p k h", k=2), heads[:, :, :, HD0]).then_inc(s["recip"].sem, 1)
                dve.wait_ge(*s["recip"](t))
                dve.tensor_tensor(on.rearrange("p (k h e) -> p k h e", k=2, e=HD0), heads[:, :, :, 0:HD0],
                                  rec.rearrange("p (k h) -> p k h", k=2).unsqueeze(3).broadcast_to([P, 2, 4, HD0]),
                                  ALU.mult).then_inc(s["onorm"].sem, 1)
            if t := at(0):
                for b in range(PAIR):
                    sc = ps[:, 6 + b, :].rearrange("p (c n) -> p c n", c=HPAIRS)
                    m = mx[:, b * HPAIRS:(b + 1) * HPAIRS]
                    dve.wait_ge(*s["s_psum"](t, b + 1))
                    dve.tensor_reduce(m, sc, AX.X, ALU.max).then_inc(s["smax"].sem, 1)
                    dve.wait_ge(*s["smax"](t, b + 1))
                    dve.tensor_tensor(prob[:, b].rearrange("p (c n) -> p c n", c=HPAIRS), sc,
                                      m.unsqueeze(2).broadcast_to([P, HPAIRS, P]), ALU.subtract)\
                        .then_inc(s["sshift"].sem, 1)
            if t := at(1):
                kk = [ps[:, n, :].rearrange("p (c i) -> p c i", i=SEQ) for n in (0, 2)]
                if t.has(1):
                    dve.wait_ge(*s["krot"](t.back(1)))
                dve.wait_ge(*s["k_psum"](t))
                dve.tensor_tensor(rotA.rearrange("p (c i) -> p c i", i=SEQ), kk[0], cosT, ALU.mult)\
                    .then_inc(s["kcos"].sem, 1)
                dve.wait_ge(*s["k2_psum"](t))
                dve.tensor_tensor(rotB.rearrange("p (c i) -> p c i", i=SEQ), kk[1], sinT, ALU.mult)\
                    .then_inc(s["ksin"].sem, 1)
            if t := at(2):
                sl = t.par
                tile_xhat(k, f, dve, t, sl)
                dve.tensor_scalar(zh[sl], cin[sl], k.mv[:, sl, 1, 0:1], k.rstd[:, sl, 1:2],
                                  ALU.subtract, ALU.mult).then_inc(s["zhat"].sem, 1)
                if t.has(2):
                    dve.wait_ge(*k.z1T_stored(t.back(2)))
                dve.wait_ge(*f["xT_psum"](t))
                for dst, n, g in ((Z[sl][:, :, 1], 0, 2), (Z[sl][:, :, 0], 1, 0),
                                  (z1o[sl].rearrange("p (b i) -> p b i", b=PAIR), 1, 4)):
                    dve.tensor_scalar(dst, ps[:, 4, n * P:(n + 1) * P].rearrange("p (b i) -> p b i", b=PAIR), k.aff[:, g:g + 1], k.aff[:, g + 1:g + 2],
                                      ALU.mult, ALU.add).then_inc(s["z_ready"].sem, 1)
            if t := at(-1):
                dve.wait_ge(*s["out_psum"](t))
                dve.scalar_tensor_tensor(out=k.x[:, t.idx, :], in0=ps[:, 5, 0:D], scalar=k.gates[:, 0:1],
                                         in1=k.x[:, t.idx, :], op0=ALU.mult, op1=ALU.add)\
                    .then_inc(f["x_updated"].sem, 1)
        steps(dve, T, 2, 1, body)

    def scalar(act):
        k.ready(act)
        act.wait_ge(preset, 3)

        def body(at):
            if t := at(0):
                for b in range(PAIR):
                    act.wait_ge(*s["sshift"](t, b + 1))
                    act.activation(prob[:, b], prob[:, b], ACT.Exp, scale=HD0 ** -0.5).then_inc(s["prob"].sem, 1)
            if t := at(1):
                act.wait_ge(*s["k_psum"](t))
                act.activation(KT[:, :, 1], ps[:, 1, :].rearrange("p (c b i) -> p c b i", c=HPAIRS, b=PAIR),
                               ACT.Copy).then_inc(s["klat"].sem, 1)
                act.wait_ge(*s["q_psum"](t))
                for h in range(2):
                    rows = slice(64 * h, 64 * h + 64)
                    act.activation(QBD[rows, :, :, h, :],
                                   ps[rows, 3, :].rearrange("p (c b i) -> p c b i", c=HPAIRS, b=PAIR),
                                   ACT.Copy).then_inc(s["qbd"].sem, 1)
            if t := at(-1):
                act.wait_ge(*s["ot_psum"](t))
                act.activation(oT, ps[:, 5, :], ACT.Copy).then_inc(s["ot_sb"].sem, 1)
            if t := at(2):
                if t.has(2):
                    act.wait_ge(*k.ctxT_stored(t.back(2)))
                act.wait_ge(*s["z_ready"](t))
                act.activation(cto[t.par], ps[:, 4, 2 * P:3 * P], ACT.Copy).then_inc(s["ctxT_sb"].sem, 1)
            if t := at(0):
                for b in range(PAIR):
                    act.wait_ge(*s["pt_psum"](t, b + 1))
                    act.activation(probT[:, b].rearrange("p c n -> p (c n)"), ps[:, b, :], ACT.Copy)\
                        .then_inc(s["pt_sb"].sem, 1)
            if t := at(1):
                for b in range(PAIR):
                    act.wait_ge(*s["v_psum"](t, b + 1))
                    act.activation(V[t.par][:, b, :, 0:HD0], ps[:, 4 + b, :].rearrange("p (h e) -> p h e", e=HD0),
                                   ACT.Copy).then_inc(s["v_sb"].sem, 1)
        steps(act, T, 2, 1, body)

    return dict(sync=sync, gpsimd=gpsimd, tensor=tensor, vector=vector, scalar=scalar)


def sub(g, j):
    return Tile(g.idx * GROUP + j, j % 2)


class Route:

    OPS = 2 * GROUP + 3

    def __init__(self, k):
        self.k = k
        self.score = k.take(GROUP * EXPERTS).rearrange("p (j e) -> p j e", j=GROUP)
        self.best = k.take(GROUP * 8).rearrange("p (j e) -> p j e", j=GROUP)
        self.where = k.take(GROUP * 8).bitcast(U32).rearrange("p (j e) -> p j e", j=GROUP)
        self.wheref = k.take(GROUP * 2).rearrange("p (j e) -> p j e", j=GROUP)
        self.hit = [k.take(GROUP * EXPERTS).rearrange("p (j e) -> p j e", j=GROUP) for _ in range(2)]
        self.done = k.sig(k.T // GROUP, "routed", self.OPS)

    def run(self, dve, g):
        k, wide = self.k, [P, GROUP, EXPERTS]
        for j in range(GROUP):
            dve.max(self.best[:, j], self.score[:, j]).then_inc(self.done.sem, 1)
        dve.wait_ge(*self.done(g, GROUP))
        k.hold(dve)
        for j in range(GROUP):
            dve.max_index(self.where[:, j], self.best[:, j], self.score[:, j]).then_inc(self.done.sem, 1)
        dve.wait_ge(*self.done(g, 2 * GROUP))
        dve.tensor_copy(self.wheref, self.where[:, :, 0:2]).then_inc(self.done.sem, 1)
        dve.wait_ge(*self.done(g, 2 * GROUP + 1))
        for n in range(2):
            iota = k.konst[:, C_IOTA:C_IOTA + EXPERTS].unsqueeze(1).broadcast_to(wide)
            dve.tensor_tensor(self.hit[n], iota, self.wheref[:, :, n:n + 1].broadcast_to(wide), ALU.is_equal)\
                .then_inc(self.done.sem, 1)


def group_front(k, f, xTg, bank, twice=False):
    def dve_stats(dve, g, j):
        dve.bn_stats(k.st[:, j, 0, :], k.x[:, sub(g, j).idx, :]).then_inc(f["stats"].sem, 1)

    def dve_aggr(dve, g):
        dve.wait_ge(*f["stats"](sub(g, GROUP - 1)))
        k.hold(dve)
        for j in range(GROUP):
            dve.bn_aggr(k.mv[:, j, 0, :], k.st[:, j, 0, :]).then_inc(f["aggr"].sem, 1)

    def dve_xhat(dve, g, j):
        if g.has(1) and j == 0:
            dve.wait_ge(*f["xT_psum"](g.back(1)))
        tile_xhat(k, f, dve, sub(g, j), j)

    def dve_part(dve, g):
        for j in range(GROUP):
            dve_stats(dve, g, j)
        dve_aggr(dve, g)
        for j in range(GROUP):
            dve_xhat(dve, g, j)

    dve_part.stats, dve_part.aggr, dve_part.xhat = dve_stats, dve_aggr, dve_xhat

    def pool_part(pool, g):
        last = sub(g, GROUP - 1)
        pool.wait_ge(*f["aggr"](last))
        k.hold(pool)
        pool.tensor_scalar(k.ve[:, :, 0], k.mv[:, :, 0, 1], 1.0 + EPS if twice else 1.0,
                           EPS * EPS if twice else EPS, ALU.mult, ALU.add).then_inc(f["vareps"].sem, GROUP)
        pool.wait_ge(*f["vareps"](last))
        pool.tensor_tensor(k.rstd[:, :, 0], k.ve[:, :, 0], k.konst[:, C_MHALF:C_MHALF + GROUP],
                           ALU.pow).then_inc(f["rstd_ready"].sem, GROUP)

    def pe_part(pe, g):
        pe.wait_ge(*f["xhat_ready"](sub(g, GROUP - 1)))
        if g.has(1):
            pe.wait_ge(*f["xT_sb"](g.back(1)))
        for j in range(GROUP):
            mm = pe.transpose(k.psum[:, bank, j * P:(j + 1) * P], k.xh[:, j, :], k.ident)
        mm.then_inc(f["xT_psum"].sem, 1)

    def act_part(act, g):
        act.wait_ge(*f["xT_psum"](g))
        act.activation(xTg[g.par], k.psum[:, bank, :], ACT.Copy).then_inc(f["xT_sb"].sem, 1)
    return dve_part, pool_part, pe_part, act_part


def group_signals(k, no):
    f = k.front(no)
    f.update(k.sigs(k.T // GROUP, dict(xT_psum=1, xT_sb=1)))
    return f


class Combine:

    def __init__(self, k, f, experts, extra=False):
        self.k, self.f, self.experts, self.extra = k, f, experts, extra
        some = lambda slots, n: [k.take(n) for _ in range(slots)]
        self.scaled, self.pairs = some(2, 4 * D), some(2, 2 * D)
        self.rest, self.half = some(GROUP, D), some(2, D)
        self.s = k.sigs(k.T, dict(y_psum=1, scaled=4, summed=3 if extra else 2, acc=4))

    def scalar(self, act, g, j, coef, bank):
        s, t = self.s, sub(g, j)
        act.wait_ge(*s["y_psum"](t))
        if t.has(2):
            act.wait_ge(*s["summed"](t.back(2), 1))
        for i, e in enumerate(self.experts[1]):
            act.activation(self.scaled[t.par][:, i * D:(i + 1) * D], self.k.psum[:, bank, i * D:(i + 1) * D],
                           ACT.Copy, scale=coef[:, j, e:e + 1]).then_inc(s["scaled"].sem, 1)

    def gpsimd(self, pool, g, j, extra=None):
        s, t = self.s, sub(g, j)
        sc, pair, rest = self.scaled[t.par], self.pairs[t.par], self.rest[j]
        pool.wait_ge(*s["scaled"](t))
        pool.tensor_tensor(pair, sc[:, 0:2 * D], sc[:, 2 * D:4 * D], ALU.add).then_inc(s["summed"].sem, 1)
        pool.wait_ge(*s["summed"](t, 1))
        if t.has(GROUP):
            pool.wait_ge(*s["acc"](t.back(GROUP), 2))
        pool.tensor_tensor(rest, pair[:, 0:D], pair[:, D:2 * D], ALU.add).then_inc(s["summed"].sem, 1)
        if self.extra:
            pool.wait_ge(*s["summed"](t, 2))
            pool.tensor_tensor(rest, rest, extra[:, j * D:(j + 1) * D], ALU.add).then_inc(s["summed"].sem, 1)

    def vector(self, dve, g, j, coef, bank):
        s, t = self.s, sub(g, j)
        x, half = self.k.x[:, t.idx, :], self.half[t.par]

        def add(i, into, base):
            e = self.experts[0][i]
            return dve.scalar_tensor_tensor(out=into, in0=self.k.psum[:, bank, i * D:(i + 1) * D],
                                            scalar=coef[:, j, e:e + 1], in1=base, op0=ALU.mult, op1=ALU.add)

        dve.wait_ge(*s["y_psum"](t))
        add(0, x, x).then_inc(s["acc"].sem, 1)
        dve.wait_ge(*s["summed"](t))
        if t.has(2):
            dve.wait_ge(*self.f["x_updated"](t.back(2)))
        add(1, half, self.rest[j]).then_inc(s["acc"].sem, 1)
        dve.wait_ge(*s["acc"](t, 1))
        add(2, x, x).then_inc(s["acc"].sem, 1)
        dve.wait_ge(*s["acc"](t, 2))
        add(3, half, half).then_inc(s["acc"].sem, 1)
        dve.wait_ge(*s["acc"](t, 4))
        dve.tensor_tensor(x, x, half, ALU.add).then_inc(self.f["x_updated"].sem, 1)


def experts0(k, no):
    ps, G = k.psum, k.T // GROUP
    f = group_signals(k, no)
    k.stage_memory()
    xTg = [k.take(GCOLS) for _ in range(2)]
    route = Route(k)
    gap, e, den, rden = (k.take(GROUP) for _ in range(4))
    w = [k.take(GROUP) for _ in range(2)]
    part = [k.take(GROUP * EXPERTS).rearrange("p (j e) -> p j e", j=GROUP) for _ in range(2)]
    coef = [k.take(GROUP * EXPERTS).rearrange("p (j e) -> p j e", j=GROUP) for _ in range(2)]
    combine = Combine(k, f, (range(4), range(4, 8)))
    y_psum = combine.s["y_psum"]
    s = k.sigs(G, dict(l_psum=1, l_sb=1, gap=1, e=1, w=4, part=2, coef=1))
    d_front, p_front, t_front, a_front = group_front(k, f, xTg, 0)
    wide = [P, GROUP, EXPERTS]

    def gpsimd(pool):
        def body(at):
            if g := at(2):
                p_front(pool, g)
            if g := at(0):
                for j in range(GROUP):
                    combine.gpsimd(pool, g, j)
        steps(pool, G, 2, 0, body)

    def tensor(pe):
        def body(at):
            if g := at(1):
                pe.wait_ge(*f["xT_sb"](g))
                if g.has(1):
                    pe.wait_ge(*s["l_sb"](g.back(1)))
                for j in range(GROUP):
                    mm = pe.matmul(ps[:, 1, j * EXPERTS:(j + 1) * EXPERTS], xTg[g.par][:, j * P:(j + 1) * P],
                                   k.wg0[:, :], start=True, stop=True)
                mm.then_inc(s["l_psum"].sem, 1)
            if g := at(0):
                for j in range(GROUP):
                    t = sub(g, j)
                    if t.has(GROUP):
                        pe.wait_ge(*f["x_updated"](t.back(GROUP)))
                    if t.has(2):
                        pe.wait_ge(*combine.s["scaled"](t.back(2)))
                    for h in range(2):
                        mm = pe.matmul(ps[:, 6 + t.par if h else 2 + j, :], xTg[g.par][:, j * P:(j + 1) * P],
                                       k.we0[:, 4 * h:4 * h + 4, :].rearrange("p e m -> p (e m)"),
                                       start=True, stop=True)
                    mm.then_inc(y_psum.sem, 1)
            if g := at(2):
                t_front(pe, g)
        steps(pe, G, 2, 0, body)

    def vector(dve):
        def top_two(g):
            dve.wait_ge(*s["l_psum"](g))
            dve.tensor_copy(route.score, ps[:, 1, 0:GROUP * EXPERTS].rearrange("p (j e) -> p j e", j=GROUP))\
                .then_inc(s["l_sb"].sem, 1)
            dve.wait_ge(*s["l_sb"](g))
            k.hold(dve)
            route.run(dve, g)
            dve.tensor_tensor(gap, route.best[:, :, 1], route.best[:, :, 0], ALU.subtract).then_inc(s["gap"].sem, 1)

        def coefficients(g):
            dve.wait_ge(*s["e"](g))
            dve.tensor_scalar(den, e, 1.0, None, ALU.add).then_inc(s["w"].sem, 1)
            dve.wait_ge(*s["w"](g, 1))
            dve.reciprocal(rden, den).then_inc(s["w"].sem, 1)
            dve.wait_ge(*s["w"](g, 2))
            dve.tensor_scalar(w[0], rden, k.gates[:, 4:5], None, ALU.mult).then_inc(s["w"].sem, 1)
            dve.wait_ge(*s["w"](g, 3))
            dve.tensor_tensor(w[1], e, w[0], ALU.mult).then_inc(s["w"].sem, 1)
            dve.wait_ge(*s["w"](g, 4))
            dve.wait_ge(*route.done(g))
            for n in range(2):
                dve.tensor_tensor(part[n], route.hit[n], w[n].unsqueeze(2).broadcast_to(wide), ALU.mult)\
                    .then_inc(s["part"].sem, 1)
            dve.wait_ge(*s["part"](g))
            dve.tensor_tensor(coef[g.par], part[0], part[1], ALU.add).then_inc(s["coef"].sem, 1)

        def body(at):
            if g := at(2):
                for j in range(GROUP):
                    d_front.stats(dve, g, j)
                d_front.aggr(dve, g)

            def tile(j):
                if g := at(0):
                    combine.vector(dve, g, j, coef[g.par], 2 + j)

            if g := at(1):
                top_two(g)
            tile(0)
            if g := at(2):
                for j in range(GROUP):
                    d_front.xhat(dve, g, j)
            tile(1)
            if g := at(1):
                coefficients(g)
            tile(2)
            tile(3)
        steps(dve, G, 2, 0, body)

    def scalar(act):
        def body(at):
            for j in range(GROUP):
                if g := at(0):
                    if j == 0:
                        act.wait_ge(*s["coef"](g))
                    combine.scalar(act, g, j, coef[g.par], 6 + j % 2)
                if j == 0 and (g := at(1)):
                    act.wait_ge(*s["gap"](g))
                    act.activation(e, gap, ACT.Exp).then_inc(s["e"].sem, 1)
            if g := at(2):
                a_front(act, g)
        steps(act, G, 2, 0, body)

    return dict(gpsimd=gpsimd, tensor=tensor, vector=vector, scalar=scalar)


def attention1(k, no):
    ps, T = k.psum, k.T
    f = k.front(no)
    f["xT_psum"] = k.sig(T, "xT_psum")
    k.stage_memory()
    two = lambda n: [k.take(n) for _ in range(2)]
    HALF = H1 // 2
    zt = two(P)
    zs = [z.rearrange("p (b u i) -> p b u i", b=PAIR, u=2) for z in two(4 * SEQ)]
    QB = [q.rearrange("p (n b i) -> p n b i", n=2, b=PAIR) for q in two(4 * SEQ)]
    KM = [v.rearrange("p (n h i) -> p n h i", n=2, h=HALF) for v in two(2 * HALF * SEQ)]
    NV = HD1 + 1
    VB = [v.rearrange("p (b n h e) -> p b n h e", b=PAIR, h=2, e=NV) for v in two(PAIR * H1 * NV)]
    mx = k.take(H1).rearrange("p (n h) -> p n h", n=2)
    prob = [v.rearrange("p (n h i) -> p n h i", n=2, h=HALF) for v in two(H1 * SEQ)]
    probT = k.take(H1 * SEQ).rearrange("p (n i) -> p n i", n=2)
    rec = k.take(H1)
    on, oT = k.take(D), k.take(D)
    loads = [k.transfers(T, f"z_loaded{u}") for u in range(2)]
    s = k.sigs(T, dict(
        zt=1, k_psum=1, vq_psum=1, qb=2, km=1, vb=2, s_psum=2, smax=2, sshift=2, prob=2, pt_psum=2, pt_sb=2,
        av=1, recip=1, onorm=1, ot_psum=1, ot_sb=1, out_psum=1))
    preset = k.sem("A1_preset")

    def sync(sp):
        def body(at):
            if t := at(3):
                if t.has(2):
                    sp.wait_ge(*s["vq_psum"](t.back(2)))
                for u in range(2):
                    sp.dma_start(zs[t.par][:, :, u, :], k.z1T_dram[t.idx].rearrange("p (b i) -> p b i", b=PAIR))\
                        .then_inc(loads[u].at(t), 16)
        steps(sp, T, 3, 0, body)

    def gpsimd(pool):
        for n in range(2):
            pool.memset(VB[n], 0.0).then_inc(preset, 1)
            pool.memset(QB[n], 0.0).then_inc(preset, 1)
        pool.wait_ge(preset, 4)
        for n in range(2):
            for h in range(2):
                pool.memset(VB[n][64 * h:64 * h + 64, :, :, h, HD1:NV], 1.0).then_inc(preset, 1)
        pool.wait_ge(preset, 8)

        def body(at):
            if t := at(3):
                tile_rstd(k, f, pool, t, t.par, True)
        steps(pool, T, 3, 0, body)

    def tensor(pe):
        def body(at):
            if t := at(0):
                pe.wait_ge(*s["qb"](t))
                pe.wait_ge(*s["km"](t))
                for n in range(2):
                    pe.matmul(ps[:, 3 + n, :], QB[t.par][:, n].rearrange("p b i -> p (b i)"),
                              KM[t.par][:, n].rearrange("p h i -> p (h i)"), start=True, stop=True)\
                        .then_inc(s["s_psum"].sem, 1)
            if t := at(-2):
                pe.wait_ge(*s["ot_sb"](t))
                pe.matmul(ps[:, 0, D:2 * D], oT, k.w1a[:, 3, :], start=True, stop=True).then_inc(s["out_psum"].sem, 1)
            if t := at(-1):
                pe.wait_ge(*s["vb"](t))
                for n in range(2):
                    pe.wait_ge(*s["pt_sb"](t, n + 1))
                    for c in range(4):
                        for b in range(PAIR):
                            m = 4 * n + c
                            mm = pe.matmul(ps[64 * b:64 * b + 64, 7, m * 2 * NV:(m + 1) * 2 * NV],
                                           probT[:, n, c * P + b * SEQ:c * P + (b + 1) * SEQ],
                                           VB[t.par][:, b, m].rearrange("p h e -> p (h e)"), start=True, stop=True)
                mm.then_inc(s["av"].sem, 1)
            if t := at(2):
                for u in range(2):
                    pe.wait_ge(*loads[u](t))
                if t.has(1):
                    pe.wait_ge(*s["km"](t.back(1)))
                for n in range(2):
                    for b in range(PAIR):
                        mm = pe.matmul(ps[64 * b:64 * b + 64, 2, n * SEQ:(n + 1) * SEQ],
                                       k.w1a[:, 1, 64 * n:64 * n + 64], zs[t.par][:, b, 0, :], start=True, stop=True)
                mm.then_inc(s["k_psum"].sem, 1)
            if t := at(1):
                pe.wait_ge(*s["zt"](t))
                for b in range(PAIR):
                    pe.matmul(ps[:, 1, (b + 1) * D:(b + 2) * D], zs[t.par][:, b].rearrange("p u i -> p (u i)"),
                              k.w1a[:, 2, :], start=True, stop=True)
                for n in range(2):
                    for b in range(PAIR):
                        mm = pe.matmul(ps[64 * b:64 * b + 64, 1, n * SEQ:(n + 1) * SEQ],
                                       k.w1a[:, 0, 64 * n:64 * n + 64], zt[t.par][:, b * SEQ:(b + 1) * SEQ],
                                       start=True, stop=True)
                mm.then_inc(s["vq_psum"].sem, 1)
            if t := at(0):
                for n in range(2):
                    pe.wait_ge(*s["prob"](t, n + 1))
                    for c in range(4):
                        mm = pe.transpose(ps[:, 5 + n, c * P:(c + 1) * P],
                                          prob[t.par][:, n, 2 * c:2 * c + 2].rearrange("p h i -> p (h i)"), k.ident)
                    mm.then_inc(s["pt_psum"].sem, 1)
            if t := at(-1):
                pe.wait_ge(*s["onorm"](t))
                if t.has(1):
                    pe.wait_ge(*f["x_updated"](t.back(1)))
                pe.transpose(ps[:, 0, 0:D], on, k.ident).then_inc(s["ot_psum"].sem, 1)
            if t := at(2):
                pe.wait_ge(*f["xhat_ready"](t))
                if t.has(1):
                    pe.wait_ge(*s["vb"](t.back(1)))
                pe.transpose(ps[:, 1, 3 * D:4 * D], k.xh[:, t.par, :], k.ident).then_inc(f["xT_psum"].sem, 1)
        steps(pe, T, 2, 2, body)

    def vector(dve):
        def maxima(t, n):
            dve.wait_ge(*s["s_psum"](t, n + 1))
            dve.tensor_reduce(mx[:, n], ps[:, 3 + n, :].rearrange("p (h i) -> p h i", i=SEQ), AX.X, ALU.max)\
                .then_inc(s["smax"].sem, 1)

        def shift(t, n):
            dve.wait_ge(*s["smax"](t, n + 1))
            dve.tensor_tensor(prob[t.par][:, n], ps[:, 3 + n, :].rearrange("p (h i) -> p h i", i=SEQ),
                              mx[:, n].unsqueeze(2).broadcast_to([P, HALF, SEQ]), ALU.subtract)\
                .then_inc(s["sshift"].sem, 1)

        def body(at):
            if t := at(0):
                maxima(t, 0)
            if t := at(3):
                dve.bn_stats(k.st[:, t.par, 0, :], k.x[:, t.idx, :]).then_inc(f["stats"].sem, 1)
            if t := at(0):
                shift(t, 0)
                maxima(t, 1)
            if t := at(3):
                dve.wait_ge(*f["stats"](t))
                k.hold(dve)
                dve.bn_aggr(k.mv[:, t.par, 0, :], k.st[:, t.par, 0, :]).then_inc(f["aggr"].sem, 1)
            if t := at(0):
                shift(t, 1)
            heads = ps[:, 7, 0:H1 * NV].rearrange("p (n e) -> p n e", e=NV)
            if t := at(-1):
                dve.wait_ge(*s["av"](t))
                dve.reciprocal(rec, heads[:, :, HD1]).then_inc(s["recip"].sem, 1)
            if t := at(-2):
                dve.wait_ge(*s["out_psum"](t))
                dve.scalar_tensor_tensor(out=k.x[:, t.idx, :], in0=ps[:, 0, D:2 * D], scalar=k.gates[:, 1:2],
                                         in1=k.x[:, t.idx, :], op0=ALU.mult, op1=ALU.add)\
                    .then_inc(f["x_updated"].sem, 1)
            if t := at(-1):
                dve.wait_ge(*s["recip"](t))
                dve.tensor_tensor(on.rearrange("p (n e) -> p n e", e=HD1), heads[:, :, 0:HD1],
                                  rec.unsqueeze(2).broadcast_to([P, H1, HD1]), ALU.mult).then_inc(s["onorm"].sem, 1)
            if t := at(2):
                dve.wait_ge(*s["k_psum"](t))
                dve.tensor_tensor(KM[t.par], ps[:, 2, 0:P].rearrange("p (n i) -> p n i", n=2).unsqueeze(2)
                                  .broadcast_to([P, 2, HALF, SEQ]),
                                  k.konst[:, C_MASK8:C_MASK8 + HALF].unsqueeze(1).unsqueeze(3)
                                  .broadcast_to([P, 2, HALF, SEQ]), ALU.mult).then_inc(s["km"].sem, 1)
            if t := at(3):
                tile_xhat(k, f, dve, t, t.par)
        steps(dve, T, 3, 2, body)

    def scalar(act):
        act.wait_ge(preset, 8)

        def body(at):
            if t := at(0):
                for n in range(2):
                    act.wait_ge(*s["sshift"](t, n + 1))
                    act.activation(prob[t.par][:, n], prob[t.par][:, n], ACT.Exp, scale=HD1 ** -0.5)\
                        .then_inc(s["prob"].sem, 1)
            if t := at(1):
                act.wait_ge(*s["vq_psum"](t))
                for b in range(PAIR):
                    rows = slice(64 * b, 64 * b + 64)
                    act.activation(QB[t.par][rows, :, b, :], ps[rows, 1, 0:P].rearrange("p (n i) -> p n i", n=2),
                                   ACT.Copy).then_inc(s["qb"].sem, 1)
                for h in range(2):
                    rows = slice(64 * h, 64 * h + 64)
                    act.activation(VB[t.par][rows, :, :, h, 0:HD1],
                                   ps[rows, 1, D:3 * D].rearrange("p (b n h e) -> p b n h e", b=PAIR, h=2,
                                                                  e=HD1)[:, :, :, h],
                                   ACT.Copy).then_inc(s["vb"].sem, 1)
            if t := at(0):
                for n in range(2):
                    act.wait_ge(*s["pt_psum"](t, n + 1))
                    act.activation(probT[:, n], ps[:, 5 + n, :], ACT.Copy).then_inc(s["pt_sb"].sem, 1)
            if t := at(-1):
                act.wait_ge(*s["ot_psum"](t))
                act.activation(oT, ps[:, 0, 0:D], ACT.Copy).then_inc(s["ot_sb"].sem, 1)
            if t := at(2):
                act.wait_ge(*f["xT_psum"](t))
                act.activation(zt[t.par], ps[:, 1, 3 * D:4 * D], ACT.Identity, scale=k.aff[:, 6:7],
                               bias=k.aff[:, 7:8]).then_inc(s["zt"].sem, 1)
        steps(act, T, 2, 1, body)

    return dict(sync=sync, gpsimd=gpsimd, tensor=tensor, vector=vector, scalar=scalar)


def spiking1(k, no):
    ps, G = k.psum, k.T // GROUP
    f = group_signals(k, no)
    k.stage_memory()
    NC = FF1 // P
    xTg = [k.take(GCOLS) for _ in range(2)]
    relu = k.take(NC * GCOLS).rearrange("p (c n) -> p c n", c=NC)
    sq = [v.rearrange("p (c n) -> p c n", c=NC) for v in (k.take(NC * GCOLS) for _ in range(2))]
    mem = [k.take(GCOLS) for _ in range(2)]
    spike = [k.take(GCOLS) for _ in range(SPIKE_STEPS)]
    decayed, drive, count = k.take(GCOLS), [k.take(GCOLS) for _ in range(2)], [k.take(GCOLS) for _ in range(2)]
    s = k.sigs(G, dict(h_psum=NC, relu=NC, sq=NC, y_psum=1, drive=1, decayed=SPIKE_STEPS - 1,
                       mem=SPIKE_STEPS - 1, spike=SPIKE_STEPS, count=SPIKE_STEPS - 1))
    d_front, p_front, t_front, a_front = group_front(k, f, xTg, 0)

    def gpsimd(pool):
        def body(at):
            if g := at(3):
                p_front(pool, g)
            if g := at(-1):
                c = count[g.par]
                if g.has(2):
                    pool.wait_ge(*f["x_updated"](sub(g.back(2), GROUP - 1)))
                for n in range(1, SPIKE_STEPS):
                    pool.wait_ge(*s["spike"](g, n + 1))
                    if n > 1:
                        pool.wait_ge(*s["count"](g, n - 1))
                    pool.tensor_tensor(c, spike[n], spike[0] if n == 1 else c, ALU.add).then_inc(s["count"].sem, 1)
        steps(pool, G, 3, 1, body)

    def tensor(pe):
        def body(at):
            if g := at(2):
                t_front(pe, g)
            if g := at(1):
                pe.wait_ge(*f["xT_sb"](g))
                for c in range(NC):
                    if g.has(1):
                        pe.wait_ge(*s["relu"](g.back(1), c + 1))
                    pe.matmul(ps[:, 1 + c, :], k.wfc1[:, c * P:(c + 1) * P], xTg[g.par], start=True, stop=True)\
                        .then_inc(s["h_psum"].sem, 1)
            if g := at(0):
                pe.wait_ge(*s["sq"](g))
                if g.has(1):
                    pe.wait_ge(*s["drive"](g.back(1)))
                for j in range(GROUP):
                    for c in range(NC):
                        mm = pe.matmul(ps[:, 5, j * P:(j + 1) * P], sq[g.par][:, c, j * P:(j + 1) * P],
                                       k.wpr1[:, c, :], start=c == 0, stop=c == NC - 1)
                mm.then_inc(s["y_psum"].sem, 1)
        steps(pe, G, 2, 0, body)

    def vector(dve):
        def spikes(g, n, m):
            dve.tensor_scalar(spike[n], m, 1.0, None, ALU.is_gt).then_inc(s["spike"].sem, 1)

        def body(at):
            g, new = at(-1), at(3)
            if g:
                dve.wait_ge(*s["drive"](g))
                if g.has(1):
                    dve.wait_ge(*s["count"](g.back(1)))
                m = y = drive[g.par]
            for n in range(1, SPIKE_STEPS):
                if g:
                    if n > 1:
                        dve.wait_ge(*s["mem"](g, n - 1))
                    dve.scalar_tensor_tensor(out=decayed, in0=m, scalar=BETA, in1=y, op0=ALU.mult, op1=ALU.add)\
                        .then_inc(s["decayed"].sem, 1)
                    spikes(g, n - 1, m)
                    dve.wait_ge(*s["decayed"](g, n))
                    dve.scalar_tensor_tensor(out=mem[n % 2], in0=m, scalar=1.0, in1=decayed, op0=ALU.is_gt,
                                             op1=ALU.subtract, reverse1=True).then_inc(s["mem"].sem, 1)
                    m = mem[n % 2]
                if new and n < 3:
                    d_front.stats(dve, new, 2 * n - 2)
                    d_front.stats(dve, new, 2 * n - 1)
                if new and n == 3:
                    d_front.aggr(dve, new)
            old = at(-2)
            if old:
                update(old)
            if g:
                dve.wait_ge(*s["mem"](g))
                spikes(g, SPIKE_STEPS - 1, m)
            if new:
                for j in range(GROUP):
                    d_front.xhat(dve, new, j)

        def update(g):
            dve.wait_ge(*s["count"](g))
            for j in range(GROUP):
                x = k.x[:, sub(g, j).idx, :]
                dve.scalar_tensor_tensor(out=x, in0=count[g.par][:, j * P:(j + 1) * P], scalar=k.spike_gate[:, :],
                                         in1=x, op0=ALU.mult, op1=ALU.add).then_inc(f["x_updated"].sem, 1)
        steps(dve, G, 3, 2, body)

    def scalar(act):
        def body(at):
            if g := at(0):
                act.wait_ge(*s["y_psum"](g))
                if g.has(2):
                    act.wait_ge(*s["mem"](g.back(2)))
                act.activation(drive[g.par], ps[:, 5, :], ACT.Copy).then_inc(s["drive"].sem, 1)
            if g := at(2):
                a_front(act, g)
            if g := at(1):
                for c in range(NC):
                    act.wait_ge(*s["h_psum"](g, c + 1))
                    if g.has(1):
                        act.wait_ge(*s["sq"](g.back(1), c + 1))
                    act.activation(relu[:, c, :], ps[:, 1 + c, :], ACT.Relu).then_inc(s["relu"].sem, 1)
                for c in range(NC):
                    act.wait_ge(*s["relu"](g, c + 1))
                    act.activation(sq[g.par][:, c, :], relu[:, c, :], ACT.Square).then_inc(s["sq"].sem, 1)
        steps(act, G, 2, 0, body)

    return dict(gpsimd=gpsimd, tensor=tensor, vector=vector, scalar=scalar)


def context_attention(layer):
    biased, masked = layer == 2, layer == 3
    SCALE = D ** -0.5

    def stage(k, no):
        ps, N = k.psum, k.T // DUO
        f = k.front(no)
        f["xT_psum"] = k.sig(N, "xT_psum")
        k.stage_memory()
        two = lambda n: [k.take(n) for _ in range(2)]
        by_tile = lambda v: v.rearrange("p (j n) -> p j n", j=DUO)
        xT, qT = two(DUO * P), two(DUO * P)
        cT = [by_tile(v) for v in two(DUO * P)]
        cr = [by_tile(v) for v in two(DUO * D)]
        pT, uT = two(DUO * P), two(DUO * P)
        prob, sm = [by_tile(v) for v in two(DUO * P)], [by_tile(v) for v in two(DUO * SEQ)]
        xb = [by_tile(v) for v in two(DUO * D)]
        mx, nb, rs, rec = two(DUO), two(DUO), two(DUO), two(DUO)
        A, B = k.A[layer - 2], k.B[layer - 2]
        s = k.sigs(N, dict(
            xT_sb=1, q_psum=1, q_sb=1, s_psum=1, smax=1, nb=1, prob=DUO * PAIR, pt_psum=1, pt_sb=1, u_psum=1,
            u_sb=1, recip=1, out_psum=1))
        preset = k.sem(f"A{layer}_preset")
        s["biased" if biased else "masked"] = k.sig(N, "biased" if biased else "masked")
        cT_loaded, cr_loaded = k.transfers(N, "cT_loaded"), k.transfers(N, "cr_loaded")
        ctx_dram = k.a["ctx_1024"].rearrange("(n j b) s d -> n (b s) j d", j=DUO, b=PAIR)
        ctxT_dram = k.ctxT_dram.rearrange("(n j) p i -> n p j i", j=DUO)

        def tile(d, j):
            return Tile(d.idx * DUO + j, j)

        def slots(d):
            return slice(DUO * d.par, DUO * d.par + DUO)

        def sync(sp):
            def body(at):
                if d := at(2):
                    if d.has(2):
                        sp.wait_ge(*s["s_psum"](d.back(2)))
                    sp.dma_start(cT[d.par], ctxT_dram[d.idx]).then_inc(cT_loaded.at(d), 16)
                if d := at(1):
                    if d.has(2):
                        sp.wait_ge(*s["u_psum"](d.back(2)))
                    sp.dma_start(cr[d.par], ctx_dram[d.idx]).then_inc(cr_loaded.at(d), 16)
            steps(sp, N, 2, 0, body)

        def gpsimd(pool):
            for n in range(2):
                pool.memset(prob[n], 0.0).then_inc(preset, 1)

            def body(at):
                if d := at(4):
                    pool.wait_ge(*f["aggr"](tile(d, DUO - 1)))
                    k.hold(pool)
                    pool.tensor_scalar(k.ve[:, slots(d), 0], k.mv[:, slots(d), 0, 1], 1.0, EPS, ALU.mult, ALU.add)\
                        .then_inc(f["vareps"].sem, DUO)
                    pool.wait_ge(*f["vareps"](tile(d, DUO - 1)))
                    pool.tensor_tensor(k.rstd[:, slots(d), 0], k.ve[:, slots(d), 0],
                                       k.konst[:, C_MHALF:C_MHALF + DUO], ALU.pow).then_inc(f["rstd_ready"].sem, DUO)
                if biased and (d := at(0)):
                    if d.has(2):
                        pool.wait_ge(*f["x_updated"](tile(d.back(2), DUO - 1)))
                        k.hold(pool)
                    pool.tensor_tensor(xb[d.par], k.x[:, bass.ds(d.idx * DUO, DUO), :],
                                       k.bout[:, :].unsqueeze(1).broadcast_to([P, DUO, D]), ALU.add)\
                        .then_inc(s["biased"].sem, 1)
            steps(pool, N, 4, 0, body)

        def tensor(pe):
            def body(at):
                if d := at(-2):
                    pe.wait_ge(*s["u_sb"](d))
                    if d.has(2):
                        pe.wait_ge(*f["x_updated"](tile(d.back(2), DUO - 1)))
                    for j in range(DUO):
                        mm = pe.matmul(ps[:, 6 + d.par, j * D:(j + 1) * D], uT[d.par][:, j * P:(j + 1) * P], B[:, :],
                                       start=True, stop=True)
                    mm.then_inc(s["out_psum"].sem, 1)
                if d := at(-1):
                    pe.wait_ge(*s["pt_sb"](d))
                    pe.wait_ge(*cr_loaded(d))
                    if d.has(1):
                        pe.wait_ge(*s["u_sb"](d.back(1)))
                    for j in range(DUO):
                        cols = slice(j * P, (j + 1) * P)
                        mm = pe.matmul(ps[:, 5, cols], cr[d.par][:, j], pT[d.par][:, cols], start=True, stop=True)
                    mm.then_inc(s["u_psum"].sem, 1)
                if d := at(0):
                    pe.wait_ge(*s["prob"](d))
                    if d.has(1):
                        pe.wait_ge(*s["pt_sb"](d.back(1)))
                    for j in range(DUO):
                        mm = pe.transpose(ps[:, 4, j * P:(j + 1) * P], prob[d.par][:, j], k.ident)
                    mm.then_inc(s["pt_psum"].sem, 1)
                if d := at(1):
                    pe.wait_ge(*s["q_sb"](d))
                    pe.wait_ge(*cT_loaded(d))
                    if d.has(2):
                        pe.wait_ge(*s["prob"](d.back(2)))
                    for j in range(DUO):
                        for b in range(PAIR):
                            cols = slice(b * SEQ, (b + 1) * SEQ)
                            mm = pe.matmul(ps[64 * b:64 * b + 64, 2 + d.par, j * SEQ:(j + 1) * SEQ],
                                           qT[d.par][:, j * P + b * SEQ:j * P + (b + 1) * SEQ],
                                           cT[d.par][:, j, cols], start=True, stop=True)
                    mm.then_inc(s["s_psum"].sem, 1)
                if d := at(2):
                    pe.wait_ge(*s["xT_sb"](d))
                    if d.has(1):
                        pe.wait_ge(*s["q_sb"](d.back(1)))
                    pe.matmul(ps[:, 1, 0:DUO * P], A[:, :], xT[d.par], start=True, stop=True)\
                        .then_inc(s["q_psum"].sem, 1)
                if d := at(3):
                    pe.wait_ge(*f["xhat_ready"](tile(d, DUO - 1)))
                    if d.has(1):
                        pe.wait_ge(*s["xT_sb"](d.back(1)))
                    for j in range(DUO):
                        mm = pe.transpose(ps[:, 0, j * P:(j + 1) * P], k.xh[:, DUO * d.par + j, :], k.ident)
                    mm.then_inc(f["xT_psum"].sem, 1)
            steps(pe, N, 3, 2, body)

        def vector(dve):
            def body(at):
                if d := at(4):
                    for j in range(DUO):
                        dve.bn_stats(k.st[:, DUO * d.par + j, 0, :], k.x[:, tile(d, j).idx, :])\
                            .then_inc(f["stats"].sem, 1)
                if d := at(-1):
                    dve.wait_ge(*s["u_psum"](d))
                    dve.tensor_copy(uT[d.par], ps[:, 5, 0:DUO * P]).then_inc(s["u_sb"].sem, 1)
                if d := at(4):
                    dve.wait_ge(*f["stats"](tile(d, DUO - 1)))
                    k.hold(dve)
                    for j in range(DUO):
                        sl = DUO * d.par + j
                        dve.bn_aggr(k.mv[:, sl, 0, :], k.st[:, sl, 0, :]).then_inc(f["aggr"].sem, 1)
                if d := at(1):
                    dve.wait_ge(*s["s_psum"](d))
                    src = ps[:, 2 + d.par, 0:DUO * SEQ].rearrange("p (j n) -> p j n", j=DUO)
                    if masked:
                        dve.tensor_tensor(sm[d.par], src, k.konst[:, C_CAUSAL:C_CAUSAL + SEQ].unsqueeze(1)
                                          .broadcast_to([P, DUO, SEQ]), ALU.mult).then_inc(s["masked"].sem, 1)
                        dve.wait_ge(*s["masked"](d))
                        src = sm[d.par]
                    dve.tensor_reduce(mx[d.par], src, AX.X, ALU.max).then_inc(s["smax"].sem, 1)
                if d := at(1):
                    dve.wait_ge(*s["smax"](d))
                    dve.tensor_scalar(nb[d.par], mx[d.par], -SCALE, None, ALU.mult).then_inc(s["nb"].sem, 1)
                if d := at(-2):
                    dve.wait_ge(*s["out_psum"](d))
                    if biased:
                        dve.wait_ge(*s["biased"](d))
                    for j in range(DUO):
                        x = k.x[:, tile(d, j).idx, :]
                        dve.scalar_tensor_tensor(out=x, in0=ps[:, 6 + d.par, j * D:(j + 1) * D],
                                                 scalar=rec[d.par][:, j:j + 1], in1=xb[d.par][:, j] if biased else x,
                                                 op0=ALU.mult, op1=ALU.add).then_inc(f["x_updated"].sem, 1)
                if d := at(4):
                    if d.has(2):
                        dve.wait_ge(*f["xT_psum"](d.back(2)))
                    for j in range(DUO):
                        tile_xhat(k, f, dve, tile(d, j), DUO * d.par + j)
                if d := at(0):
                    dve.wait_ge(*s["prob"](d))
                    if d.has(2):
                        dve.wait_ge(*f["x_updated"](tile(d.back(2), DUO - 1)))
                        k.hold(dve)
                    dve.reciprocal(rec[d.par], rs[d.par]).then_inc(s["recip"].sem, 1)
            steps(dve, N, 4, 2, body)

        def scalar(act):
            act.wait_ge(preset, 2)

            def body(at):
                if d := at(0):
                    act.wait_ge(*s["pt_psum"](d))
                    act.activation(pT[d.par], ps[:, 4, 0:DUO * P], ACT.Copy).then_inc(s["pt_sb"].sem, 1)
                if d := at(1):
                    act.wait_ge(*s["nb"](d))
                    for j in range(DUO):
                        for b in range(PAIR):
                            rows = slice(64 * b, 64 * b + 64)
                            src = sm[d.par][rows, j] if masked else ps[rows, 2 + d.par, j * SEQ:(j + 1) * SEQ]
                            act.activation(prob[d.par][rows, j, b * SEQ:(b + 1) * SEQ], src, ACT.Exp, scale=SCALE,
                                           bias=nb[d.par][rows, j:j + 1], accum_out=rs[d.par][rows, j:j + 1])\
                                .then_inc(s["prob"].sem, 1)
                if d := at(2):
                    act.wait_ge(*s["q_psum"](d))
                    if biased:
                        act.activation(qT[d.par], ps[:, 1, 0:DUO * P], ACT.Identity, bias=k.bqk[:, :])\
                            .then_inc(s["q_sb"].sem, 1)
                    else:
                        act.activation(qT[d.par], ps[:, 1, 0:DUO * P], ACT.Copy).then_inc(s["q_sb"].sem, 1)
                if d := at(3):
                    act.wait_ge(*f["xT_psum"](d))
                    act.activation(xT[d.par], ps[:, 0, 0:DUO * P], ACT.Copy).then_inc(s["xT_sb"].sem, 1)
            steps(act, N, 3, 0, body)

        return dict(sync=sync, gpsimd=gpsimd, tensor=tensor, vector=vector, scalar=scalar)
    return stage


def experts2(k, no):
    ps, G = k.psum, k.T // GROUP
    f = group_signals(k, no)
    k.stage_memory()
    xTg = [k.take(GCOLS) for _ in range(2)]
    hT = [v.rearrange("p (c n) -> p c n", c=CHUNKS2) for v in (k.take(CHUNKS2 * GCOLS) for _ in range(2))]
    small = lambda: k.take(GROUP * EXPERTS).rearrange("p (j e) -> p j e", j=GROUP)
    score, shifted, expd, hits, coef = small(), small(), small(), small(), [small() for _ in range(2)]
    route = Route(k)
    smax, ssum, srec = k.take(GROUP), k.take(GROUP), k.take(GROUP)
    coefT = k.take(GCOLS)
    b2sum = [k.take(GCOLS) for _ in range(2)]
    combine = Combine(k, f, (range(0, EXPERTS, 2), range(1, EXPERTS, 2)), extra=True)
    y_psum = combine.s["y_psum"]
    s = k.sigs(G, dict(
        l_psum=1, score=1, smax=1, shifted=1, expd=1, ssum=1, srec=1, routing_prob=1, hits=1, coef=1, ct_psum=1,
        ct_sb=1, b2_psum=1, b2_sb=1, h_psum=CHUNKS2, h_sb=CHUNKS2))
    d_front, p_front, t_front, a_front = group_front(k, f, xTg, 0)
    wide = [P, GROUP, EXPERTS]

    def gpsimd(pool):
        def body(at):
            if g := at(2):
                p_front(pool, g)
            if g := at(0):
                pool.wait_ge(*s["b2_sb"](g))
                for j in range(GROUP):
                    combine.gpsimd(pool, g, j, b2sum[g.par])
        steps(pool, G, 2, 0, body)

    def tensor(pe):
        def hidden(g, first):
            for c in range(first, first + 4):
                if c >= 2:
                    pe.wait_ge(*s["h_sb"](g, c - 1))
                elif g.has(1):
                    pe.wait_ge(*s["h_sb"](g.back(1), CHUNKS2 - 1 + c))
                w = k.w1s[:, c, 0:P] if c < EXPERTS else k.w1tail[:, c - EXPERTS, :]
                pe.matmul(ps[:, 2 + c % 2, :], w, xTg[g.par], start=True, stop=True).then_inc(s["h_psum"].sem, 1)

        def outputs(g, j):
            cols = slice(j * P, (j + 1) * P)
            t = sub(g, j)
            if t.has(2):
                pe.wait_ge(*f["x_updated"](t.back(2)))
            for e in range(EXPERTS):
                dst = ps[:, 4 + t.par + 2 * (e % 2), (e // 2) * D:(e // 2 + 1) * D]
                rows = slice(64 * (e % 2), 64 * (e % 2) + 64)
                pe.matmul(dst, hT[g.par][:, e, cols], k.w2a[:, e, :], start=True, stop=False)
                mm = pe.matmul(dst, hT[g.par][rows, EXPERTS + e // 2, cols], k.w2b[rows, e // 2, :],
                               start=False, stop=True)
            mm.then_inc(y_psum.sem, 1)

        def body(at):
            g, nxt = at(0), at(1)
            if g:
                pe.wait_ge(*s["h_sb"](g))
                outputs(g, 0)
            if nxt:
                pe.wait_ge(*f["xT_sb"](nxt))
                if nxt.has(1):
                    pe.wait_ge(*s["b2_sb"](nxt.back(1)))
                for j in range(GROUP):
                    mm = pe.matmul(ps[:, 1, j * EXPERTS:(j + 1) * EXPERTS], xTg[nxt.par][:, j * P:(j + 1) * P],
                                   k.wr2[:, :], start=True, stop=True)
                mm.then_inc(s["l_psum"].sem, 1)
                hidden(nxt, 0)
            if g:
                outputs(g, 1)
            if nxt:
                hidden(nxt, 4)
            if g:
                outputs(g, 2)
            if nxt:
                hidden(nxt, 8)
                pe.wait_ge(*s["coef"](nxt))
                for j in range(GROUP):
                    mm = pe.transpose(ps[0:EXPERTS, 1, j * P:(j + 1) * P], coef[nxt.par][:, j], k.ident)
                mm.then_inc(s["ct_psum"].sem, 1)
            if g:
                outputs(g, 3)
            if nxt:
                pe.wait_ge(*s["ct_sb"](nxt))
                for j in range(GROUP):
                    mm = pe.matmul(ps[:, 1, j * D:(j + 1) * D], coefT[0:EXPERTS, j * P:(j + 1) * P], k.b2r[:, :],
                                   start=True, stop=True)
                mm.then_inc(s["b2_psum"].sem, 1)
            if at(2):
                t_front(pe, at(2))
        steps(pe, G, 2, 0, body)

    def vector(dve):
        def scores(g):
            dve.wait_ge(*s["l_psum"](g))
            dve.tensor_tensor(score, ps[:, 1, 0:GROUP * EXPERTS].rearrange("p (j e) -> p j e", j=GROUP),
                              k.br2[:, :].unsqueeze(1).broadcast_to(wide), ALU.add).then_inc(s["score"].sem, 1)
            dve.wait_ge(*s["score"](g))
            dve.tensor_reduce(smax, score, AX.X, ALU.max).then_inc(s["smax"].sem, 1)
            dve.wait_ge(*s["smax"](g))
            dve.tensor_tensor(shifted, score, smax.unsqueeze(2).broadcast_to(wide), ALU.subtract)\
                .then_inc(s["shifted"].sem, 1)

        def routing(g):
            dve.wait_ge(*s["expd"](g))
            dve.tensor_reduce(ssum, expd, AX.X, ALU.add).then_inc(s["ssum"].sem, 1)
            dve.wait_ge(*s["ssum"](g))
            dve.reciprocal(srec, ssum).then_inc(s["srec"].sem, 1)
            dve.wait_ge(*s["srec"](g))
            dve.tensor_tensor(route.score, expd, srec.unsqueeze(2).broadcast_to(wide), ALU.mult)\
                .then_inc(s["routing_prob"].sem, 1)
            dve.wait_ge(*s["routing_prob"](g))
            k.hold(dve)
            route.run(dve, g)
            dve.wait_ge(*route.done(g))
            dve.tensor_tensor(hits, route.hit[0], route.hit[1], ALU.add).then_inc(s["hits"].sem, 1)
            dve.wait_ge(*s["hits"](g))
            if g.has(2):
                dve.wait_ge(*f["x_updated"](sub(g.back(2), GROUP - 1)))
            dve.scalar_tensor_tensor(out=coef[g.par], in0=hits, scalar=k.gates[:, 6:7], in1=route.score,
                                     op0=ALU.mult, op1=ALU.mult).then_inc(s["coef"].sem, 1)

        def body(at):
            g, nxt, new = at(0), at(1), at(2)
            if new:
                for j in range(GROUP):
                    d_front.stats(dve, new, j)
                d_front.aggr(dve, new)
            if g:
                combine.vector(dve, g, 0, coef[g.par], 4)
            if nxt:
                scores(nxt)
            if new:
                for j in range(GROUP):
                    d_front.xhat(dve, new, j)
            if g:
                combine.vector(dve, g, 1, coef[g.par], 5)
            if nxt:
                routing(nxt)
            if g:
                combine.vector(dve, g, 2, coef[g.par], 4)
                combine.vector(dve, g, 3, coef[g.par], 5)
        steps(dve, G, 2, 0, body)

    def scalar(act):
        def hidden_out(g, first):
            for c in range(first, first + 4):
                act.wait_ge(*s["h_psum"](g, c + 1))
                act.activation(hT[g.par][:, c, :], ps[:, 2 + c % 2, :], ACT.Gelu, bias=k.b1c[:, c:c + 1])\
                    .then_inc(s["h_sb"].sem, 1)

        def body(at):
            g, nxt = at(0), at(1)
            for j in range(GROUP):
                if nxt and j < 3:
                    hidden_out(nxt, 4 * j)
                if g and j < 3:
                    combine.scalar(act, g, j, coef[g.par], 6 + j % 2)
                if nxt and j == 1:
                    act.wait_ge(*s["shifted"](nxt))
                    act.activation(expd, shifted, ACT.Exp).then_inc(s["expd"].sem, 1)
            if nxt:
                act.wait_ge(*s["ct_psum"](nxt))
                act.activation(coefT[0:EXPERTS, :], ps[0:EXPERTS, 1, :], ACT.Copy).then_inc(s["ct_sb"].sem, 1)
            if g:
                combine.scalar(act, g, 3, coef[g.par], 7)
            if nxt:
                act.wait_ge(*s["b2_psum"](nxt))
                if nxt.has(2):
                    act.wait_ge(*combine.s["summed"](sub(nxt.back(2), GROUP - 1)))
                act.activation(b2sum[nxt.par], ps[:, 1, :], ACT.Copy).then_inc(s["b2_sb"].sem, 1)
            if at(2):
                a_front(act, at(2))
        steps(act, G, 2, 0, body)

    return dict(gpsimd=gpsimd, tensor=tensor, vector=vector, scalar=scalar)


def quantised3(k, no):
    ps, T, G = k.psum, k.T, k.T // GROUP
    f = k.front(no)
    k.stage_memory()
    W = CHUNKS3 * GCOLS
    half = lambda n: k.take(n // 2).bitcast(I16)
    upq = half(G * W).rearrange("p (g n) -> p g n", g=G)
    xdT = k.take(T * P).rearrange("p (g n) -> p g n", g=G)
    xhs = k.take(T * P).rearrange("p (g n) -> p g n", g=G)
    mark = k.taken
    gq2 = k.arena[:, mark - 2 * T * P:mark - 2 * T * P + G * W // 2].bitcast(I16).rearrange("p (g n) -> p g n", g=G)
    k.taken = mark - T * P
    gq, sig, sigq = [half(W) for _ in range(2)], [k.take(W) for _ in range(2)], k.take(W // 2).bitcast(U16)
    gs = [k.take(W) for _ in range(2)]
    k.taken = max(mark - 2 * T * P + G * W // 2, mark - T * P)
    gin, prod = [k.take(W) for _ in range(2)], [k.take(W) for _ in range(2)]
    k.taken = mark - 2 * T * P + G * W // 2
    oprod, oq, of = k.take(W), half(W), [k.take(W) for _ in range(2)]
    sb = k.sb
    xq, xd = sb("xq", [P, GCOLS], I16), sb("xd", [P, GCOLS])
    affine = sb("affine_of_norm", [P, 2, 2, GROUP])
    xmax, ugmax = sb("xmax", [P, G]), sb("ugmax", [P, 2, G, CHUNKS3])
    gsmax, omax = sb("gsmax", [P, G]), sb("omax", [P, G])
    local, wide = sb("local_max", [P, 2]), sb("wide_max", [2, P])
    top = sb("top_max", [2, 1])
    scale = {n: sb(f"scale_{n}", [P, w]) for n, w in dict(x=1, ug=2, gs=1, o=1).items()}
    inv = {n: sb(f"inv_{n}", [P, w]) for n, w in dict(x=1, ug=2, gs=1, o=1).items()}
    sprod, down = sb("scale_product", [P, 1]), sb("scale_down", [P, 1])
    gs_dram = k.nc.dram_tensor("gated_scratch", [G, P, W], F32, kind="Internal").ap()
    gs_stored, gs_loaded = k.transfers(G, "gated_stored"), k.transfers(G, "gated_loaded")
    s = k.sigs(G, dict(
        shift=2, xhs=GROUP, xmax=1, xq=1, xd=1, t_psum=1, xdT=1, p_psum=2 * CHUNKS3, pmax=2 * CHUNKS3, c_psum=2 * CHUNKS3, upq=CHUNKS3,
        gq=CHUNKS3, sig=1, sigq=1, gs=1, gsmax=1, gq2=1, prod=1, omax=1, oprod=1, oq=1, of=1, y_psum=1))
    SCALES = ("x", "ug", "gs", "o")
    found, spread = k.sem("Q3_scale_found"), k.sem("Q3_scale_spread")
    final = k.sem("Q3_final_scales")
    d_front, p_front, _, _ = group_front(k, f, None, 0)

    def scale_vector(dve, name, columns, factor):
        n, w = SCALES.index(name), scale[name].shape[1]
        dve.tensor_reduce(local[:, 0:w], columns, AX.X, ALU.max).then_inc(found, 1)
        dve.wait_ge(spread, 2 * n + 1)
        dve.tensor_reduce(top[0:w, :], ps[0:w, 7, 0:P], AX.X, ALU.max).then_inc(found, 1)
        dve.wait_ge(found, 5 * n + 2)
        dve.tensor_scalar(wide[0:w, :], k.konst[0:w, C_ONES:C_ONES + P], top[0:w, :], None, ALU.mult)\
            .then_inc(found, 1)
        dve.wait_ge(spread, 2 * n + 2)
        dve.tensor_scalar(scale[name][:, :], ps[:, 7, P:P + w], factor / QMAX_A, 1e-12, ALU.mult, ALU.max)\
            .then_inc(found, 1)
        dve.wait_ge(found, 5 * n + 4)
        dve.reciprocal(inv[name][:, :], scale[name][:, :]).then_inc(found, 1)
        dve.wait_ge(found, 5 * n + 5)

    def scale_tensor(pe, name):
        n, w = SCALES.index(name), scale[name].shape[1]
        pe.wait_ge(found, 5 * n + 1)
        pe.transpose(ps[0:w, 7, 0:P], local[:, 0:w], k.ident).then_inc(spread, 1)
        pe.wait_ge(found, 5 * n + 3)
        pe.matmul(ps[:, 7, P:P + w], wide[0:w, :], k.konst[0:w, C_IDENT:C_IDENT + w], start=True, stop=True)\
            .then_inc(spread, 1)

    def scale_known(eng, name):
        eng.wait_ge(found, 5 * SCALES.index(name) + 5)

    def sync(sp):
        def store(at):
            if g := at(0):
                sp.wait_ge(*s["gs"](g))
                sp.dma_start(gs_dram[g.idx], gs[g.par]).then_inc(gs_stored.at(g), 16)
        steps(sp, G, 0, 0, store)
        gs_stored.wait_all(sp, G)
        sp.wait_ge(*s["gsmax"].all(G))

        def load(at):
            if g := at(0):
                if g.has(2):
                    sp.wait_ge(*s["gq2"](g.back(2)))
                sp.dma_start(gin[g.par], gs_dram[g.idx]).then_inc(gs_loaded.at(g), 16)
        steps(sp, G, 0, 2, load)

    def gpsimd(pool):
        def normalise(at):
            if g := at(2):
                if g.has(1):
                    pool.wait_ge(*s["shift"](g.back(1)))
                p_front(pool, g)
        steps(pool, G, 2, 0, normalise)

    def project(pe, g, psum_signal, freed, parts=(0, 1)):
        for n in parts:
            w = (k.wup3, k.wgt3)[n]
            for c in range(CHUNKS3):
                if g.has(1):
                    freed(g.back(1), n, c)
                pe.matmul(ps[:, 1 + CHUNKS3 * n + c, :], w[:, c, :], xdT[:, g.idx, :], start=True, stop=True)\
                    .then_inc(psum_signal.sem, 1)

    def tensor(pe):
        scale_tensor(pe, "x")

        def first(at):
            def freed(b, n, c):
                pe.wait_ge(*s["pmax"](b, CHUNKS3 * n + c + 1))

            if g := at(0):
                pe.wait_ge(*s["xdT"](g))
                project(pe, g, s["p_psum"], freed, (0,))
            if g := at(1):
                pe.wait_ge(*s["xd"](g))
                if g.has(1):
                    pe.wait_ge(*s["xdT"](g.back(1)))
                for j in range(GROUP):
                    mm = pe.transpose(ps[:, 0, j * P:(j + 1) * P], xd[:, j * P:(j + 1) * P], k.ident)
                mm.then_inc(s["t_psum"].sem, 1)
            if g := at(0):
                project(pe, g, s["p_psum"], freed, (1,))
        steps(pe, G, 1, 0, first)
        scale_tensor(pe, "ug")

        def second(at):
            if g := at(0):
                project(pe, g, s["c_psum"],
                        lambda b, n, c: pe.wait_ge(*s["gq" if n else "upq"](b, c + 1)))
        pe.wait_ge(*s["pmax"].all(G))
        steps(pe, G, 0, 0, second)
        scale_tensor(pe, "gs")
        scale_tensor(pe, "o")

        def last(at):
            if g := at(0):
                pe.wait_ge(*s["of"](g))
                if g.has(2):
                    pe.wait_ge(*f["x_updated"](sub(g.back(2), GROUP - 1)))
                for j in range(GROUP):
                    for c in range(CHUNKS3):
                        mm = pe.matmul(ps[:, g.par, j * P:(j + 1) * P],
                                       of[g.par][:, c * GCOLS + j * P:c * GCOLS + (j + 1) * P], k.wdn3[:, c, :],
                                       start=c == 0, stop=c == CHUNKS3 - 1)
                mm.then_inc(s["y_psum"].sem, 1)
        steps(pe, G, 0, 0, last)

    def vector(dve):
        def normalise(at):
            if g := at(2):
                for j in range(GROUP):
                    d_front.stats(dve, g, j)
            if g := at(0):
                dve.wait_ge(*s["xhs"](g))
                k.hold(dve)
                dve.tensor_reduce(xmax[:, bass.ds(g.idx, 1)], xhs[:, g.idx, :], AX.X, ALU.max,
                                  apply_absolute_value=True).then_inc(s["xmax"].sem, 1)
            if g := at(2):
                if g.has(1):
                    dve.wait_ge(*s["shift"](g.back(1)))
                d_front.aggr(dve, g)
                dve.wait_ge(*f["rstd_ready"](sub(g, GROUP - 1)))
                dve.tensor_copy(affine[:, g.par, 0, :], k.rstd[:, :, 0]).then_inc(s["shift"].sem, 1)
                dve.scalar_tensor_tensor(out=affine[:, g.par, 1, :], in0=k.mv[:, :, 0, 0], scalar=-1.0, in1=k.rstd[:, :, 0],
                                         op0=ALU.mult, op1=ALU.mult).then_inc(s["shift"].sem, 1)
        steps(dve, G, 2, 0, normalise)
        dve.wait_ge(*s["xmax"].all(G))
        scale_vector(dve, "x", xmax[:, :], 1.0)

        def first(at):
            if g := at(0):
                for n in range(2 * CHUNKS3):
                    dve.wait_ge(*s["p_psum"](g, n + 1))
                    k.hold(dve)
                    dve.tensor_reduce(ugmax[:, n // CHUNKS3, g.idx, n % CHUNKS3:n % CHUNKS3 + 1], ps[:, 1 + n, :],
                                      AX.X, ALU.max, apply_absolute_value=True).then_inc(s["pmax"].sem, 1)
            if g := at(2):
                if g.has(1):
                    dve.wait_ge(*s["xd"](g.back(1)))
                dve.tensor_scalar(xq[:, :], xhs[:, g.idx, :], inv["x"][:, :], None, ALU.mult).then_inc(s["xq"].sem, 1)
                dve.wait_ge(*s["xq"](g))
                if g.has(1):
                    dve.wait_ge(*s["t_psum"](g.back(1)))
                dve.tensor_scalar(xd[:, :], xq[:, :], scale["x"][:, :], None, ALU.mult).then_inc(s["xd"].sem, 1)
        steps(dve, G, 2, 0, first)
        dve.wait_ge(*s["pmax"].all(G))
        scale_vector(dve, "ug", ugmax[:, :, :, :].rearrange("p w g c -> p w (g c)"), 1.0)

        def second(at):
            if g := at(0):
                dve.wait_ge(*s["sig"](g))
                dve.tensor_scalar(sigq, sig[g.par], QSIG, QSIG - 1.0, ALU.mult, ALU.min).then_inc(s["sigq"].sem, 1)
                dve.wait_ge(*s["sigq"](g))
                if g.has(2):
                    dve.wait_ge(*gs_stored(g.back(2)))
                dve.scalar_tensor_tensor(out=gs[g.par], in0=gq[g.par], scalar=scale["ug"][:, 1:2], in1=sigq, op0=ALU.mult,
                                         op1=ALU.mult).then_inc(s["gs"].sem, 1)
                dve.wait_ge(*s["gs"](g))
                k.hold(dve)
                dve.tensor_reduce(gsmax[:, bass.ds(g.idx, 1)], gs[g.par], AX.X, ALU.max, apply_absolute_value=True)\
                    .then_inc(s["gsmax"].sem, 1)
        steps(dve, G, 0, 0, second)
        dve.wait_ge(*s["gsmax"].all(G))
        scale_vector(dve, "gs", gsmax[:, :], 1.0)
        dve.tensor_scalar(sprod[:, :], scale["gs"][:, :], scale["ug"][:, 0:1], 1.0 / QSIG, ALU.mult, ALU.mult)\
            .then_inc(final, 1)
        dve.wait_ge(final, 1)

        def product(g, out, signal):
            dve.scalar_tensor_tensor(out=out, in0=gq2[:, g.idx, :], scalar=sprod[:, :], in1=upq[:, g.idx, :],
                                     op0=ALU.mult, op1=ALU.mult).then_inc(signal.sem, 1)

        def third(at):
            if g := at(1):
                dve.wait_ge(*s["gq2"](g))
                if g.has(2):
                    dve.wait_ge(*s["omax"](g.back(2)))
                product(g, prod[g.par], s["prod"])
            if g := at(0):
                dve.wait_ge(*s["prod"](g))
                k.hold(dve)
                dve.tensor_reduce(omax[:, bass.ds(g.idx, 1)], prod[g.par], AX.X, ALU.max, apply_absolute_value=True)\
                    .then_inc(s["omax"].sem, 1)
        steps(dve, G, 1, 0, third)
        dve.wait_ge(*s["omax"].all(G))
        scale_vector(dve, "o", omax[:, :], 1.0)
        dve.tensor_scalar(down[:, :], scale["o"][:, :], k.gates[:, 7:8], None, ALU.mult).then_inc(final, 1)
        dve.wait_ge(final, 2)

        def last(at):
            if g := at(2):
                if g.has(1):
                    dve.wait_ge(*s["oq"](g.back(1)))
                product(g, oprod, s["oprod"])
            if g := at(0):
                dve.wait_ge(*s["y_psum"](g))
                x = k.x[:, bass.ds(g.idx * GROUP, GROUP), :].rearrange("p j n -> p (j n)")
                dve.scalar_tensor_tensor(out=x, in0=ps[:, g.par, :], scalar=down[:, :], in1=x, op0=ALU.mult,
                                         op1=ALU.add).then_inc(f["x_updated"].sem, GROUP)
        steps(dve, G, 2, 0, last)

    def scalar(act):
        def normalise(at):
            if g := at(1):
                act.wait_ge(*s["shift"](g))
                for j in range(GROUP):
                    act.activation(xhs[:, g.idx, j * P:(j + 1) * P], k.x[:, sub(g, j).idx, :], ACT.Identity,
                                   scale=affine[:, g.par, 0, j:j + 1],
                                   bias=affine[:, g.par, 1, j:j + 1]).then_inc(s["xhs"].sem, 1)
        steps(act, G, 1, 0, normalise)
        scale_known(act, "x")

        def first(at):
            if g := at(1):
                act.wait_ge(*s["t_psum"](g))
                k.hold(act)
                act.activation(xdT[:, g.idx, :], ps[:, 0, :], ACT.Copy).then_inc(s["xdT"].sem, 1)
        steps(act, G, 1, 0, first)
        scale_known(act, "ug")

        def second(at):
            if g := at(0):
                for c in range(CHUNKS3):
                    act.wait_ge(*s["c_psum"](g, c + 1))
                    k.hold(act)
                    act.activation(upq[:, g.idx, c * GCOLS:(c + 1) * GCOLS], ps[:, 1 + c, :], ACT.Copy,
                                   scale=inv["ug"][:, 0:1]).then_inc(s["upq"].sem, 1)
                if g.has(2):
                    act.wait_ge(*s["gs"](g.back(2)))
                for c in range(CHUNKS3):
                    act.wait_ge(*s["c_psum"](g, CHUNKS3 + c + 1))
                    act.activation(gq[g.par][:, c * GCOLS:(c + 1) * GCOLS], ps[:, 1 + CHUNKS3 + c, :], ACT.Copy,
                                   scale=inv["ug"][:, 1:2]).then_inc(s["gq"].sem, 1)
                act.wait_ge(*s["gq"](g))
                act.activation(sig[g.par], gq[g.par], ACT.Sigmoid, scale=scale["ug"][:, 1:2]).then_inc(s["sig"].sem, 1)
        steps(act, G, 0, 0, second)
        scale_known(act, "gs")
        act.wait_ge(gs_stored.sems[0], G // 2 * 16)
        act.wait_ge(gs_stored.sems[1], G // 2 * 16)

        def third(at):
            if g := at(0):
                act.wait_ge(*gs_loaded(g))
                k.hold(act)
                act.activation(gq2[:, g.idx, :], gin[g.par], ACT.Copy, scale=inv["gs"][:, :])\
                    .then_inc(s["gq2"].sem, 1)
        steps(act, G, 0, 0, third)
        scale_known(act, "o")

        def last(at):
            if g := at(0):
                act.wait_ge(*s["oq"](g))
                if g.has(2):
                    act.wait_ge(*s["y_psum"](g.back(2)))
                act.activation(of[g.par], oq, ACT.Copy).then_inc(s["of"].sem, 1)
            if g := at(1):
                act.wait_ge(*s["oprod"](g))
                if g.has(1):
                    act.wait_ge(*s["of"](g.back(1)))
                act.activation(oq, oprod, ACT.Copy, scale=inv["o"][:, :]).then_inc(s["oq"].sem, 1)
        steps(act, G, 1, 0, last)

    return dict(sync=sync, gpsimd=gpsimd, tensor=tensor, vector=vector, scalar=scalar)


STAGES = [attention0, experts0, attention1, spiking1, context_attention(2), experts2, context_attention(3), quantised3]


def flamingo(nc, args, out, last=8):
    with ExitStack() as ctx:
        k = Kit(nc, ctx, args, out)
        parts = [prepare(k)]
        for no, stage in enumerate(STAGES[:last]):
            parts.append(stage(k, no))
        stored = k.sem("x_stored")
        ov = out.rearrange("(t b) s d -> (b s) t d", b=PAIR)
        QUARTERS = 4
        block = ctx.enter_context(nc.Block())

        def run(engine, name):
            for no, part in enumerate(parts):
                if name in part:
                    if no > 1:
                        stage_start(engine, k, no - 1)
                    part[name](engine)

        @block.sync
        def _(sp):
            run(sp, "sync")
            updated = k.front(last - 1)["x_updated"]
            for j in range(QUARTERS):
                n = k.T // QUARTERS
                sp.wait_ge(*updated.all((j + 1) * n))
                sp.dma_start(ov[:, j * n:(j + 1) * n, :], k.x[:, j * n:(j + 1) * n, :]).then_inc(stored, 16)
            sp.wait_ge(stored, 16 * QUARTERS)
            k.ctxT_stored.wait_all(sp, k.T)
            k.z1T_stored.wait_all(sp, k.T)

        @block.gpsimd
        def _(pool):
            run(pool, "gpsimd")

        @block.tensor
        def _(pe):
            run(pe, "tensor")

        @block.vector
        def _(dve):
            run(dve, "vector")

        @block.scalar
        def _(act):
            run(act, "scalar")


def shape_constants():
    import numpy as np
    c = np.zeros((P, C_END), np.float32)
    c[:, C_IDENT:C_IDENT + P] = np.eye(P)
    freq = (np.float32(1.0) / np.float32(10000.0) ** (np.arange(0, HD0, 2, dtype=np.float32) / np.float32(HD0)))
    theta = np.arange(SEQ, dtype=np.float32)[:, None] * freq.astype(np.float32)[None, :]
    angles = np.concatenate([theta, theta] * 2, axis=1).T
    c[:, C_COS:C_COS + SEQ], c[:, C_SIN:C_SIN + SEQ] = np.cos(angles), np.sin(angles)
    c[:, C_IOTA:C_IOTA + EXPERTS] = np.arange(EXPERTS)
    rows = np.arange(P)
    c[:, C_MASK8:C_MASK8 + 8] = (rows[:, None] // HD1) % 8 == np.arange(8)
    c[:, C_CAUSAL:C_CAUSAL + SEQ] = np.arange(SEQ) <= rows[:, None] % SEQ
    c[:, C_MHALF:C_MHALF + 4] = -0.5
    c[:, C_ONES:C_ONES + P] = 1.0
    return c


def kernel(**inputs):
    import numpy as np
    import concourse.bacc as bacc
    from concourse.bass_utils import run_bass_kernel_spmd

    nc = bacc.Bacc("TRN2", target_bir_lowering=False, num_devices=1)
    arrays, args = {}, {}
    for name, a in list(inputs.items()) + [("shape_constants", shape_constants())]:
        a = np.ascontiguousarray(a)
        arrays[f"in_{name}"] = a
        args[name] = nc.dram_tensor(f"in_{name}", a.shape, mybir.dt.from_np(a.dtype), kind="ExternalInput").ap()
    out = nc.dram_tensor("out_x", inputs["x"].shape, F32, kind="ExternalOutput").ap()
    flamingo(nc, args, out)
    r = run_bass_kernel_spmd(nc, [arrays], core_ids=[0])
    return r.results[0]["out_x"]
```
